# Optimizing a Trainium2 kernel written in Bass

```python
import numpy as np
import jax
import jax.numpy as jnp

def _softmax(x, axis=-1):
    return jax.nn.softmax(x, axis=axis)

def _gelu(x):
    return jax.nn.gelu(x, approximate=True)

def _silu(x):
    return jax.nn.silu(x)

def _sigmoid(x):
    return jax.nn.sigmoid(x)

def _layernorm(x, axis=-1, eps=1e-05):
    m = jnp.mean(x, axis=axis, keepdims=True)
    v = jnp.var(x, axis=axis, keepdims=True)
    return (x - m) / jnp.sqrt(v + eps)

def _scatter_add(tgt, idx, src, axis=0):
    return tgt.at[idx].add(src)

def _segment_sum(src, seg, n):
    return jax.ops.segment_sum(src, seg, n)
kernel_name = 'mk_pixart_seq_d4_seqx_r8_c5febb'

def setup_inputs(seed: int=0):
    np.random.seed(seed)
    _w = jnp.asarray

    def _rec_inputs():
        import jax
        import jax.numpy as jnp
        _rk = jax.random.key(seed)
        x = 7.22e-05 + 1 * jax.random.normal(jax.random.fold_in(_rk, 1), (32, 100, 128), jnp.float32)
        _lenS = 100 - jax.random.randint(jax.random.fold_in(_rk, 7), (32,), 0, max(1, 100 // 4) + 1, jnp.int32)
        _lenS2 = 1444 - jax.random.randint(jax.random.fold_in(_rk, 8), (32,), 0, max(1, 1444 // 4) + 1, jnp.int32)
        cond_1024 = 0.0061147 + 1.02565 * jax.random.normal(jax.random.fold_in(_rk, 11), (32, 128), jnp.float32)
        _ctx_1024P = jax.random.normal(jax.random.fold_in(_rk, 12), (32, 16, 128), jnp.float32)
        _ctx_1024c = jax.random.dirichlet(jax.random.fold_in(_rk, 512), 0.3 * jnp.ones((16,), jnp.float32), (32, 1444))
        _ctx_1024t = jnp.einsum('bsk,bkd->bsd', _ctx_1024c, _ctx_1024P)
        _ctx_1024t = _ctx_1024t * jax.lax.rsqrt(jnp.mean(jnp.square(_ctx_1024t)) + 1e-12) * 0.953939
        ctx_1024 = 0.000376506 + 0.999991 * (_ctx_1024t + 0.3 * jax.random.normal(jax.random.fold_in(_rk, 612), (32, 1444, 128), jnp.float32))
        return (x, cond_1024, ctx_1024)
    x, cond_1024, ctx_1024 = _rec_inputs()

    def _L0_xcond_setup():
        import jax, jax.numpy as jnp
        import numpy as np
        EPS = 1e-06
        H = 16

        def layer_norm(x, gamma=None, beta=None):
            x32 = x.astype(jnp.float32)
            mu = jnp.mean(x32, axis=-1, keepdims=True)
            var = jnp.var(x32, axis=-1, keepdims=True)
            y = (x32 - mu) * jax.lax.rsqrt(var + EPS)
            if gamma is not None:
                y = y * gamma + beta
            return y.astype(x.dtype)

        def mha(q, k, v):
            B, Nq, C = q.shape
            d = C // H
            qh = q.reshape(B, Nq, H, d)
            kh = k.reshape(B, k.shape[1], H, d)
            vh = v.reshape(B, v.shape[1], H, d)
            scores = jnp.einsum('bqhd,bkhd->bhqk', qh, kh) / jnp.sqrt(jnp.asarray(d, q.dtype))
            attn = jax.nn.softmax(scores, axis=-1)
            out = jnp.einsum('bhqk,bkhd->bqhd', attn, vh)
            return out.reshape(B, Nq, C)
        key = jax.random.key(seed)
        ks = jax.random.split(key, 24)
        B, N, C, M, Cc = (4, 256, 128, 128, 128)
        hid = 4 * C
        s = 0.02
        return {'x': jax.random.normal(ks[0], (B, N, C), jnp.float32), 'mod': jax.random.normal(ks[1], (B, C), jnp.float32), 'context': jax.random.normal(ks[2], (B, M, Cc), jnp.float32), 'ada_w': jax.random.normal(ks[3], (C, 6 * C), jnp.float32) * s, 'ada_b': jnp.zeros((6 * C,), jnp.float32), 'qkv_w': jax.random.normal(ks[4], (C, 3 * C), jnp.float32) * s, 'qkv_b': jnp.zeros((3 * C,), jnp.float32), 'self_o_w': jax.random.normal(ks[5], (C, C), jnp.float32) * s, 'self_o_b': jnp.zeros((C,), jnp.float32), 'norm2_g': jnp.ones((C,), jnp.float32), 'norm2_b': jnp.zeros((C,), jnp.float32), 'q_w': jax.random.normal(ks[6], (C, C), jnp.float32) * s, 'q_b': jnp.zeros((C,), jnp.float32), 'kv_w': jax.random.normal(ks[7], (Cc, 2 * C), jnp.float32) * s, 'kv_b': jnp.zeros((2 * C,), jnp.float32), 'cross_o_w': jax.random.normal(ks[8], (C, C), jnp.float32) * s, 'cross_o_b': jnp.zeros((C,), jnp.float32), 'mlp_w1': jax.random.normal(ks[9], (C, hid), jnp.float32) * s, 'mlp_b1': jnp.zeros((hid,), jnp.float32), 'mlp_w2': jax.random.normal(ks[10], (hid, C), jnp.float32) * s, 'mlp_b2': jnp.zeros((C,), jnp.float32)}
    _L0_xcond_all = _L0_xcond_setup()
    _L0_xcond_in = {k: v for k, v in _L0_xcond_all.items() if k in ('ada_w', 'ada_b', 'qkv_w', 'qkv_b', 'self_o_w', 'self_o_b', 'norm2_g', 'norm2_b', 'q_w', 'q_b', 'kv_w', 'kv_b', 'cross_o_w', 'cross_o_b', 'mlp_w1', 'mlp_b1', 'mlp_w2', 'mlp_b2')}
    del _L0_xcond_all

    def _L1_xcond_setup():
        import jax, jax.numpy as jnp
        import numpy as np
        LN_EPS = 1e-06

        def _ln(x):
            mu = jnp.mean(x, axis=-1, keepdims=True)
            var = jnp.var(x, axis=-1, keepdims=True)
            return (x - mu) * jax.lax.rsqrt(var + LN_EPS)
        key = jax.random.key(seed)
        H, NH = (128, 16)
        B, N, S = (4, 128, 77)
        MLP = int(H * 4.0)
        ks = jax.random.split(key, 20)
        s = 1.0 / np.sqrt(H)
        return {'x': jax.random.normal(ks[0], (B, N, H), jnp.float32), 'c': jax.random.normal(ks[1], (B, H), jnp.float32), 'context': jax.random.normal(ks[2], (B, S, H), jnp.float32), 'W_mod': jax.random.normal(ks[3], (H, 6 * H), jnp.float32) * s, 'b_mod': jnp.zeros((6 * H,), jnp.float32), 'W_qkv': jax.random.normal(ks[4], (H, 3 * H), jnp.float32) * s, 'b_qkv': jnp.zeros((3 * H,), jnp.float32), 'W_proj': jax.random.normal(ks[5], (H, H), jnp.float32) * s, 'b_proj': jnp.zeros((H,), jnp.float32), 'W_qc': jax.random.normal(ks[6], (H, H), jnp.float32) * s, 'b_qc': jnp.zeros((H,), jnp.float32), 'W_kvc': jax.random.normal(ks[7], (H, 2 * H), jnp.float32) * s, 'b_kvc': jnp.zeros((2 * H,), jnp.float32), 'W_cproj': jax.random.normal(ks[8], (H, H), jnp.float32) * s, 'b_cproj': jnp.zeros((H,), jnp.float32), 'W_mlp1': jax.random.normal(ks[9], (H, MLP), jnp.float32) * s, 'b_mlp1': jnp.zeros((MLP,), jnp.float32), 'W_mlp2': jax.random.normal(ks[10], (MLP, H), jnp.float32) * (1.0 / np.sqrt(MLP)), 'b_mlp2': jnp.zeros((H,), jnp.float32)}
    _L1_xcond_all = _L1_xcond_setup()
    _L1_xcond_in = {k: v for k, v in _L1_xcond_all.items() if k in ('W_mod', 'b_mod', 'W_qkv', 'b_qkv', 'W_proj', 'b_proj', 'W_qc', 'b_qc', 'W_kvc', 'b_kvc', 'W_cproj', 'b_cproj', 'W_mlp1', 'b_mlp1', 'W_mlp2', 'b_mlp2')}
    del _L1_xcond_all

    def _L2_xcond_setup():
        import jax, jax.numpy as jnp
        import numpy as np
        H = 128
        RH = 2 * H
        E = 3
        B, T, P = (8, 256, 64)
        LN_EPS = 1e-05

        def _layer_norm(x, gamma, beta):
            mu = jnp.mean(x, axis=-1, keepdims=True)
            var = jnp.mean(jnp.square(x - mu), axis=-1, keepdims=True)
            return (x - mu) * jax.lax.rsqrt(var + LN_EPS) * gamma + beta
        key = jax.random.key(seed)
        ks = jax.random.split(key, 24)
        s = lambda fan_in: 1.0 / np.sqrt(fan_in)
        inp = {'mix_hidden_states': jax.random.normal(ks[0], (B, T, H), jnp.float32), 'global_anchor': jax.random.normal(ks[1], (B, H), jnp.float32), 'prototype_bank': jax.random.normal(ks[2], (B, P, H), jnp.float32), 'ln_gamma': jnp.ones((H,), jnp.float32), 'ln_beta': jnp.zeros((H,), jnp.float32), 'Wq': jax.random.normal(ks[3], (H, H), jnp.float32) * s(H), 'Wk': jax.random.normal(ks[4], (H, H), jnp.float32) * s(H), 'Wv': jax.random.normal(ks[5], (H, H), jnp.float32) * s(H), 'router_W': jax.random.normal(ks[6], (3 * H, E), jnp.float32) * s(3 * H), 'router_b': jnp.zeros((E,), jnp.float32), 'e_w1': jax.random.normal(ks[7], (E, 3 * H, RH), jnp.float32) * s(3 * H), 'e_b1': jnp.zeros((E, RH), jnp.float32), 'e_w2': jax.random.normal(ks[8], (E, RH, H), jnp.float32) * s(RH), 'e_b2': jnp.zeros((E, H), jnp.float32), 'gate_w1': jax.random.normal(ks[9], (3 * H, H), jnp.float32) * s(3 * H), 'gate_b1': jnp.zeros((H,), jnp.float32), 'gate_w2': jax.random.normal(ks[10], (H, H), jnp.float32) * s(H), 'gate_b2': jnp.zeros((H,), jnp.float32), 'out_w': jax.random.normal(ks[11], (H, H), jnp.float32) * s(H), 'out_b': jnp.zeros((H,), jnp.float32)}
        return inp
    _L2_xcond_all = _L2_xcond_setup()
    _L2_xcond_in = {k: v for k, v in _L2_xcond_all.items() if k in ('ln_gamma', 'ln_beta', 'Wq', 'Wk', 'Wv', 'router_W', 'router_b', 'e_w1', 'e_b1', 'e_w2', 'e_b2', 'gate_w1', 'gate_b1', 'gate_w2', 'gate_b2', 'out_w', 'out_b')}
    del _L2_xcond_all

    def _L3_xcond_setup():
        import jax, jax.numpy as jnp
        import numpy as np
        EPS = 1e-05

        def _ada_ln(x, c, W_ss, b_ss):
            mu = jnp.mean(x, axis=-1, keepdims=True)
            var = jnp.mean((x - mu) ** 2, axis=-1, keepdims=True)
            h = (x - mu) / jnp.sqrt(var + EPS)
            ss = jax.nn.silu(c) @ W_ss + b_ss
            scale, bias = jnp.split(ss, 2, axis=-1)
            return (1.0 + scale)[:, None, :] * h + bias[:, None, :]
        key = jax.random.key(seed)
        ks = jax.random.split(key, 12)
        B, Lq, Lkv, H = (8, 256, 64, 128)
        s = 0.02
        return {'x_q': jax.random.normal(ks[0], (B, Lq, H), jnp.float32), 'x_kv': jax.random.normal(ks[1], (B, Lkv, H), jnp.float32), 't_vec': jax.random.normal(ks[2], (B, H), jnp.float32), 'Wq': jax.random.normal(ks[3], (H, H), jnp.float32) * s, 'bq': jnp.zeros((H,), jnp.float32), 'Wkv': jax.random.normal(ks[4], (H, 2 * H), jnp.float32) * s, 'bkv': jnp.zeros((2 * H,), jnp.float32), 'Wp': jax.random.normal(ks[5], (H, H), jnp.float32) * s, 'bp': jnp.zeros((H,), jnp.float32), 'Wss_q': jax.random.normal(ks[6], (H, 2 * H), jnp.float32) * s, 'bss_q': jnp.zeros((2 * H,), jnp.float32), 'Wss_kv': jax.random.normal(ks[7], (H, 2 * H), jnp.float32) * s, 'bss_kv': jnp.zeros((2 * H,), jnp.float32)}
    _L3_xcond_all = _L3_xcond_setup()
    _L3_xcond_in = {k: v for k, v in _L3_xcond_all.items() if k in ('Wq', 'bq', 'Wkv', 'bkv', 'Wp', 'bp', 'Wss_q', 'bss_q', 'Wss_kv', 'bss_kv')}
    del _L3_xcond_all
    return {'x': x, 'cond_1024': cond_1024, 'ctx_1024': ctx_1024, 'L0_xcond_ada_w': _L0_xcond_in['ada_w'], 'L0_xcond_ada_b': _L0_xcond_in['ada_b'], 'L0_xcond_qkv_w': _L0_xcond_in['qkv_w'], 'L0_xcond_qkv_b': _L0_xcond_in['qkv_b'], 'L0_xcond_self_o_w': _L0_xcond_in['self_o_w'], 'L0_xcond_self_o_b': _L0_xcond_in['self_o_b'], 'L0_xcond_norm2_g': _L0_xcond_in['norm2_g'], 'L0_xcond_norm2_b': _L0_xcond_in['norm2_b'], 'L0_xcond_q_w': _L0_xcond_in['q_w'], 'L0_xcond_q_b': _L0_xcond_in['q_b'], 'L0_xcond_kv_w': _L0_xcond_in['kv_w'], 'L0_xcond_kv_b': _L0_xcond_in['kv_b'], 'L0_xcond_cross_o_w': _L0_xcond_in['cross_o_w'], 'L0_xcond_cross_o_b': _L0_xcond_in['cross_o_b'], 'L0_xcond_mlp_w1': _L0_xcond_in['mlp_w1'], 'L0_xcond_mlp_b1': _L0_xcond_in['mlp_b1'], 'L0_xcond_mlp_w2': _L0_xcond_in['mlp_w2'], 'L0_xcond_mlp_b2': _L0_xcond_in['mlp_b2'], 'L1_xcond_W_mod': _L1_xcond_in['W_mod'], 'L1_xcond_b_mod': _L1_xcond_in['b_mod'], 'L1_xcond_W_qkv': _L1_xcond_in['W_qkv'], 'L1_xcond_b_qkv': _L1_xcond_in['b_qkv'], 'L1_xcond_W_proj': _L1_xcond_in['W_proj'], 'L1_xcond_b_proj': _L1_xcond_in['b_proj'], 'L1_xcond_W_qc': _L1_xcond_in['W_qc'], 'L1_xcond_b_qc': _L1_xcond_in['b_qc'], 'L1_xcond_W_kvc': _L1_xcond_in['W_kvc'], 'L1_xcond_b_kvc': _L1_xcond_in['b_kvc'], 'L1_xcond_W_cproj': _L1_xcond_in['W_cproj'], 'L1_xcond_b_cproj': _L1_xcond_in['b_cproj'], 'L1_xcond_W_mlp1': _L1_xcond_in['W_mlp1'], 'L1_xcond_b_mlp1': _L1_xcond_in['b_mlp1'], 'L1_xcond_W_mlp2': _L1_xcond_in['W_mlp2'], 'L1_xcond_b_mlp2': _L1_xcond_in['b_mlp2'], 'L2_xcond_ln_gamma': _L2_xcond_in['ln_gamma'], 'L2_xcond_ln_beta': _L2_xcond_in['ln_beta'], 'L2_xcond_Wq': _L2_xcond_in['Wq'], 'L2_xcond_Wk': _L2_xcond_in['Wk'], 'L2_xcond_Wv': _L2_xcond_in['Wv'], 'L2_xcond_router_W': _L2_xcond_in['router_W'], 'L2_xcond_router_b': _L2_xcond_in['router_b'], 'L2_xcond_e_w1': _L2_xcond_in['e_w1'], 'L2_xcond_e_b1': _L2_xcond_in['e_b1'], 'L2_xcond_e_w2': _L2_xcond_in['e_w2'], 'L2_xcond_e_b2': _L2_xcond_in['e_b2'], 'L2_xcond_gate_w1': _L2_xcond_in['gate_w1'], 'L2_xcond_gate_b1': _L2_xcond_in['gate_b1'], 'L2_xcond_gate_w2': _L2_xcond_in['gate_w2'], 'L2_xcond_gate_b2': _L2_xcond_in['gate_b2'], 'L2_xcond_out_w': _L2_xcond_in['out_w'], 'L2_xcond_out_b': _L2_xcond_in['out_b'], 'L3_xcond_Wq': _L3_xcond_in['Wq'], 'L3_xcond_bq': _L3_xcond_in['bq'], 'L3_xcond_Wkv': _L3_xcond_in['Wkv'], 'L3_xcond_bkv': _L3_xcond_in['bkv'], 'L3_xcond_Wp': _L3_xcond_in['Wp'], 'L3_xcond_bp': _L3_xcond_in['bp'], 'L3_xcond_Wss_q': _L3_xcond_in['Wss_q'], 'L3_xcond_bss_q': _L3_xcond_in['bss_q'], 'L3_xcond_Wss_kv': _L3_xcond_in['Wss_kv'], 'L3_xcond_bss_kv': _L3_xcond_in['bss_kv']}

def reference(x, cond_1024, ctx_1024, L0_xcond_ada_w, L0_xcond_ada_b, L0_xcond_qkv_w, L0_xcond_qkv_b, L0_xcond_self_o_w, L0_xcond_self_o_b, L0_xcond_norm2_g, L0_xcond_norm2_b, L0_xcond_q_w, L0_xcond_q_b, L0_xcond_kv_w, L0_xcond_kv_b, L0_xcond_cross_o_w, L0_xcond_cross_o_b, L0_xcond_mlp_w1, L0_xcond_mlp_b1, L0_xcond_mlp_w2, L0_xcond_mlp_b2, L1_xcond_W_mod, L1_xcond_b_mod, L1_xcond_W_qkv, L1_xcond_b_qkv, L1_xcond_W_proj, L1_xcond_b_proj, L1_xcond_W_qc, L1_xcond_b_qc, L1_xcond_W_kvc, L1_xcond_b_kvc, L1_xcond_W_cproj, L1_xcond_b_cproj, L1_xcond_W_mlp1, L1_xcond_b_mlp1, L1_xcond_W_mlp2, L1_xcond_b_mlp2, L2_xcond_ln_gamma, L2_xcond_ln_beta, L2_xcond_Wq, L2_xcond_Wk, L2_xcond_Wv, L2_xcond_router_W, L2_xcond_router_b, L2_xcond_e_w1, L2_xcond_e_b1, L2_xcond_e_w2, L2_xcond_e_b2, L2_xcond_gate_w1, L2_xcond_gate_b1, L2_xcond_gate_w2, L2_xcond_gate_b2, L2_xcond_out_w, L2_xcond_out_b, L3_xcond_Wq, L3_xcond_bq, L3_xcond_Wkv, L3_xcond_bkv, L3_xcond_Wp, L3_xcond_bp, L3_xcond_Wss_q, L3_xcond_bss_q, L3_xcond_Wss_kv, L3_xcond_bss_kv):
    import jax
    import jax.numpy as jnp

    def _L0_xcond_ref(x, mod, context, ada_w, ada_b, qkv_w, qkv_b, self_o_w, self_o_b, norm2_g, norm2_b, q_w, q_b, kv_w, kv_b, cross_o_w, cross_o_b, mlp_w1, mlp_b1, mlp_w2, mlp_b2):
        import jax, jax.numpy as jnp
        import numpy as np
        EPS = 1e-06
        H = 16

        def layer_norm(x, gamma=None, beta=None):
            x32 = x.astype(jnp.float32)
            mu = jnp.mean(x32, axis=-1, keepdims=True)
            var = jnp.var(x32, axis=-1, keepdims=True)
            y = (x32 - mu) * jax.lax.rsqrt(var + EPS)
            if gamma is not None:
                y = y * gamma + beta
            return y.astype(x.dtype)

        def mha(q, k, v):
            B, Nq, C = q.shape
            d = C // H
            qh = q.reshape(B, Nq, H, d)
            kh = k.reshape(B, k.shape[1], H, d)
            vh = v.reshape(B, v.shape[1], H, d)
            scores = jnp.einsum('bqhd,bkhd->bhqk', qh, kh) / jnp.sqrt(jnp.asarray(d, q.dtype))
            attn = jax.nn.softmax(scores, axis=-1)
            out = jnp.einsum('bhqk,bkhd->bqhd', attn, vh)
            return out.reshape(B, Nq, C)
        C = x.shape[-1]
        m = jax.nn.silu(mod) @ ada_w + ada_b
        shift_msa, scale_msa, gate_msa, shift_mlp, scale_mlp, gate_mlp = [c[:, None, :] for c in jnp.split(m, 6, axis=-1)]
        h = layer_norm(x)
        h = h * (1.0 + scale_msa) + shift_msa
        qkv = h @ qkv_w + qkv_b
        q, k, v = jnp.split(qkv, 3, axis=-1)
        h = mha(q, k, v) @ self_o_w + self_o_b
        x = x + h * gate_msa
        h = layer_norm(x, norm2_g, norm2_b)
        q = h @ q_w + q_b
        kv = context @ kv_w + kv_b
        k, v = jnp.split(kv, 2, axis=-1)
        h = mha(q, k, v) @ cross_o_w + cross_o_b
        x = x + h
        h = layer_norm(x)
        h = h * (1.0 + scale_mlp) + shift_mlp
        h = jax.nn.gelu(h @ mlp_w1 + mlp_b1) @ mlp_w2 + mlp_b2
        x = x + h * gate_mlp
        return x

    def _L1_xcond_ref(x, c, context, W_mod, b_mod, W_qkv, b_qkv, W_proj, b_proj, W_qc, b_qc, W_kvc, b_kvc, W_cproj, b_cproj, W_mlp1, b_mlp1, W_mlp2, b_mlp2):
        import jax, jax.numpy as jnp
        import numpy as np
        LN_EPS = 1e-06

        def _ln(x):
            mu = jnp.mean(x, axis=-1, keepdims=True)
            var = jnp.var(x, axis=-1, keepdims=True)
            return (x - mu) * jax.lax.rsqrt(var + LN_EPS)
        B, N, H = x.shape
        NH = 16
        hd = H // NH
        scale = hd ** (-0.5)
        c_proj = jax.nn.silu(c) @ W_mod + b_mod
        shift_a, scale_a, gate_a, shift_m, scale_m, gate_m = jnp.split(c_proj, 6, axis=-1)

        def modulate(t, shift, sc):
            return t * (1 + sc[:, None]) + shift[:, None]
        x_norm = modulate(_ln(x), shift_a, scale_a)
        qkv = x_norm @ W_qkv + b_qkv
        q, k, v = jnp.split(qkv, 3, axis=-1)
        q = q.reshape(B, N, NH, hd).transpose(0, 2, 1, 3)
        k = k.reshape(B, N, NH, hd).transpose(0, 2, 1, 3)
        v = v.reshape(B, N, NH, hd).transpose(0, 2, 1, 3)
        attn_w = jax.nn.softmax(jnp.einsum('bhqd,bhkd->bhqk', q, k) * scale, axis=-1)
        attn_out = jnp.einsum('bhqk,bhkd->bhqd', attn_w, v)
        attn_out = attn_out.transpose(0, 2, 1, 3).reshape(B, N, H)
        attn_out = attn_out @ W_proj + b_proj
        x = x + gate_a[:, None] * attn_out
        S = context.shape[1]
        q_c = _ln(x) @ W_qc + b_qc
        kv_c = _ln(context) @ W_kvc + b_kvc
        k_c, v_c = jnp.split(kv_c, 2, axis=-1)
        q_c = q_c.reshape(B, N, NH, hd).transpose(0, 2, 1, 3)
        k_c = k_c.reshape(B, S, NH, hd).transpose(0, 2, 1, 3)
        v_c = v_c.reshape(B, S, NH, hd).transpose(0, 2, 1, 3)
        c_attn_w = jax.nn.softmax(jnp.einsum('bhqd,bhsd->bhqs', q_c, k_c) * scale, axis=-1)
        c_attn_out = jnp.einsum('bhqs,bhsd->bhqd', c_attn_w, v_c)
        c_attn_out = c_attn_out.transpose(0, 2, 1, 3).reshape(B, N, H)
        c_attn_out = c_attn_out @ W_cproj + b_cproj
        x = x + c_attn_out
        x_norm2 = modulate(_ln(x), shift_m, scale_m)
        h = jax.nn.gelu(x_norm2 @ W_mlp1 + b_mlp1)
        h = h @ W_mlp2 + b_mlp2
        x = x + gate_m[:, None] * h
        return x

    def _L2_xcond_ref(mix_hidden_states, global_anchor, prototype_bank, ln_gamma, ln_beta, Wq, Wk, Wv, router_W, router_b, e_w1, e_b1, e_w2, e_b2, gate_w1, gate_b1, gate_w2, gate_b2, out_w, out_b):
        import jax, jax.numpy as jnp
        import numpy as np
        H = 128
        RH = 2 * H
        E = 3
        B, T, P = (8, 256, 64)
        LN_EPS = 1e-05

        def _layer_norm(x, gamma, beta):
            mu = jnp.mean(x, axis=-1, keepdims=True)
            var = jnp.mean(jnp.square(x - mu), axis=-1, keepdims=True)
            return (x - mu) * jax.lax.rsqrt(var + LN_EPS) * gamma + beta
        x = mix_hidden_states
        nx = _layer_norm(x, ln_gamma, ln_beta)
        q = nx @ Wq
        k = prototype_bank @ Wk
        v = prototype_bank @ Wv
        scores = jnp.einsum('bth,bph->btp', q, k) * H ** (-0.5)
        weights = jax.nn.softmax(scores, axis=-1)
        evidence = jnp.einsum('btp,bph->bth', weights, v)
        anchor = jnp.broadcast_to(global_anchor[:, None, :], nx.shape)
        combined = jnp.concatenate([nx, evidence, anchor], axis=-1)
        router_logits = combined @ router_W + router_b
        router_probs = jax.nn.softmax(router_logits, axis=-1)
        h = jax.nn.silu(jnp.einsum('btc,ecr->bter', combined, e_w1) + e_b1)
        expert_out = jnp.einsum('bter,erh->bteh', h, e_w2) + e_b2
        routed = jnp.sum(expert_out * router_probs[..., None], axis=-2)
        g = jax.nn.sigmoid(jax.nn.silu(combined @ gate_w1 + gate_b1) @ gate_w2 + gate_b2)
        refined_delta = g * (routed @ out_w + out_b)
        return x + refined_delta

    def _L3_xcond_ref(x_q, x_kv, t_vec, Wq, bq, Wkv, bkv, Wp, bp, Wss_q, bss_q, Wss_kv, bss_kv):
        import jax, jax.numpy as jnp
        import numpy as np
        EPS = 1e-05

        def _ada_ln(x, c, W_ss, b_ss):
            mu = jnp.mean(x, axis=-1, keepdims=True)
            var = jnp.mean((x - mu) ** 2, axis=-1, keepdims=True)
            h = (x - mu) / jnp.sqrt(var + EPS)
            ss = jax.nn.silu(c) @ W_ss + b_ss
            scale, bias = jnp.split(ss, 2, axis=-1)
            return (1.0 + scale)[:, None, :] * h + bias[:, None, :]
        B, Lq, H = x_q.shape
        Lkv = x_kv.shape[1]
        nh = 16
        dh = H // nh
        xq = _ada_ln(x_q, t_vec, Wss_q, bss_q)
        xkv = _ada_ln(x_kv, t_vec, Wss_kv, bss_kv)
        q = (xq @ Wq + bq).reshape(B, Lq, nh, dh)
        kv = (xkv @ Wkv + bkv).reshape(B, Lkv, 2, nh, dh)
        k = kv[:, :, 0]
        v = kv[:, :, 1]
        scores = jnp.einsum('bqhd,bkhd->bhqk', q, k) / jnp.sqrt(jnp.float32(dh))
        attn = jax.nn.softmax(scores, axis=-1)
        out = jnp.einsum('bhqk,bkhd->bqhd', attn, v).reshape(B, Lq, H)
        return x_q + (out @ Wp + bp)
    x = _L0_xcond_ref(x, cond_1024, ctx_1024, L0_xcond_ada_w, L0_xcond_ada_b, L0_xcond_qkv_w, L0_xcond_qkv_b, L0_xcond_self_o_w, L0_xcond_self_o_b, L0_xcond_norm2_g, L0_xcond_norm2_b, L0_xcond_q_w, L0_xcond_q_b, L0_xcond_kv_w, L0_xcond_kv_b, L0_xcond_cross_o_w, L0_xcond_cross_o_b, L0_xcond_mlp_w1, L0_xcond_mlp_b1, L0_xcond_mlp_w2, L0_xcond_mlp_b2)
    x = _L1_xcond_ref(x, cond_1024, ctx_1024, L1_xcond_W_mod, L1_xcond_b_mod, L1_xcond_W_qkv, L1_xcond_b_qkv, L1_xcond_W_proj, L1_xcond_b_proj, L1_xcond_W_qc, L1_xcond_b_qc, L1_xcond_W_kvc, L1_xcond_b_kvc, L1_xcond_W_cproj, L1_xcond_b_cproj, L1_xcond_W_mlp1, L1_xcond_b_mlp1, L1_xcond_W_mlp2, L1_xcond_b_mlp2)
    x = _L2_xcond_ref(x, cond_1024, ctx_1024, L2_xcond_ln_gamma, L2_xcond_ln_beta, L2_xcond_Wq, L2_xcond_Wk, L2_xcond_Wv, L2_xcond_router_W, L2_xcond_router_b, L2_xcond_e_w1, L2_xcond_e_b1, L2_xcond_e_w2, L2_xcond_e_b2, L2_xcond_gate_w1, L2_xcond_gate_b1, L2_xcond_gate_w2, L2_xcond_gate_b2, L2_xcond_out_w, L2_xcond_out_b)
    x = _L3_xcond_ref(x, ctx_1024, cond_1024, L3_xcond_Wq, L3_xcond_bq, L3_xcond_Wkv, L3_xcond_bkv, L3_xcond_Wp, L3_xcond_bp, L3_xcond_Wss_q, L3_xcond_bss_q, L3_xcond_Wss_kv, L3_xcond_bss_kv)
    return x

_drawn_inputs = setup_inputs


def setup_inputs(seed=0):
    import zlib

    import numpy as np

    out = dict(_drawn_inputs(seed))
    spreads = {'L0_xcond_ada_b': (0.0, 0.475),
     'L0_xcond_qkv_b': (0.0, 0.8),
     'L0_xcond_self_o_b': (0.0, 0.412),
     'L0_xcond_norm2_g': (1.0, 0.6),
     'L0_xcond_norm2_b': (0.0, 2.0),
     'L0_xcond_q_b': (0.0, 2.0),
     'L0_xcond_kv_b': (0.0, 0.369),
     'L0_xcond_cross_o_b': (0.0, 0.1),
     'L0_xcond_mlp_b1': (0.0, 0.8),
     'L0_xcond_mlp_b2': (0.0, 0.487),
     'L1_xcond_b_mod': (0.0, 0.1),
     'L1_xcond_b_qkv': (0.0, 0.368),
     'L1_xcond_b_proj': (0.0, 0.401),
     'L1_xcond_b_qc': (0.0, 0.524),
     'L1_xcond_b_kvc': (0.0, 0.1),
     'L1_xcond_b_cproj': (0.0, 0.1),
     'L1_xcond_b_mlp1': (0.0, 0.57),
     'L1_xcond_b_mlp2': (0.0, 0.406),
     'L2_xcond_ln_gamma': (1.0, 0.6),
     'L2_xcond_ln_beta': (0.0, 0.8),
     'L2_xcond_router_b': (0.0, 0.8),
     'L2_xcond_e_b1': (0.0, 0.513),
     'L2_xcond_e_b2': (0.0, 0.307),
     'L2_xcond_gate_b1': (0.0, 2.0),
     'L2_xcond_gate_b2': (0.0, 0.8),
     'L2_xcond_out_b': (0.0, 0.451),
     'L3_xcond_bq': (0.0, 2.0),
     'L3_xcond_bkv': (0.0, 0.509),
     'L3_xcond_bp': (0.0, 0.1),
     'L3_xcond_bss_q': (0.0, 2.0),
     'L3_xcond_bss_kv': (0.0, 0.8)}
    factors = {'L0_xcond_qkv_w': 8.0,
     'L0_xcond_self_o_w': 8.0,
     'L0_xcond_q_w': 64.0,
     'L0_xcond_mlp_w1': 6.907,
     'L0_xcond_mlp_w2': 5.994,
     'L3_xcond_Wq': 8.0,
     'L3_xcond_Wkv': 2.816,
     'L3_xcond_Wss_q': 8.0,
     'L3_xcond_Wss_kv': 8.0,
     'L0_xcond_kv_w': 4.788,
     'L2_xcond_Wq': 2.905,
     'L2_xcond_Wk': 2.773}
    for name, (base, spread) in spreads.items():
        noise = np.random.default_rng([zlib.crc32(name.encode()), seed]).standard_normal(out[name].shape)
        drawn = base * np.exp(spread * noise) if base else spread * noise
        out[name] = jnp.asarray(drawn.astype(out[name].dtype))
    for name, factor in factors.items():
        out[name] = (out[name] * factor).astype(out[name].dtype)
    return out
```

```python
from contextlib import ExitStack

import numpy as np
import concourse.bass as bass
from concourse import mybir

F32 = mybir.dt.float32
BF16 = mybir.dt.bfloat16
ALU = mybir.AluOpType
ACT = mybir.ActivationFunctionType
AX = mybir.AxisListType

P = 128
TOK = 100
CTX = 1444
HEADS = 16
DH = 8
PAIRS = HEADS // 2
GB = 4
GT = GB * TOK
KC = 121
CHUNKS = -(-CTX // KC)
KLAST = CTX - (CHUNKS - 1) * KC
BLK = 4 * KC
ISQ = float(DH) ** -0.5
SLOT = 64
MROWS = 2
TERMS = 6
K_PART = (0, 0, 0, 1, 1, 2)
Q_PART = (0, 1, 2, 0, 1, 0)
QBLK = CTX // 4

OPEN = 1
PERM = [(2 * p + a) * DH + d for a in range(2) for d in range(DH) for p in range(PAIRS)]


class Layout:

    def __init__(self):
        self.at, self.width = {}, 0

    def add(self, name, n):
        self.at[name] = (self.width, self.width + n)
        self.width += n

    def __getitem__(self, name):
        return self.at[name]


WEIGHTS = Layout()
COLS = Layout()
ROWS = Layout()
CONST = Layout()

for _name, _n in [("mod", 16 * P),
                  ("pre0", 3 * P), ("mid0", 2 * P), ("kv0", 2 * P), ("post0", 9 * P),
                  ("pre1", 3 * P), ("mid1", 2 * P), ("kv1", 2 * P), ("post1", 9 * P),
                  ("pre2", 2 * P), ("moe", P + 9 + 18 * P + 3 * P + 6 * P + 2 * P),
                  ("pre3", P), ("kv3", 2 * P), ("post3", P)]:
    WEIGHTS.add(_name, _n)
for _name, _n in [("mod", 16), ("bq0", 1), ("bk0", 1), ("bv0", 1), ("bo0", 1), ("ng0", 1), ("nb0", 1), ("bqc0", 1),
                  ("bkc0", 1), ("bvc0", 1), ("boc0", 1), ("b10", 4), ("b20", 1),
                  ("bq1", 1), ("bk1", 1), ("bv1", 1), ("bo1", 1), ("bqc1", 1),
                  ("bkc1", 1), ("bvc1", 1), ("boc1", 1), ("b11", 4), ("b21", 1),
                  ("ng2", 1), ("nb2", 1), ("eb1", 6), ("gb1", 1),
                  ("bq3", 1), ("bkc3", 1), ("bvc3", 1), ("bo3", 1)]:
    COLS.add(_name, _n)
for _name, _n in [("router", 3), ("eb2", 3 * P), ("gb2", P), ("outb", P)]:
    ROWS.add(_name, _n)
CONST.add("ident", P)
CONST.add("mask", 4)


def build(nc, x, ctx_t, ctx_n, cond_t, weights, cols, rows, const, out, NB, last=99, probe=None):
    NG = NB // GB
    with ExitStack() as top:
        def keep(name, shape, dt=F32):
            return top.enter_context(nc.sbuf_tensor(name, shape, dt))

        X = keep("x_tokens", [TOK, NB, P])
        QT = keep("q_channels", [P, NB * TOK])
        KT = keep("k_channels", [P, NB * TOK])
        V0 = keep("v_tokens", [TOK, NB, P])
        AT = keep("attn_channels", [P, NB * TOK])
        MOD = keep("modulation", [P, 16, NB])
        COND = keep("cond", [P, NB])
        C = keep("bias_columns", [P, COLS.width])
        K = keep("constants", [P, CONST.width])
        passed = top.enter_context(nc.semaphore("passed"))
        ident = K[:, CONST["ident"][0]:CONST["ident"][1]]
        mask = K[:, CONST["mask"][0]:CONST["mask"][1]]

        def col(name, n=0, rows=P):
            return C[0:rows, COLS[name][0] + n:COLS[name][0] + n + 1]

        class Stage:

            def __init__(self, name):
                self.name = name

            def __enter__(self):
                self.stack = ExitStack()
                self.sems = []
                self.ps = self.stack.enter_context(nc.psum_tensor(f"{self.name}_psum", [P, 8, 512], F32))
                return self

            def sb(self, name, shape, dt=F32):
                return self.stack.enter_context(nc.sbuf_tensor(f"{self.name}_{name}", shape, dt))

            def sem(self, name):
                s = self.stack.enter_context(nc.semaphore(f"{self.name}_{name}"))
                self.sems.append(s)
                return s

            def block(self):
                for s in self.sems:
                    nc.gpsimd.sem_inc(s, 1)
                nc.all_engine_barrier()
                return nc.Block()

            def __exit__(self, *a):
                if a[0] is None:
                    nc.all_engine_barrier()
                    for s in self.sems:
                        nc.gpsimd.sem_clear(s)
                    nc.all_engine_barrier()
                self.stack.close()

        class Chain:

            def __init__(self, eng, sem, it, per, own=False):
                self.eng, self.sem, self.it, self.per, self.n, self.own = eng, sem, it, per, 0, own

            def __call__(self, ins):
                self.n += 1
                ins.then_inc(self.sem, 1)
                if self.own:
                    self.eng.wait_ge(self.sem, OPEN + self.it * self.per + self.n)
                    self.eng.sem_inc(passed, 1)
                else:
                    self.eng.wait_ge(self.sem, OPEN + self.it * self.per + self.n)

        def weights_in(sp, tile, name, sem):
            a, b = WEIGHTS[name]
            sp.dma_start(tile[:, :], weights[:, a:b]).then_inc(sem, 16)

        with Stage("mods") as st:
            W = st.sb("w", [P, 16 * P])
            SC = st.sb("silu_cond", [P, NB])
            x_in = st.sem("x_in")
            constants_in = st.sem("constants_in")
            w_in = st.sem("w_in")
            silu_ready = st.sem("silu_ready")
            mod_ps = st.sem("mod_ps")
            mod_ready = st.sem("mod_ready")
            with st.block() as block:
                @block.sync
                def _(sp):
                    sp.dma_start(COND[:, :], cond_t).then_inc(constants_in, 16)
                    sp.dma_start(C[:, :], cols).then_inc(constants_in, 16)
                    sp.dma_start(K[:, :], const).then_inc(constants_in, 16)
                    weights_in(sp, W, "mod", w_in)
                    sp.dma_start(X[:, :, :], x.rearrange("b t c -> t b c")).then_inc(x_in, 16)
                    sp.wait_ge(x_in, OPEN + 16)

                @block.scalar
                def _(act):
                    act.wait_ge(constants_in, OPEN + 48)
                    act.activation(SC[:, :], COND[:, :], ACT.Silu).then_inc(silu_ready, 1)

                @block.tensor
                def _(pe):
                    pe.wait_ge(silu_ready, OPEN + 1)
                    pe.wait_ge(w_in, OPEN + 16)
                    for k in range(16):
                        mm = pe.matmul(st.ps[:, 0, k * NB:(k + 1) * NB], W[:, k * P:(k + 1) * P], SC[:, :],
                                       start=True, stop=True)
                    mm.then_inc(mod_ps, 1)

                @block.vector
                def _(dve):
                    dve.wait_ge(mod_ps, OPEN + 1)
                    b0 = COLS["mod"][0]
                    dve.tensor_tensor(MOD[:, :, :], st.ps[:, 0, 0:16 * NB].rearrange("p (k b) -> p k b", k=16),
                                      C[:, b0:b0 + 16].rearrange("p (k o) -> p k o", o=1).to_broadcast([P, 16, NB]), ALU.add).then_inc(mod_ready, 1)
                    dve.wait_ge(mod_ready, OPEN + 1)
                    for n in (1, 4, 7, 10, 12, 14):
                        dve.tensor_scalar(MOD[:, n, :], MOD[:, n, :], 1.0, None, ALU.add).then_inc(mod_ready, 1)
                    dve.wait_ge(mod_ready, OPEN + 7)

        class Norm:

            def __init__(self, st, tag, eps):
                self.eps = eps
                self.stats = st.sb(tag + "_stats", [TOK, GB, 6])
                self.mv = st.sb(tag + "_mean_var", [TOK, GB, 2])
                self.ve = st.sb(tag + "_var_eps", [TOK, GB])
                self.half = st.sb(tag + "_minus_half", [TOK, GB])
                self.rstd = st.sb(tag + "_rstd", [TOK, GB])
                self.xn = st.sb(tag + "_xn", [TOK, GB, P])
                self.h = st.sb(tag + "_h", [P, GT])
                self.stats_done = st.sem(tag + "_stats_done")
                self.var_ready = st.sem(tag + "_var_ready")
                self.rstd_ready = st.sem(tag + "_rstd_ready")
                self.xn_ready = st.sem(tag + "_xn_ready")
                self.xnT_ready = st.sem(tag + "_xnT_ready")
                self.h_ready = st.sem(tag + "_h_ready")

            def vector(self, dve, g):
                for k in range(GB):
                    ins = dve.bn_stats(self.stats[:, k, :], X[:, g * GB + k, :])
                    ins.then_inc(self.stats_done, 1)
                for k in range(GB):
                    dve.wait_ge(self.stats_done, OPEN + g * 2 * GB + GB)
                    dve.sem_inc(passed, 1)
                    dve.bn_aggr(self.mv[:, k, :], self.stats[:, k, :]).then_inc(self.stats_done, 1)
                dve.wait_ge(self.stats_done, OPEN + g * 2 * GB + 2 * GB)
                dve.tensor_scalar(self.ve[:, :], self.mv[:, :, 1], self.eps, None, ALU.add).then_inc(self.var_ready, 1)
                dve.wait_ge(self.rstd_ready, OPEN + g + 1)
                for k in range(GB):
                    dve.tensor_scalar(self.xn[:, k, :], X[:, g * GB + k, :], self.mv[:, k, 0:1],
                                      self.rstd[:, k:k + 1], ALU.subtract, ALU.mult).then_inc(self.xn_ready, 1)

            def gpsimd_init(self, pool):
                pool.memset(self.half[:, :], -0.5).then_inc(self.var_ready, 1)

            def gpsimd(self, pool, g):
                pool.wait_ge(self.var_ready, OPEN + g + 2)
                pool.tensor_tensor(self.rstd[:, :], self.ve[:, :], self.half[:, :], ALU.pow).then_inc(self.rstd_ready, 1)

            def tensor(self, pe, g, bank):
                for k in range(GB):
                    pe.wait_ge(self.xn_ready, OPEN + g * GB + k + 1)
                    tr = pe.transpose(bank[:, k * TOK:(k + 1) * TOK], self.xn[:, k, :], ident[0:TOK, 0:TOK])
                tr.then_inc(self.xnT_ready, 1)

            def scalar(self, act, g, bank, scale, shift):
                act.wait_ge(self.xnT_ready, OPEN + g + 1)
                act.sem_inc(passed, 1)
                if scale is None:
                    act.activation(self.h[:, :], bank[:, 0:GT], ACT.Copy).then_inc(self.h_ready, GB)
                    return
                for k in range(GB):
                    act.activation(self.h[:, k * TOK:(k + 1) * TOK], bank[:, k * TOK:(k + 1) * TOK], ACT.Identity,
                                   scale=scale(g, k), bias=shift(g, k)).then_inc(self.h_ready, 1)

        def by_mod(n):
            return lambda g, k: MOD[:, n, bass.ds(g * GB + k, 1)]

        def by_col(name):
            return lambda g, k: col(name)

        def pre(name, weights_name, scale, shift, eps, bk, bq):
            with Stage(name) as st:
                nw = 3 if bq else 2
                W = st.sb("w", [P, nw * P])
                w_in = st.sem("w_in")
                norm = Norm(st, "ln", eps)
                k_ps, q_ps, v_ps = st.sem("k_ps"), st.sem("q_ps"), st.sem("v_ps")
                qk_out, v_out = st.sem("qk_out"), st.sem("v_out")
                ps = st.ps
                nqk = nw - 1
                with st.block() as block:
                    @block.sync
                    def _(sp):
                        weights_in(sp, W, weights_name, w_in)

                    @block.vector
                    def _(dve):
                        with dve.Fori(0, NG) as g:
                            dve.wait_ge(qk_out, OPEN + g * nqk)
                            dve.sem_inc(passed, 1)
                            norm.vector(dve, g)
                            dve.wait_ge(v_ps, OPEN + g + 1)
                            dve.tensor_copy(V0[:, bass.ds(g * GB, GB), :],
                                            ps[0:TOK, 3, 0:GB * P].rearrange("p (k c) -> p k c", k=GB)).then_inc(v_out, 1)

                    @block.gpsimd
                    def _(pool):
                        norm.gpsimd_init(pool)
                        with pool.Fori(0, NG) as g:
                            norm.gpsimd(pool, g)

                    @block.tensor
                    def _(pe):
                        pe.wait_ge(w_in, OPEN + 16)
                        with pe.Fori(0, NG) as g:
                            norm.tensor(pe, g, ps[:, 0, :])
                            pe.wait_ge(norm.h_ready, OPEN + (g + 1) * GB)
                            pe.wait_ge(qk_out, OPEN + g * nqk)
                            pe.matmul(ps[:, 1, 0:GT], W[:, 0:P], norm.h[:, :], start=True, stop=True).then_inc(k_ps, 1)
                            if bq:
                                pe.matmul(ps[:, 2, 0:GT], W[:, 2 * P:3 * P], norm.h[:, :], start=True, stop=True).then_inc(q_ps, 1)
                            pe.wait_ge(v_out, OPEN + g)
                            for k in range(GB):
                                mm = pe.matmul(ps[0:TOK, 3, k * P:(k + 1) * P], norm.h[:, k * TOK:(k + 1) * TOK],
                                               W[:, P:2 * P], start=True, stop=True)
                            mm.then_inc(v_ps, 1)

                    @block.scalar
                    def _(act):
                        with act.Fori(0, NG) as g:
                            act.wait_ge(v_ps, OPEN + g)
                            norm.scalar(act, g, ps[:, 0, :], scale, shift)
                            act.wait_ge(k_ps, OPEN + g + 1)
                            act.sem_inc(passed, 1)
                            act.activation(KT[:, bass.ds(g * GT, GT)], ps[:, 1, 0:GT], ACT.Identity, bias=col(bk)).then_inc(qk_out, 1)
                            if bq:
                                act.wait_ge(q_ps, OPEN + g + 1)
                                act.sem_inc(passed, 1)
                                act.activation(QT[:, bass.ds(g * GT, GT)], ps[:, 2, 0:GT], ACT.Identity, bias=col(bq)).then_inc(qk_out, 1)

        class Residual:

            def __init__(self, st, tag, bias, gate):
                self.bias, self.gate = bias, gate
                self.y = st.sb(tag + "_y", [P, GT])
                self.y_ps = st.sem(tag + "_y_ps")
                self.y_ready = st.sem(tag + "_y_ready")
                self.yT_ready = st.sem(tag + "_yT_ready")
                self.x_ready = st.sem(tag + "_x_ready")

            def vector_gate(self, dve, g, bank):
                dve.wait_ge(self.y_ps, OPEN + g + 1)
                for k in range(GB):
                    s = slice(k * TOK, (k + 1) * TOK)
                    if self.gate is None:
                        ins = dve.tensor_scalar(self.y[:, s], bank[:, s], col(self.bias), None, ALU.add)
                    else:
                        ins = dve.tensor_scalar(self.y[:, s], bank[:, s], col(self.bias), self.gate(g, k), ALU.add, ALU.mult)
                    ins.then_inc(self.y_ready, 1)

            def tensor(self, pe, g, bank):
                for k in range(GB):
                    pe.wait_ge(self.y_ready, OPEN + g * GB + k + 1)
                    tr = pe.transpose(bank[0:TOK, k * P:(k + 1) * P], self.y[:, k * TOK:(k + 1) * TOK], ident)
                tr.then_inc(self.yT_ready, 1)

            def vector_add(self, dve, g, bank):
                dve.wait_ge(self.yT_ready, OPEN + g + 1)
                xs = X[:, bass.ds(g * GB, GB), :]
                dve.tensor_tensor(xs, xs, bank[0:TOK, 0:GB * P].rearrange("p (k c) -> p k c", k=GB), ALU.add).then_inc(self.x_ready, 1)
                dve.wait_ge(self.x_ready, OPEN + g + 1)
                dve.sem_inc(passed, 1)

        def mid(name, weights_name, bo, gate, scale, shift, bq):
            with Stage(name) as st:
                W = st.sb("w", [P, 2 * P])
                w_in = st.sem("w_in")
                res = Residual(st, "o", bo, gate)
                norm = Norm(st, "ln", 1e-6)
                q_ps, q_out = st.sem("q_ps"), st.sem("q_out")
                ps = st.ps
                with st.block() as block:
                    @block.sync
                    def _(sp):
                        weights_in(sp, W, weights_name, w_in)

                    @block.vector
                    def _(dve):
                        with dve.Fori(0, NG) as g:
                            res.vector_gate(dve, g, ps[:, 0, :])
                            res.vector_add(dve, g, ps[:, 1, :])
                            norm.vector(dve, g)

                    @block.gpsimd
                    def _(pool):
                        norm.gpsimd_init(pool)
                        with pool.Fori(0, NG) as g:
                            norm.gpsimd(pool, g)

                    @block.tensor
                    def _(pe):
                        pe.wait_ge(w_in, OPEN + 16)
                        with pe.Fori(0, NG) as g:
                            pe.matmul(ps[:, 0, 0:GT], W[:, 0:P], AT[:, bass.ds(g * GT, GT)], start=True, stop=True).then_inc(res.y_ps, 1)
                            res.tensor(pe, g, ps[:, 1, :])
                            norm.tensor(pe, g, ps[:, 2, :])
                            pe.wait_ge(norm.h_ready, OPEN + (g + 1) * GB)
                            pe.wait_ge(q_out, OPEN + g)
                            pe.matmul(ps[:, 3, 0:GT], W[:, P:2 * P], norm.h[:, :], start=True, stop=True).then_inc(q_ps, 1)

                    @block.scalar
                    def _(act):
                        with act.Fori(0, NG) as g:
                            norm.scalar(act, g, ps[:, 2, :], scale, shift)
                            act.wait_ge(q_ps, OPEN + g + 1)
                            act.sem_inc(passed, 1)
                            act.activation(QT[:, bass.ds(g * GT, GT)], ps[:, 3, 0:GT], ACT.Identity, bias=col(bq)).then_inc(q_out, 1)

        def post(name, weights_name, bo, scale, shift, b1, b2, gate):
            with Stage(name) as st:
                W = st.sb("w", [P, 9 * P])
                hid = st.sb("hidden", [P, 4, GT])
                w_in = st.sem("w_in")
                res = Residual(st, "o", bo, None)
                norm = Norm(st, "ln", 1e-6)
                res2 = Residual(st, "mlp", b2, gate)
                hid_ps, hid_ready = st.sem("hid_ps"), st.sem("hid_ready")
                ps = st.ps
                with st.block() as block:
                    @block.sync
                    def _(sp):
                        weights_in(sp, W, weights_name, w_in)

                    @block.vector
                    def _(dve):
                        with dve.Fori(0, NG) as g:
                            res.vector_gate(dve, g, ps[:, 0, :])
                            res.vector_add(dve, g, ps[:, 1, :])
                            norm.vector(dve, g)
                            res2.vector_gate(dve, g, ps[:, 3, :])
                            res2.vector_add(dve, g, ps[:, 1, :])

                    @block.gpsimd
                    def _(pool):
                        norm.gpsimd_init(pool)
                        with pool.Fori(0, NG) as g:
                            norm.gpsimd(pool, g)

                    @block.tensor
                    def _(pe):
                        pe.wait_ge(w_in, OPEN + 16)
                        with pe.Fori(0, NG) as g:
                            pe.wait_ge(res2.x_ready, OPEN + g)
                            pe.matmul(ps[:, 0, 0:GT], W[:, 0:P], AT[:, bass.ds(g * GT, GT)], start=True, stop=True).then_inc(res.y_ps, 1)
                            res.tensor(pe, g, ps[:, 1, :])
                            norm.tensor(pe, g, ps[:, 2, :])
                            pe.wait_ge(norm.h_ready, OPEN + (g + 1) * GB)
                            for n in range(4):
                                pe.matmul(ps[:, 4 + n, 0:GT], W[:, (1 + n) * P:(2 + n) * P], norm.h[:, :],
                                          start=True, stop=True).then_inc(hid_ps, 1)
                            for n in range(4):
                                pe.wait_ge(hid_ready, OPEN + g * 4 + n + 1)
                                mm = pe.matmul(ps[:, 3, 0:GT], W[:, (5 + n) * P:(6 + n) * P], hid[:, n, :],
                                               start=(n == 0), stop=(n == 3))
                            mm.then_inc(res2.y_ps, 1)
                            pe.wait_ge(res.x_ready, OPEN + g + 1)
                            res2.tensor(pe, g, ps[:, 1, :])

                    @block.scalar
                    def _(act):
                        with act.Fori(0, NG) as g:
                            norm.scalar(act, g, ps[:, 2, :], scale, shift)
                            for n in range(4):
                                act.wait_ge(hid_ps, OPEN + g * 4 + n + 1)
                                act.activation(hid[:, n, :], ps[:, 4 + n, 0:GT], ACT.Gelu_apprx_tanh,
                                               bias=col(b1, n)).then_inc(hid_ready, 1)

        def split_rest(pool, link, parts, rest):
            link(pool.tensor_copy(parts[1], rest))
            link(pool.tensor_tensor(parts[2], rest, parts[1], ALU.subtract))

        def split(pool, link, value, parts, rest):
            link(pool.tensor_copy(parts[0], value))
            link(pool.tensor_tensor(rest, value, parts[0], ALU.subtract))
            split_rest(pool, link, parts, rest)

        def slot_rows(a, j):
            at = a * SLOT + MROWS + j * DH
            return slice(at, at + DH)

        def attend(name, kv=None, normed=False, bk=None, bv=None, eps=1e-6, modulated=False):
            cross = kv is not None
            nk = CTX if cross else TOK
            spans = [(c * KC, KC if c < CHUNKS - 1 else KLAST) for c in range(CHUNKS)] if cross else [(0, TOK)]
            NU = 2 * len(spans)
            kr = KC if cross else TOK
            MAXN = HEADS if cross else 4
            with Stage(name) as st:
                ps = st.ps
                kx = st.sb("k_packed", [P, PAIRS, nk], BF16)
                qx = st.sb("q_packed", [P, PAIRS, 2 * TOK], BF16)
                kp = [st.sb(f"k_part{i}", [P, nk], BF16) for i in range(3)]
                qp = [st.sb(f"q_part{i}", [P, TOK], BF16) for i in range(3)]
                krest = st.sb("k_rest", [P, nk])
                qrest = st.sb("q_rest", [P, TOK])
                v = st.sb("v", [kr, len(spans), P])
                ones = st.sb("ones", [kr, 32])
                prob = st.sb("prob", [kr, 3, 2 * GT])
                nmax = st.sb("minus_max", [TOK, HEADS])
                nmax1 = st.sb("minus_max_part", [TOK, HEADS], BF16)
                mcols = st.sb("shift_columns", [TOK, 2, MROWS, PAIRS])
                mrows = st.sb("shift_rows", [2 * MROWS * PAIRS, TOK], BF16)
                onat = st.sb("o_sum", [P, TOK])
                dnat = st.sb("d_sum", [P, TOK])
                rden = st.sb("d_reciprocal", [P, TOK])
                prepared = st.sem("prepared")
                k1_ready, rest_ready = st.sem("k1_ready"), st.sem("rest_ready")
                parts_ready, cleared = st.sem("parts_ready"), st.sem("cleared")
                packed_in, shift_in = st.sem("packed_in"), st.sem("shift_in")
                v_ready = st.sem("v_ready")
                max_ps, max_done = st.sem("max_ps"), st.sem("max_done")
                shift_ps, shift_ready, shift_chain = st.sem("shift_ps"), st.sem("shift_ready"), st.sem("shift_chain")
                score_ps, prob_ready, pv_done = st.sem("score_ps"), st.sem("prob_ready"), st.sem("pv_done")
                fin = st.sem("fin")
                NFIN = 12
                if cross:
                    W = st.sb("w", [P, 2 * P])
                    xt = st.sb("ctx_channels", [P, CTX])
                    w_in, ctx_in = st.sem("w_in"), st.sem("ctx_in")
                    k_ps, v_ps = st.sem("k_ps"), st.sem("v_ps")
                    NV = 4
                else:
                    NV = 1
                if normed:
                    xn = st.sb("ctx_tokens", [KC, CHUNKS, P])
                    stats = st.sb("stats", [KC, CHUNKS, 6])
                    mv = st.sb("mean_var", [KC, CHUNKS, 2])
                    ve = st.sb("var_eps", [KC, CHUNKS])
                    half = st.sb("minus_half", [KC, CHUNKS])
                    rstd = st.sb("rstd", [KC, CHUNKS])
                    mv_zero = st.sem("mv_zero")
                    stats_done, var_ready, rstd_ready = st.sem("stats_done"), st.sem("var_ready"), st.sem("rstd_ready")
                    xn_ready, xnT_ps, xt_ready = st.sem("xn_ready"), st.sem("xnT_ps"), st.sem("xt_ready")
                NPART = 6 if cross else 8
                kbank = 3 if normed else 0
                vbank = 3 - kbank

                def chunk_rows(c):
                    return spans[c][1]

                with st.block() as block:
                    @block.sync
                    def _(sp):
                        if cross:
                            weights_in(sp, W, kv, w_in)
                        sp.wait_ge(prepared, OPEN + 5)
                        with sp.Fori(0, NB) as b:
                            if normed:
                                sp.wait_ge(xnT_ps, OPEN + b * 3)
                                sp.sem_inc(passed, 1)
                                sp.dma_start(xn[:, 0:CHUNKS - 1, :],
                                             ctx_n[b, 0:(CHUNKS - 1) * KC, :].rearrange("(c p) d -> p c d", p=KC)).then_inc(ctx_in, 16)
                                sp.dma_start(xn[0:KLAST, CHUNKS - 1, :], ctx_n[b, (CHUNKS - 1) * KC:CTX, :]).then_inc(ctx_in, 16)
                            elif cross:
                                sp.wait_ge(v_ps, OPEN + b * 3)
                                sp.sem_inc(passed, 1)
                                sp.dma_start(xt[:, :], ctx_t[b]).then_inc(ctx_in, 16)
                            sp.wait_ge(score_ps, OPEN + b * NU)
                            sp.wait_ge(parts_ready, OPEN + (b + 1) * NPART)
                            sp.sem_inc(passed, 1)
                            if cross:
                                sp.wait_ge(k1_ready, OPEN + (b + 1) * 3)
                            for a in range(2):
                                for j in range(TERMS):
                                    sp.dma_start(qx[slot_rows(a, j), :, a * TOK:(a + 1) * TOK],
                                                 qp[Q_PART[j]][a * SLOT:(a + 1) * SLOT, :]).then_inc(packed_in, 16)
                            for a in range(2):
                                for j in range(TERMS):
                                    sp.dma_start(kx[slot_rows(a, j), :, :],
                                                 kp[K_PART[j]][a * SLOT:(a + 1) * SLOT, :]).then_inc(packed_in, 16)
                            sp.wait_ge(shift_ready, OPEN + b + 1)
                            for a in range(2):
                                n = MROWS * PAIRS
                                sp.dma_start(qx[a * SLOT:a * SLOT + MROWS, :, a * TOK:(a + 1) * TOK],
                                             mrows[a * n:(a + 1) * n, :]).then_inc(shift_in, 16)

                    @block.gpsimd
                    def _(pool):
                        pool.memset(kx[:, :, :], 0.0).then_inc(prepared, 1)
                        pool.memset(qx[:, :, :], 0.0).then_inc(prepared, 1)
                        pool.memset(ones[:, :], 1.0).then_inc(prepared, 1)
                        if normed:
                            pool.memset(half[:, :], -0.5).then_inc(var_ready, 1)
                        with pool.Fori(0, NB) as b:
                            link = Chain(pool, parts_ready, b, NPART, own=True)
                            if normed:
                                pool.wait_ge(var_ready, OPEN + b + 2)
                                pool.tensor_tensor(rstd[:, :], ve[:, :], half[:, :], ALU.pow).then_inc(rstd_ready, 1)
                            pool.wait_ge(score_ps, OPEN + b * NU)
                            pool.wait_ge(packed_in, OPEN + b * 2 * 2 * TERMS * 16)
                            pool.sem_inc(passed, 1)
                            qs = QT[:, bass.ds(b * TOK, TOK)]
                            split(pool, link, qs, [t[:, :] for t in qp], qrest[:, :])
                            if cross:
                                pool.wait_ge(k1_ready, OPEN + (b + 1) * 3)
                                pool.wait_ge(rest_ready, OPEN + (b + 1) * 3)
                                pool.sem_inc(passed, 1)
                                split_rest(pool, link, [t[:, :] for t in kp], krest[:, :])
                            else:
                                split(pool, link, KT[:, bass.ds(b * TOK, TOK)], [t[:, :] for t in kp], krest[:, :])
                            assert link.n == NPART

                    @block.tensor
                    def _(pe):
                        if cross:
                            pe.wait_ge(w_in, OPEN + 16)
                        with pe.Fori(0, NB) as b:
                            pe.wait_ge(prob_ready, OPEN + b * NU)
                            if normed:
                                for t in range(3):
                                    pe.wait_ge(xn_ready, OPEN + b * CHUNKS + 4 * t + 4)
                                    for c in range(4 * t, 4 * t + 4):
                                        tr = pe.transpose(ps[:, t, (c % 4) * KC:(c % 4) * KC + chunk_rows(c)],
                                                          xn[0:chunk_rows(c), c, :], ident[0:chunk_rows(c), 0:chunk_rows(c)])
                                    tr.then_inc(xnT_ps, 1)
                                pe.wait_ge(xt_ready, OPEN + (b + 1) * 3)
                            elif cross:
                                pe.wait_ge(ctx_in, OPEN + (b + 1) * 16)
                            if cross:
                                for t in range(3):
                                    n = min(BLK, CTX - t * BLK)
                                    pe.matmul(ps[:, kbank + t, 0:n], W[:, 0:P], xt[:, t * BLK:t * BLK + n],
                                              start=True, stop=True).then_inc(k_ps, 1)
                                for t in range(3):
                                    for c in range(4 * t, 4 * t + 4):
                                        mm = pe.matmul(ps[0:chunk_rows(c), vbank + t, (c % 4) * P:(c % 4 + 1) * P],
                                                       xt[:, c * KC:c * KC + chunk_rows(c)], W[:, P:2 * P],
                                                       start=True, stop=True)
                                    mm.then_inc(v_ps, 1)
                                pe.wait_ge(k1_ready, OPEN + (b + 1) * 3)
                                pe.wait_ge(rest_ready, OPEN + (b + 1) * 3)
                            pe.wait_ge(v_ready, OPEN + (b + 1) * NV)
                            pe.wait_ge(packed_in, OPEN + (b + 1) * 2 * 2 * TERMS * 16)
                            pe.wait_ge(cleared, OPEN + (b + 1) * 2)
                            for n in range(MAXN):
                                if n >= 2:
                                    pe.wait_ge(max_done, OPEN + b * MAXN + n - 1)
                                if cross:
                                    p, a = n // 2, n % 2
                                    for t in range(3):
                                        k0 = t * (CTX // 3)
                                        mm = pe.matmul(ps[0:TOK, 3 * (n % 2) + t, 0:CTX // 3 + 1],
                                                       qx[:, p, a * TOK:(a + 1) * TOK], kx[:, p, k0:k0 + CTX // 3 + 1],
                                                       start=True, stop=True)
                                else:
                                    for i in range(4):
                                        p, a = (4 * n + i) // 2, i % 2
                                        mm = pe.matmul(ps[0:TOK, n % 2, i * TOK:(i + 1) * TOK],
                                                       qx[:, p, a * TOK:(a + 1) * TOK], kx[:, p, :],
                                                       start=True, stop=True)
                                mm.then_inc(max_ps, 1)
                            pe.wait_ge(shift_chain, OPEN + (b + 1) * 3)
                            pe.wait_ge(fin, OPEN + b * NFIN)
                            pe.transpose(ps[0:2 * MROWS * PAIRS, 6, 0:TOK],
                                         mcols[:, :, :, :].rearrange("q a i p -> q (a i p)"), ident[0:TOK, 0:TOK]).then_inc(shift_ps, 1)
                            pe.wait_ge(shift_in, OPEN + (b + 1) * 32)

                            def scores(n):
                                c, half_ = n // 2, n % 2
                                if n >= 3:
                                    pe.wait_ge(prob_ready, OPEN + b * NU + n - 2)
                                k0, kn = spans[c]
                                for i in range(4):
                                    p = 4 * half_ + i
                                    mm = pe.matmul(ps[0:kn, 2 * (n % 3) + i // 2, (i % 2) * 2 * TOK:(i % 2 + 1) * 2 * TOK],
                                                   kx[:, p, k0:k0 + kn], qx[:, p, :], start=True, stop=True)
                                mm.then_inc(score_ps, 1)

                            def values(n):
                                c, half_ = n // 2, n % 2
                                pe.wait_ge(prob_ready, OPEN + b * NU + n + 1)
                                kn = spans[c][1]
                                first, final = c == 0, c == len(spans) - 1
                                for i in range(2):
                                    g = 2 * half_ + i
                                    pr = prob[0:kn, n % 3, i * GT:(i + 1) * GT]
                                    pe.matmul(ps[32 * g:32 * g + 32, 6, 0:GT], v[0:kn, c, 32 * g:32 * g + 32], pr,
                                              start=first, stop=final, tile_position=(0, 32 * g))
                                    dg = (g + 2) % 4
                                    mm = pe.matmul(ps[32 * dg:32 * dg + 32, 7, 0:GT], ones[0:kn, :], pr,
                                                   start=first, stop=final, tile_position=(0, 32 * dg))
                                mm.then_inc(pv_done, 1)

                            pe.wait_ge(shift_ready, OPEN + b + 1)
                            for n in range(NU + 2):
                                if n < NU:
                                    scores(n)
                                if n >= 2:
                                    values(n - 2)

                    @block.scalar
                    def _(act):
                        with act.Fori(0, NB) as b:
                            if normed:
                                act.wait_ge(v_ps, OPEN + b * 3)
                                for t in range(3):
                                    n = min(BLK, CTX - t * BLK)
                                    act.wait_ge(xnT_ps, OPEN + b * 3 + t + 1)
                                    act.sem_inc(passed, 1)
                                    if modulated:
                                        act.activation(xt[:, t * BLK:t * BLK + n], ps[:, t, 0:n], ACT.Identity,
                                                       scale=MOD[:, 14, bass.ds(b, 1)], bias=MOD[:, 15, bass.ds(b, 1)]).then_inc(xt_ready, 1)
                                    else:
                                        act.activation(xt[:, t * BLK:t * BLK + n], ps[:, t, 0:n], ACT.Copy).then_inc(xt_ready, 1)
                            if cross:
                                act.wait_ge(packed_in, OPEN + b * 2 * 2 * TERMS * 16)
                                for t in range(3):
                                    n = min(BLK, CTX - t * BLK)
                                    act.wait_ge(k_ps, OPEN + b * 3 + t + 1)
                                    act.activation(kp[0][:, t * BLK:t * BLK + n], ps[:, kbank + t, 0:n], ACT.Identity,
                                                   bias=col(bk)).then_inc(k1_ready, 1)
                                act.wait_ge(pv_done, OPEN + b * NU)
                                for t in range(3):
                                    act.wait_ge(v_ps, OPEN + b * 3 + t + 1)
                                    m = 4 if t < 2 else 3
                                    act.activation(v[:, 4 * t:4 * t + m, :],
                                                   ps[0:KC, vbank + t, 0:m * P].rearrange("p (c d) -> p c d", c=m), ACT.Copy).then_inc(v_ready, 1)
                                act.activation(v[0:KLAST, CHUNKS - 1, :], ps[0:KLAST, vbank + 2, 3 * P:4 * P], ACT.Copy).then_inc(v_ready, 1)
                            else:
                                act.wait_ge(pv_done, OPEN + b * NU)
                                act.sem_inc(passed, 1)
                                act.activation(v[:, 0, :], V0[:, bass.ds(b, 1), :].rearrange("p o c -> p (o c)"), ACT.Copy).then_inc(v_ready, 1)
                            for n in range(NU):
                                kn = spans[n // 2][1]
                                act.wait_ge(score_ps, OPEN + b * NU + n + 1)
                                act.wait_ge(pv_done, OPEN + (b * NU + n - 2 if n >= 3 else b * NU))
                                act.activation(prob[0:kn, n % 3, :].rearrange("p (i c) -> p i c", i=2),
                                               ps[0:kn, 2 * (n % 3):2 * (n % 3) + 2, 0:GT], ACT.Exp, scale=ISQ).then_inc(prob_ready, 1)

                    @block.vector
                    def _(dve):
                        if normed:
                            dve.memset(mv[:, :, :], 0.0).then_inc(mv_zero, 1)
                            dve.wait_ge(mv_zero, OPEN + 1)
                        dve.wait_ge(prepared, OPEN + 3)
                        for a in range(2):
                            dve.memset(kx[a * SLOT:a * SLOT + MROWS, :, :], 1.0).then_inc(prepared, 1)
                        with dve.Fori(0, NB) as b:
                            dve.wait_ge(score_ps, OPEN + b * NU)
                            for a in range(2):
                                dve.memset(qx[a * SLOT:a * SLOT + MROWS, :, a * TOK:(a + 1) * TOK], 0.0).then_inc(cleared, 1)
                            if normed:
                                dve.wait_ge(ctx_in, OPEN + (b + 1) * 32)
                                for c in range(CHUNKS):
                                    dve.bn_stats(stats[0:chunk_rows(c), c, :], xn[0:chunk_rows(c), c, :]).then_inc(stats_done, 1)
                                for c in range(CHUNKS):
                                    dve.wait_ge(stats_done, OPEN + b * 2 * CHUNKS + CHUNKS)
                                    dve.sem_inc(passed, 1)
                                    dve.bn_aggr(mv[0:chunk_rows(c), c, :], stats[0:chunk_rows(c), c, :]).then_inc(stats_done, 1)
                                dve.wait_ge(stats_done, OPEN + (b + 1) * 2 * CHUNKS)
                                dve.tensor_scalar(ve[:, :], mv[:, :, 1], eps, None, ALU.add).then_inc(var_ready, 1)
                                dve.wait_ge(rstd_ready, OPEN + b + 1)
                                for c in range(CHUNKS):
                                    s = xn[0:chunk_rows(c), c, :]
                                    dve.tensor_scalar(s, s, mv[0:chunk_rows(c), c, 0:1], rstd[0:chunk_rows(c), c:c + 1],
                                                      ALU.subtract, ALU.mult).then_inc(xn_ready, 1)
                            if cross:
                                for t in range(3):
                                    n = min(BLK, CTX - t * BLK)
                                    s = slice(t * BLK, t * BLK + n)
                                    dve.wait_ge(k1_ready, OPEN + b * 3 + t + 1)
                                    dve.wait_ge(parts_ready, OPEN + b * NPART)
                                    dve.scalar_tensor_tensor(krest[:, s], ps[:, kbank + t, 0:n], col(bk), kp[0][:, s],
                                                             ALU.add, ALU.subtract).then_inc(rest_ready, 1)
                            for n in range(MAXN):
                                dve.wait_ge(max_ps, OPEN + b * MAXN + n + 1)
                                if cross:
                                    dve.tensor_reduce(nmax[:, n:n + 1], ps[0:TOK, 3 * (n % 2):3 * (n % 2) + 3, 0:CTX // 3 + 1],
                                                      AX.XY, ALU.max, negate=True).then_inc(max_done, 1)
                                else:
                                    dve.tensor_reduce(nmax[:, 4 * n:4 * n + 4], ps[0:TOK, n % 2, 0:GT].rearrange("p (h k) -> p h k", h=4),
                                                      AX.X, ALU.max, negate=True).then_inc(max_done, 1)
                            link = Chain(dve, shift_chain, b, 3)
                            dve.wait_ge(max_done, OPEN + (b + 1) * MAXN)
                            link(dve.tensor_copy(nmax1[:, :], nmax[:, :]))
                            hv = nmax1[:, :].rearrange("q (p a) -> q a p", a=2)
                            link(dve.tensor_copy(mcols[:, :, 0, :], hv))
                            link(dve.tensor_tensor(mcols[:, :, 1, :], nmax[:, :].rearrange("q (p a) -> q a p", a=2), hv, ALU.subtract))
                            dve.wait_ge(shift_ps, OPEN + b + 1)
                            dve.wait_ge(shift_in, OPEN + b * 32)
                            dve.tensor_copy(mrows[:, :], ps[0:2 * MROWS * PAIRS, 6, 0:TOK]).then_inc(shift_ready, 1)
                            dve.wait_ge(pv_done, OPEN + (b + 1) * NU)
                            flink = Chain(dve, fin, b, NFIN)
                            flink(dve.tensor_scalar(onat[:, :], ps[:, 6, 0:TOK], mask[:, 0:1], None, ALU.mult))
                            flink(dve.tensor_scalar(dnat[:, :], ps[:, 7, 0:TOK], mask[:, 0:1], None, ALU.mult))
                            for i in range(1, 4):
                                s = slice(i * TOK, (i + 1) * TOK)
                                flink(dve.scalar_tensor_tensor(onat[:, :], ps[:, 6, s], mask[:, i:i + 1], onat[:, :], ALU.mult, ALU.add))
                                flink(dve.scalar_tensor_tensor(dnat[:, :], ps[:, 7, s], mask[:, i:i + 1], dnat[:, :], ALU.mult, ALU.add))
                            flink(dve.reciprocal(rden[0:64, :], dnat[64:128, :]))
                            flink(dve.reciprocal(rden[64:128, :], dnat[0:64, :]))
                            flink(dve.tensor_tensor(onat[:, :], onat[:, :], rden[:, :], ALU.mult))
                            flink(dve.tensor_scalar(AT[:, bass.ds(b * TOK, TOK)], onat[:, :], col(bv), None, ALU.add))
                            assert flink.n == NFIN

        def pre2():
            with Stage("pre2") as st:
                W = st.sb("w", [P, 2 * P])
                w_in = st.sem("w_in")
                norm = Norm(st, "ln", 1e-5)
                q = st.sb("q", [P, GT])
                q_ps, q_ready, qk_ps, qk_out = st.sem("q_ps"), st.sem("q_ready"), st.sem("qk_ps"), st.sem("qk_out")
                ps = st.ps
                with st.block() as block:
                    @block.sync
                    def _(sp):
                        weights_in(sp, W, "pre2", w_in)

                    @block.vector
                    def _(dve):
                        with dve.Fori(0, NG) as g:
                            norm.vector(dve, g)
                            dve.wait_ge(norm.h_ready, OPEN + (g + 1) * GB)
                            dve.tensor_copy(KT[:, bass.ds(g * GT, GT)], norm.h[:, :]).then_inc(qk_out, 1)
                            dve.wait_ge(qk_ps, OPEN + g + 1)
                            dve.tensor_copy(QT[:, bass.ds(g * GT, GT)], ps[:, 2, 0:GT]).then_inc(qk_out, 1)

                    @block.gpsimd
                    def _(pool):
                        norm.gpsimd_init(pool)
                        with pool.Fori(0, NG) as g:
                            norm.gpsimd(pool, g)

                    @block.tensor
                    def _(pe):
                        pe.wait_ge(w_in, OPEN + 16)
                        with pe.Fori(0, NG) as g:
                            norm.tensor(pe, g, ps[:, 0, :])
                            pe.wait_ge(norm.h_ready, OPEN + (g + 1) * GB)
                            pe.matmul(ps[:, 1, 0:GT], W[:, 0:P], norm.h[:, :], start=True, stop=True).then_inc(q_ps, 1)
                            pe.wait_ge(q_ready, OPEN + g + 1)
                            pe.matmul(ps[:, 2, 0:GT], W[:, P:2 * P], q[:, :], start=True, stop=True).then_inc(qk_ps, 1)

                    @block.scalar
                    def _(act):
                        with act.Fori(0, NG) as g:
                            act.wait_ge(qk_out, OPEN + g * 2)
                            norm.scalar(act, g, ps[:, 0, :], by_col("ng2"), by_col("nb2"))
                            act.wait_ge(q_ps, OPEN + g + 1)
                            act.sem_inc(passed, 1)
                            act.activation(q[:, :], ps[:, 1, 0:GT], ACT.Copy).then_inc(q_ready, 1)

        def attend2():
            scale = float(P) ** -0.5
            with Stage("attend2") as st:
                ps = st.ps
                q = st.sb("q", [P, TOK])
                xt = st.sb("ctx_channels", [P, CTX])
                xn = st.sb("ctx_tokens", [KC, CHUNKS, P])
                prob = st.sb("prob", [TOK, CTX])
                probn = st.sb("prob_normal", [TOK, CTX])
                probT = st.sb("prob_turned", [KC, CHUNKS, TOK])
                mx = st.sb("minus_max", [TOK, 3])
                nm = st.sb("shift", [TOK, 1])
                den = st.sb("den", [TOK, 3])
                den1 = st.sb("den_sum", [TOK, 1])
                rden = st.sb("den_reciprocal", [TOK, 1])
                xt_in, xn_in = st.sem("xt_in"), st.sem("xn_in")
                q_ready, score_ps, chain = st.sem("q_ready"), st.sem("score_ps"), st.sem("chain")
                prob_ready, norm_ready, norm_chain = st.sem("prob_ready"), st.sem("norm_ready"), st.sem("norm_chain")
                turned_ps, turned_ready, o_ps, o_out = st.sem("turned_ps"), st.sem("turned_ready"), st.sem("o_ps"), st.sem("o_out")
                spans = [(t * BLK, min(BLK, CTX - t * BLK)) for t in range(3)]
                rows_of = [KC if c < CHUNKS - 1 else KLAST for c in range(CHUNKS)]
                with st.block() as block:
                    @block.sync
                    def _(sp):
                        with sp.Fori(0, NB) as b:
                            sp.wait_ge(score_ps, OPEN + b * 3)
                            sp.sem_inc(passed, 1)
                            sp.dma_start(xt[:, :], ctx_t[b]).then_inc(xt_in, 16)
                            sp.wait_ge(o_ps, OPEN + b)
                            sp.sem_inc(passed, 1)
                            sp.dma_start(xn[:, 0:CHUNKS - 1, :],
                                         ctx_n[b, 0:(CHUNKS - 1) * KC, :].rearrange("(c p) d -> p c d", p=KC)).then_inc(xn_in, 16)
                            sp.dma_start(xn[0:KLAST, CHUNKS - 1, :], ctx_n[b, (CHUNKS - 1) * KC:CTX, :]).then_inc(xn_in, 16)

                    @block.tensor
                    def _(pe):
                        with pe.Fori(0, NB) as b:
                            pe.wait_ge(xt_in, OPEN + (b + 1) * 16)
                            pe.wait_ge(q_ready, OPEN + b + 1)
                            pe.wait_ge(prob_ready, OPEN + b * 3)
                            for t, (k0, n) in enumerate(spans):
                                pe.matmul(ps[0:TOK, t, 0:n], q[:, :], xt[:, k0:k0 + n], start=True, stop=True).then_inc(score_ps, 1)
                            pe.wait_ge(turned_ready, OPEN + b * 4)
                            for t in range(3):
                                pe.wait_ge(norm_ready, OPEN + b * 3 + t + 1)
                                for c in range(4 * t, 4 * t + 4):
                                    tr = pe.transpose(ps[0:rows_of[c], 3 + t, (c % 4) * TOK:(c % 4 + 1) * TOK],
                                                      probn[:, c * KC:c * KC + rows_of[c]], ident[0:TOK, 0:TOK])
                                tr.then_inc(turned_ps, 1)
                            pe.wait_ge(xn_in, OPEN + (b + 1) * 32)
                            pe.wait_ge(o_out, OPEN + b)
                            for c in range(CHUNKS):
                                if c % 4 == 0:
                                    pe.wait_ge(turned_ready, OPEN + (b * 4 + (c // 4 + 1 if c < 8 else 4)))
                                mm = pe.matmul(ps[:, 6, 0:TOK], xn[0:rows_of[c], c, :], probT[0:rows_of[c], c, :],
                                               start=(c == 0), stop=(c == CHUNKS - 1))
                            mm.then_inc(o_ps, 1)

                    @block.scalar
                    def _(act):
                        with act.Fori(0, NB) as b:
                            act.wait_ge(score_ps, OPEN + b * 3)
                            act.sem_inc(passed, 1)
                            act.activation(q[:, :], QT[:, bass.ds(b * TOK, TOK)], ACT.Copy).then_inc(q_ready, 1)
                            act.wait_ge(chain, OPEN + (b + 1) * 5)
                            for t, (k0, n) in enumerate(spans):
                                act.activation(prob[:, k0:k0 + n], ps[0:TOK, t, 0:n], ACT.Exp, scale=scale,
                                               bias=nm[:, 0:1], accum_out=den[:, t:t + 1]).then_inc(prob_ready, 1)
                            act.wait_ge(o_ps, OPEN + b)
                            for t in range(3):
                                act.wait_ge(turned_ps, OPEN + b * 3 + t + 1)
                                m = 4 if t < 2 else 3
                                act.activation(probT[:, 4 * t:4 * t + m, :],
                                               ps[0:KC, 3 + t, 0:m * TOK].rearrange("p (c q) -> p c q", c=m), ACT.Copy).then_inc(turned_ready, 1)
                            act.activation(probT[0:KLAST, CHUNKS - 1, :], ps[0:KLAST, 5, 3 * TOK:4 * TOK], ACT.Copy).then_inc(turned_ready, 1)

                    @block.vector
                    def _(dve):
                        with dve.Fori(0, NB) as b:
                            link = Chain(dve, chain, b, 5)
                            for t, (k0, n) in enumerate(spans[:2]):
                                dve.wait_ge(score_ps, OPEN + b * 3 + t + 1)
                                link(dve.tensor_reduce(mx[:, t:t + 1], ps[0:TOK, t, 0:n], AX.X, ALU.max))
                            dve.wait_ge(score_ps, OPEN + b * 3 + 3)
                            link(dve.tensor_reduce(mx[:, 2:3], ps[0:TOK, 2, 0:spans[2][1]], AX.X, ALU.max))
                            link(dve.tensor_reduce(nm[:, 0:1], mx[:, :], AX.X, ALU.max, negate=True))
                            link(dve.tensor_scalar(nm[:, 0:1], nm[:, 0:1], scale, None, ALU.mult))
                            dve.wait_ge(prob_ready, OPEN + b * 3 + 3)
                            dlink = Chain(dve, norm_chain, b, 2)
                            dlink(dve.tensor_reduce(den1[:, 0:1], den[:, :], AX.X, ALU.add))
                            dlink(dve.reciprocal(rden[:, 0:1], den1[:, 0:1]))
                            for t, (k0, n) in enumerate(spans):
                                dve.tensor_scalar(probn[:, k0:k0 + n], prob[:, k0:k0 + n], rden[:, 0:1], None, ALU.mult).then_inc(norm_ready, 1)
                            dve.wait_ge(o_ps, OPEN + b + 1)
                            dve.tensor_copy(AT[:, bass.ds(b * TOK, TOK)], ps[:, 6, 0:TOK]).then_inc(o_out, 1)

        def experts():
            a, n = 0, {}
            for key, width in [("wv", P), ("router", 9), ("w1", 18 * P), ("gw1", 3 * P), ("w2", 6 * P), ("gw2", P), ("out", P)]:
                n[key] = a
                a += width
            with Stage("experts") as st:
                ps = st.ps
                W = st.sb("w", [P, a])
                R = st.sb("rows", [TOK, ROWS.width])
                comb = st.sb("combined", [P, 3, GT])
                hid = st.sb("hidden", [P, 7, GT])
                probs = st.sb("probs", [TOK, GB, 3])
                logit = st.sb("logits", [TOK, GB, 3])
                lmax = st.sb("logit_max", [TOK, GB])
                lsum = st.sb("logit_sum", [TOK, GB])
                lrec = st.sb("logit_rec", [TOK, GB])
                eo = st.sb("expert_out", [TOK, GB, 3 * P])
                routed = st.sb("routed", [TOK, GB, P])
                gp = st.sb("gate_pre", [TOK, GB, P])
                gt = st.sb("gate_tanh", [TOK, GB, P])
                gate = st.sb("gate", [TOK, GB, P])
                rT = st.sb("routed_turned", [P, GT])
                dx = st.sb("delta", [TOK, GB, P])
                w_in = st.sem("w_in")
                ev_ps, comb_ready = st.sem("ev_ps"), st.sem("comb_ready")
                logit_ps, lchain, exp_ready = st.sem("logit_ps"), st.sem("logit_chain"), st.sem("exp_ready")
                hid_ps, hid_ready = st.sem("hid_ps"), st.sem("hid_ready")
                eo_ps, eo_out = st.sem("eo_ps"), st.sem("eo_out")
                gp_ready, tanh_ready, rchain = st.sem("gp_ready"), st.sem("tanh_ready"), st.sem("routed_chain")
                rT_ps, rT_ready, out_ps, out_chain = st.sem("rT_ps"), st.sem("rT_ready"), st.sem("out_ps"), st.sem("out_chain")

                def row(name, shape):
                    r0, r1 = ROWS[name]
                    return R[:, r0:r1].rearrange("p (o c) -> p o c", o=1).to_broadcast(shape)

                with st.block() as block:
                    @block.sync
                    def _(sp):
                        weights_in(sp, W, "moe", w_in)
                        sp.dma_start(R[:, :], rows.to_broadcast([TOK, ROWS.width])).then_inc(w_in, 16)

                    @block.vector
                    def _(dve):
                        dve.wait_ge(w_in, OPEN + 32)
                        with dve.Fori(0, NG) as g:
                            dve.tensor_copy(comb[:, 0, :], KT[:, bass.ds(g * GT, GT)]).then_inc(comb_ready, 1)
                            dve.tensor_copy(comb[:, 2, :].rearrange("p (k t) -> p k t", k=GB),
                                            COND[:, bass.ds(g * GB, GB)].rearrange("p (k o) -> p k o", o=1).to_broadcast([P, GB, TOK])).then_inc(comb_ready, 1)
                            dve.wait_ge(ev_ps, OPEN + g + 1)
                            dve.tensor_copy(comb[:, 1, :], ps[:, 0, 0:GT]).then_inc(comb_ready, 1)
                            link = Chain(dve, lchain, g, 3)
                            dve.wait_ge(logit_ps, OPEN + g + 1)
                            link(dve.tensor_tensor(logit[:, :, :], ps[0:TOK, 1, 0:GB * 3].rearrange("p (k e) -> p k e", k=GB),
                                                   row("router", [TOK, GB, 3]), ALU.add))
                            link(dve.tensor_reduce(lmax[:, :], logit[:, :, :], AX.X, ALU.max))
                            link(dve.tensor_tensor(logit[:, :, :], logit[:, :, :],
                                                   lmax[:, :].rearrange("p (k o) -> p k o", o=1).to_broadcast([TOK, GB, 3]), ALU.subtract))
                            dve.wait_ge(exp_ready, OPEN + g + 1)
                            link = Chain(dve, rchain, g, 3 + 3 * GB)
                            link(dve.tensor_reduce(lsum[:, :], probs[:, :, :], AX.X, ALU.add))
                            link(dve.reciprocal(lrec[:, :], lsum[:, :]))
                            link(dve.tensor_tensor(probs[:, :, :], probs[:, :, :],
                                                   lrec[:, :].rearrange("p (k o) -> p k o", o=1).to_broadcast([TOK, GB, 3]), ALU.mult))
                            for k in range(GB):
                                dve.wait_ge(eo_ps, OPEN + g * GB + k + 1)
                                bank = ps[0:TOK, 4 + k, :]
                                dve.tensor_tensor(eo[:, k, :], bank[:, 0:3 * P], R[:, ROWS["eb2"][0]:ROWS["eb2"][1]], ALU.add).then_inc(eo_out, 1)
                                dve.tensor_tensor(gp[:, k, :], bank[:, 3 * P:4 * P], R[:, ROWS["gb2"][0]:ROWS["gb2"][1]], ALU.add).then_inc(gp_ready, 1)
                            for k in range(GB):
                                dve.wait_ge(eo_out, OPEN + g * GB + k + 1)
                                link(dve.tensor_scalar(routed[:, k, :], eo[:, k, 0:P], probs[:, k, 0:1], None, ALU.mult))
                                for e in (1, 2):
                                    link(dve.scalar_tensor_tensor(routed[:, k, :], eo[:, k, e * P:(e + 1) * P], probs[:, k, e:e + 1],
                                                                  routed[:, k, :], ALU.mult, ALU.add))
                            olink = Chain(dve, out_chain, g, 4)
                            dve.wait_ge(tanh_ready, OPEN + g + 1)
                            olink(dve.tensor_scalar(gate[:, :, :], gt[:, :, :], 0.5, 0.5, ALU.mult, ALU.add))
                            dve.wait_ge(out_ps, OPEN + g + 1)
                            olink(dve.tensor_tensor(dx[:, :, :], ps[0:TOK, 3, 0:GB * P].rearrange("p (k c) -> p k c", k=GB),
                                                    row("outb", [TOK, GB, P]), ALU.add))
                            olink(dve.tensor_tensor(dx[:, :, :], dx[:, :, :], gate[:, :, :], ALU.mult))
                            xs = X[:, bass.ds(g * GB, GB), :]
                            olink(dve.tensor_tensor(xs, xs, dx[:, :, :], ALU.add))

                    @block.tensor
                    def _(pe):
                        pe.wait_ge(w_in, OPEN + 32)

                        def over_inputs(o, w0, width, dst_cols=None):
                            for i in range(3):
                                mm = pe.matmul(o, W[:, w0 + i * width:w0 + i * width + P], comb[:, i, :], start=(i == 0), stop=(i == 2))
                            return mm

                        with pe.Fori(0, NG) as g:
                            pe.wait_ge(out_chain, OPEN + g * 4)
                            pe.matmul(ps[:, 0, 0:GT], W[:, n["wv"]:n["wv"] + P], AT[:, bass.ds(g * GT, GT)], start=True, stop=True).then_inc(ev_ps, 1)
                            pe.wait_ge(comb_ready, OPEN + (g + 1) * 3)
                            for k in range(GB):
                                for i in range(3):
                                    mm = pe.matmul(ps[0:TOK, 1, 3 * k:3 * k + 3], comb[:, i, k * TOK:(k + 1) * TOK],
                                                   W[:, n["router"] + 3 * i:n["router"] + 3 * i + 3], start=(i == 0), stop=(i == 2))
                            mm.then_inc(logit_ps, 1)
                            for j in range(7):
                                if j >= 2:
                                    pe.wait_ge(hid_ready, OPEN + g * 7 + j - 1)
                                o = ps[:, 2 + j % 2, 0:GT]
                                if j < 6:
                                    over_inputs(o, n["w1"] + (j // 2) * 6 * P + (j % 2) * P, 2 * P).then_inc(hid_ps, 1)
                                else:
                                    over_inputs(o, n["gw1"], P).then_inc(hid_ps, 1)
                            pe.wait_ge(hid_ready, OPEN + (g + 1) * 7)
                            for k in range(GB):
                                s = slice(k * TOK, (k + 1) * TOK)
                                bank = ps[0:TOK, 4 + k, :]
                                for e in range(3):
                                    for i in range(2):
                                        pe.matmul(bank[:, e * P:(e + 1) * P], hid[:, 2 * e + i, s],
                                                  W[:, n["w2"] + (2 * e + i) * P:n["w2"] + (2 * e + i + 1) * P], start=(i == 0), stop=(i == 1))
                                pe.matmul(bank[:, 3 * P:4 * P], hid[:, 6, s], W[:, n["gw2"]:n["gw2"] + P], start=True, stop=True).then_inc(eo_ps, 1)
                            for k in range(GB):
                                pe.wait_ge(rchain, OPEN + g * (3 + 3 * GB) + 3 + 3 * (k + 1))
                                tr = pe.transpose(ps[:, 2, k * TOK:(k + 1) * TOK], routed[:, k, :], ident[0:TOK, 0:TOK])
                            tr.then_inc(rT_ps, 1)
                            pe.wait_ge(rT_ready, OPEN + g + 1)
                            for k in range(GB):
                                mm = pe.matmul(ps[0:TOK, 3, k * P:(k + 1) * P], rT[:, k * TOK:(k + 1) * TOK],
                                               W[:, n["out"]:n["out"] + P], start=True, stop=True)
                            mm.then_inc(out_ps, 1)

                    @block.scalar
                    def _(act):
                        with act.Fori(0, NG) as g:
                            act.wait_ge(lchain, OPEN + (g + 1) * 3)
                            act.activation(probs[:, :, :], logit[:, :, :], ACT.Exp).then_inc(exp_ready, 1)
                            for j in range(7):
                                act.wait_ge(hid_ps, OPEN + g * 7 + j + 1)
                                act.activation(hid[:, j, :], ps[:, 2 + j % 2, 0:GT], ACT.Silu,
                                               bias=col("eb1", j) if j < 6 else col("gb1")).then_inc(hid_ready, 1)
                            act.wait_ge(gp_ready, OPEN + (g + 1) * GB)
                            act.activation(gt[:, :, :], gp[:, :, :], ACT.Tanh, scale=0.5).then_inc(tanh_ready, 1)
                            act.wait_ge(rT_ps, OPEN + g + 1)
                            act.activation(rT[:, :], ps[:, 2, 0:GT], ACT.Copy).then_inc(rT_ready, 1)

        def pre3():
            with Stage("pre3") as st:
                W = st.sb("w", [P, P])
                w_in = st.sem("w_in")
                norm = Norm(st, "ln", 1e-5)
                q_ps, q_out = st.sem("q_ps"), st.sem("q_out")
                ps = st.ps
                with st.block() as block:
                    @block.sync
                    def _(sp):
                        weights_in(sp, W, "pre3", w_in)

                    @block.vector
                    def _(dve):
                        with dve.Fori(0, NG) as g:
                            dve.wait_ge(norm.xnT_ready, OPEN + g)
                            dve.sem_inc(passed, 1)
                            norm.vector(dve, g)

                    @block.gpsimd
                    def _(pool):
                        norm.gpsimd_init(pool)
                        with pool.Fori(0, NG) as g:
                            norm.gpsimd(pool, g)

                    @block.tensor
                    def _(pe):
                        pe.wait_ge(w_in, OPEN + 16)
                        with pe.Fori(0, NG) as g:
                            norm.tensor(pe, g, ps[:, 2, :])
                            pe.wait_ge(norm.h_ready, OPEN + (g + 1) * GB)
                            pe.wait_ge(q_out, OPEN + g)
                            pe.matmul(ps[:, 3, 0:GT], W[:, :], norm.h[:, :], start=True, stop=True).then_inc(q_ps, 1)

                    @block.scalar
                    def _(act):
                        with act.Fori(0, NG) as g:
                            norm.scalar(act, g, ps[:, 2, :], by_mod(12), by_mod(13))
                            act.wait_ge(q_ps, OPEN + g + 1)
                            act.sem_inc(passed, 1)
                            act.activation(QT[:, bass.ds(g * GT, GT)], ps[:, 3, 0:GT], ACT.Identity, bias=col("bq3")).then_inc(q_out, 1)

        def post3():
            with Stage("post3") as st:
                W = st.sb("w", [P, P])
                w_in, out_done = st.sem("w_in"), st.sem("out_done")
                res = Residual(st, "o", "bo3", None)
                ps = st.ps
                with st.block() as block:
                    @block.sync
                    def _(sp):
                        weights_in(sp, W, "post3", w_in)
                        with sp.Fori(0, NG) as g:
                            sp.wait_ge(res.x_ready, OPEN + g + 1)
                            sp.sem_inc(passed, 1)
                            sp.dma_start(out[bass.ds(g * GB, GB)].rearrange("b t c -> t b c"),
                                         X[:, bass.ds(g * GB, GB), :]).then_inc(out_done, 16)
                        sp.wait_ge(out_done, OPEN + 16 * NG)

                    @block.vector
                    def _(dve):
                        with dve.Fori(0, NG) as g:
                            res.vector_gate(dve, g, ps[:, 0, :])
                            res.vector_add(dve, g, ps[:, 1, :])

                    @block.tensor
                    def _(pe):
                        pe.wait_ge(w_in, OPEN + 16)
                        with pe.Fori(0, NG) as g:
                            pe.wait_ge(res.x_ready, OPEN + g)
                            pe.matmul(ps[:, 0, 0:GT], W[:, 0:P], AT[:, bass.ds(g * GT, GT)], start=True, stop=True).then_inc(res.y_ps, 1)
                            res.tensor(pe, g, ps[:, 1, :])

        stages = [
            lambda: pre("pre0", "pre0", by_mod(1), by_mod(0), 1e-6, "bk0", "bq0"),
            lambda: attend("self0", bv="bv0"),
            lambda: mid("mid0", "mid0", "bo0", by_mod(2), by_col("ng0"), by_col("nb0"), "bqc0"),
            lambda: attend("cross0", kv="kv0", bk="bkc0", bv="bvc0"),
            lambda: post("post0", "post0", "boc0", by_mod(4), by_mod(3), "b10", "b20", by_mod(5)),
            lambda: pre("pre1", "pre1", by_mod(7), by_mod(6), 1e-6, "bk1", "bq1"),
            lambda: attend("self1", bv="bv1"),
            lambda: mid("mid1", "mid1", "bo1", by_mod(8), None, None, "bqc1"),
            lambda: attend("cross1", kv="kv1", normed=True, bk="bkc1", bv="bvc1"),
            lambda: post("post1", "post1", "boc1", by_mod(10), by_mod(9), "b11", "b21", by_mod(11)),
            pre2, attend2, experts, pre3,
            lambda: attend("cross3", kv="kv3", normed=True, bk="bkc3", bv="bvc3", eps=1e-5, modulated=True),
            post3,
        ]
        for s in stages[:last]:
            s()
        if probe is not None:
            probe(nc, dict(X=X, QT=QT, KT=KT, V0=V0, AT=AT, MOD=MOD))


def layout(t):
    L0, L1, L2, L3 = ({k[len(f"L{n}_xcond_"):]: v for k, v in t.items() if k.startswith(f"L{n}_xcond_")} for n in range(4))

    def blocks(w):
        n = w.shape[0] // P
        return [w[i * P:(i + 1) * P] for i in range(n)]

    def cat(*parts):
        return np.concatenate([np.ascontiguousarray(x) for x in parts], axis=1)

    kvc = L1["W_kvc"]
    groups = {
        "mod": cat(L0["ada_w"], L1["W_mod"], L3["Wss_q"], L3["Wss_kv"]),
        "pre0": cat(L0["qkv_w"][:, P:2 * P][:, PERM], L0["qkv_w"][:, 2 * P:], L0["qkv_w"][:, :P][:, PERM]),
        "mid0": cat(L0["self_o_w"], L0["q_w"][:, PERM]),
        "kv0": cat(L0["kv_w"][:, :P][:, PERM], L0["kv_w"][:, P:]),
        "post0": cat(L0["cross_o_w"], L0["mlp_w1"], *blocks(L0["mlp_w2"])),
        "pre1": cat(L1["W_qkv"][:, P:2 * P][:, PERM], L1["W_qkv"][:, 2 * P:], L1["W_qkv"][:, :P][:, PERM]),
        "mid1": cat(L1["W_proj"], L1["W_qc"][:, PERM]),
        "kv1": cat(kvc[:, :P][:, PERM], kvc[:, P:]),
        "post1": cat(L1["W_cproj"], L1["W_mlp1"], *blocks(L1["W_mlp2"])),
        "pre2": cat(L2["Wq"], L2["Wk"].T),
        "moe": cat(L2["Wv"], *blocks(L2["router_W"]), *[b for e in range(3) for b in blocks(L2["e_w1"][e])],
                   *blocks(L2["gate_w1"]), *[b for e in range(3) for b in blocks(L2["e_w2"][e])],
                   L2["gate_w2"], L2["out_w"]),
        "pre3": L3["Wq"][:, PERM],
        "kv3": cat(L3["Wkv"][:, :P][:, PERM], L3["Wkv"][:, P:]),
        "post3": L3["Wp"],
    }
    for n, g in groups.items():
        a, b = WEIGHTS[n]
        assert g.shape == (P, b - a), (n, g.shape, b - a)

    def columns(v):
        return np.ascontiguousarray(v.reshape(-1, P).T)

    cols = {
        "mod": cat(columns(L0["ada_b"]), columns(L1["b_mod"]), columns(L3["bss_q"]), columns(L3["bss_kv"])),
        "bq0": columns(L0["qkv_b"][:P][PERM]), "bk0": columns(L0["qkv_b"][P:2 * P][PERM]), "bv0": columns(L0["qkv_b"][2 * P:]),
        "bo0": columns(L0["self_o_b"]), "ng0": columns(L0["norm2_g"]), "nb0": columns(L0["norm2_b"]),
        "bqc0": columns(L0["q_b"][PERM]), "bkc0": columns(L0["kv_b"][:P][PERM]), "bvc0": columns(L0["kv_b"][P:]),
        "boc0": columns(L0["cross_o_b"]), "b10": columns(L0["mlp_b1"]), "b20": columns(L0["mlp_b2"]),
        "bq1": columns(L1["b_qkv"][:P][PERM]), "bk1": columns(L1["b_qkv"][P:2 * P][PERM]), "bv1": columns(L1["b_qkv"][2 * P:]),
        "bo1": columns(L1["b_proj"]), "bqc1": columns(L1["b_qc"][PERM]), "bkc1": columns(L1["b_kvc"][:P][PERM]),
        "bvc1": columns(L1["b_kvc"][P:]), "boc1": columns(L1["b_cproj"]), "b11": columns(L1["b_mlp1"]), "b21": columns(L1["b_mlp2"]),
        "ng2": columns(L2["ln_gamma"]), "nb2": columns(L2["ln_beta"]), "eb1": columns(L2["e_b1"]), "gb1": columns(L2["gate_b1"]),
        "bq3": columns(L3["bq"][PERM]), "bkc3": columns(L3["bkv"][:P][PERM]), "bvc3": columns(L3["bkv"][P:]), "bo3": columns(L3["bp"]),
    }
    assert list(cols) == list(COLS.at)
    rows = [L2["router_b"], L2["e_b2"].reshape(-1), L2["gate_b2"], L2["out_b"]]
    lane = np.arange(P)
    own = (lane[:, None] // DH % 4 == np.arange(4)[None, :])
    arrays = {
        "x": t["x"],
        "ctx_t": np.swapaxes(t["ctx_1024"], 1, 2),
        "ctx_n": t["ctx_1024"],
        "cond_t": t["cond_1024"].T,
        "weights": cat(*groups.values()),
        "cols": cat(*cols.values()),
        "rows": np.concatenate(rows)[None, :],
        "const": cat(np.eye(P, dtype=np.float32), own.astype(np.float32)),
    }
    return {k: np.ascontiguousarray(v) for k, v in arrays.items()}, t["x"].shape


def kernel(**inputs):
    import numpy as _np
    import concourse.bacc as _bacc
    from concourse import mybir as _mybir
    from concourse.bass_utils import run_bass_kernel_spmd as _run

    arrays, shape = layout({k: _np.asarray(v) for k, v in inputs.items()})
    nc = _bacc.Bacc("TRN2", target_bir_lowering=False, num_devices=1)
    aps = {n: nc.dram_tensor(f"in_{n}", a.shape, _mybir.dt.float32, kind="ExternalInput").ap() for n, a in arrays.items()}
    out = nc.dram_tensor("out_0", shape, _mybir.dt.float32, kind="ExternalOutput").ap()
    build(nc, out=out, NB=shape[0], **aps)
    r = _run(nc, [{f"in_{n}": a for n, a in arrays.items()}], core_ids=[0])
    return r.results[0]["out_0"]
```

```python
from contextlib import ExitStack

import numpy as np
import concourse.bass as bass
from concourse import mybir

F32 = mybir.dt.float32
BF16 = mybir.dt.bfloat16
ALU = mybir.AluOpType
ACT = mybir.ActivationFunctionType
AX = mybir.AxisListType

P = 128
TOK = 100
CTX = 1444
HEADS = 16
DH = 8
PAIRS = HEADS // 2
GB = 4
GT = GB * TOK
KC = 121
CHUNKS = -(-CTX // KC)
KLAST = CTX - (CHUNKS - 1) * KC
BLK = 4 * KC
ISQ = float(DH) ** -0.5
SLOT = 64
MROWS = 2
TERMS = 6
K_PART = (0, 0, 0, 1, 1, 2)
Q_PART = (0, 1, 2, 0, 1, 0)
QBLK = CTX // 4

OPEN = 1
COLT = 4
NHALF = PAIRS // COLT
PERM = [(2 * p + a) * DH + d for a in range(2) for d in range(DH) for p in range(PAIRS)]


class Layout:

    def __init__(self):
        self.at, self.width = {}, 0

    def add(self, name, n):
        self.at[name] = (self.width, self.width + n)
        self.width += n

    def __getitem__(self, name):
        return self.at[name]


WEIGHTS = Layout()
COLS = Layout()
ROWS = Layout()
CONST = Layout()

for _name, _n in [("mod", 16 * P),
                  ("pre0", 3 * P), ("mid0", 3 * P), ("kv0", 2 * P), ("post0", 10 * P),
                  ("pre1", 3 * P), ("mid1", 3 * P), ("kv1", 2 * P), ("post1", 10 * P),
                  ("pre2", 2 * P), ("moe", P + 9 + 18 * P + 3 * P + 6 * P + 2 * P),
                  ("pre3", P), ("kv3", 2 * P), ("post3", 2 * P)]:
    WEIGHTS.add(_name, _n)
for _name, _n in [("mod", 16), ("bq0", 1), ("bk0", 1), ("bv0", 2), ("bo0", 1), ("ng0", 1), ("nb0", 1), ("bqc0", 1),
                  ("bkc0", 1), ("bvc0", 2), ("boc0", 1), ("b10", 4), ("b20", 1),
                  ("bq1", 1), ("bk1", 1), ("bv1", 2), ("bo1", 1), ("bqc1", 1),
                  ("bkc1", 1), ("bvc1", 2), ("boc1", 1), ("b11", 4), ("b21", 1),
                  ("ng2", 1), ("nb2", 1), ("eb1", 6), ("gb1", 1),
                  ("bq3", 1), ("bkc3", 1), ("bvc3", 2), ("bo3", 1)]:
    COLS.add(_name, _n)
for _name, _n in [("router", 3), ("eb2", 3 * P), ("gb2", P), ("outb", P)]:
    ROWS.add(_name, _n)
CONST.add("ident", P)
CONST.add("mask", 2)


def build(nc, x, ctx_t, ctx_n, cond_t, weights, cols, rows, const, out, NB, last=99, probe=None):
    NG = NB // GB
    with ExitStack() as top:
        def keep(name, shape, dt=F32):
            return top.enter_context(nc.sbuf_tensor(name, shape, dt))

        X = keep("x_tokens", [TOK, NB, P])
        QT = keep("q_channels", [P, NB * TOK])
        AT = keep("attn_channels", [P, NHALF, NB * TOK])
        MOD = keep("modulation", [P, 16, NB])
        COND = keep("cond", [P, NB])
        C = keep("bias_columns", [P, COLS.width])
        K = keep("constants", [P, CONST.width])
        passed = top.enter_context(nc.semaphore("passed"))
        ctx_in = top.enter_context(nc.semaphore("ctx_in"))
        ident = K[:, CONST["ident"][0]:CONST["ident"][1]]
        mask = K[:, CONST["mask"][0]:CONST["mask"][1]]

        def col(name, n=0, rows=P):
            return C[0:rows, COLS[name][0] + n:COLS[name][0] + n + 1]

        class Stage:

            def __init__(self, name):
                self.name = name

            def __enter__(self):
                self.stack = ExitStack()
                self.sems = []
                self.ps = self.stack.enter_context(nc.psum_tensor(f"{self.name}_psum", [P, 8, 512], F32))
                return self

            def sb(self, name, shape, dt=F32):
                return self.stack.enter_context(nc.sbuf_tensor(f"{self.name}_{name}", shape, dt))

            def sem(self, name):
                s = self.stack.enter_context(nc.semaphore(f"{self.name}_{name}"))
                self.sems.append(s)
                return s

            def block(self):
                for s in self.sems:
                    nc.gpsimd.sem_inc(s, 1)
                nc.all_engine_barrier()
                return nc.Block()

            def __exit__(self, *a):
                if a[0] is None:
                    nc.all_engine_barrier()
                    for s in self.sems:
                        nc.gpsimd.sem_clear(s)
                    nc.all_engine_barrier()
                self.stack.close()

        class Chain:

            def __init__(self, eng, sem, it, per, own=False):
                self.eng, self.sem, self.it, self.per, self.n, self.own = eng, sem, it, per, 0, own

            def __call__(self, ins):
                self.n += 1
                ins.then_inc(self.sem, 1)
                if self.own:
                    self.eng.wait_ge(self.sem, OPEN + self.it * self.per + self.n)
                    self.eng.sem_inc(passed, 1)
                else:
                    self.eng.wait_ge(self.sem, OPEN + self.it * self.per + self.n)

        def weights_in(sp, tile, name, sem):
            a, b = WEIGHTS[name]
            sp.dma_start(tile[:, :], weights[:, a:b]).then_inc(sem, 16)

        with Stage("mods") as st:
            W = st.sb("w", [P, 16 * P])
            SC = st.sb("silu_cond", [P, NB])
            x_in = st.sem("x_in")
            constants_in = st.sem("constants_in")
            w_in = st.sem("w_in")
            silu_ready = st.sem("silu_ready")
            mod_ps = st.sem("mod_ps")
            mod_ready = st.sem("mod_ready")
            with st.block() as block:
                @block.sync
                def _(sp):
                    sp.dma_start(COND[:, :], cond_t).then_inc(constants_in, 16)
                    sp.dma_start(C[:, :], cols).then_inc(constants_in, 16)
                    sp.dma_start(K[:, :], const).then_inc(constants_in, 16)
                    weights_in(sp, W, "mod", w_in)
                    sp.dma_start(X[:, :, :], x.rearrange("b t c -> t b c")).then_inc(x_in, 16)
                    sp.wait_ge(x_in, OPEN + 16)

                @block.scalar
                def _(act):
                    act.wait_ge(constants_in, OPEN + 48)
                    act.activation(SC[:, :], COND[:, :], ACT.Silu).then_inc(silu_ready, 1)

                @block.tensor
                def _(pe):
                    pe.wait_ge(silu_ready, OPEN + 1)
                    pe.wait_ge(w_in, OPEN + 16)
                    for k in range(16):
                        mm = pe.matmul(st.ps[:, 0, k * NB:(k + 1) * NB], W[:, k * P:(k + 1) * P], SC[:, :],
                                       start=True, stop=True)
                    mm.then_inc(mod_ps, 1)

                @block.vector
                def _(dve):
                    dve.wait_ge(mod_ps, OPEN + 1)
                    b0 = COLS["mod"][0]
                    dve.tensor_tensor(MOD[:, :, :], st.ps[:, 0, 0:16 * NB].rearrange("p (k b) -> p k b", k=16),
                                      C[:, b0:b0 + 16].rearrange("p (k o) -> p k o", o=1).to_broadcast([P, 16, NB]), ALU.add).then_inc(mod_ready, 1)
                    dve.wait_ge(mod_ready, OPEN + 1)
                    for n in (1, 4, 7, 10, 12, 14):
                        dve.tensor_scalar(MOD[:, n, :], MOD[:, n, :], 1.0, None, ALU.add).then_inc(mod_ready, 1)
                    dve.wait_ge(mod_ready, OPEN + 7)

        class Norm:

            def __init__(self, st, tag, eps):
                self.eps = eps
                self.stats = st.sb(tag + "_stats", [TOK, GB, 6])
                self.mv = st.sb(tag + "_mean_var", [TOK, GB, 2])
                self.ve = st.sb(tag + "_var_eps", [TOK, GB])
                self.half = st.sb(tag + "_minus_half", [TOK, GB])
                self.rstd = st.sb(tag + "_rstd", [TOK, GB])
                self.xn = st.sb(tag + "_xn", [TOK, GB, P])
                self.h = st.sb(tag + "_h", [P, GT])
                self.stats_done = st.sem(tag + "_stats_done")
                self.var_ready = st.sem(tag + "_var_ready")
                self.rstd_ready = st.sem(tag + "_rstd_ready")
                self.xn_ready = st.sem(tag + "_xn_ready")
                self.xnT_ready = st.sem(tag + "_xnT_ready")
                self.h_ready = st.sem(tag + "_h_ready")

            def vector(self, dve, g):
                for k in range(GB):
                    ins = dve.bn_stats(self.stats[:, k, :], X[:, g * GB + k, :])
                    ins.then_inc(self.stats_done, 1)
                for k in range(GB):
                    dve.wait_ge(self.stats_done, OPEN + g * 2 * GB + GB)
                    dve.sem_inc(passed, 1)
                    dve.bn_aggr(self.mv[:, k, :], self.stats[:, k, :]).then_inc(self.stats_done, 1)
                dve.wait_ge(self.stats_done, OPEN + g * 2 * GB + 2 * GB)
                dve.tensor_scalar(self.ve[:, :], self.mv[:, :, 1], self.eps, None, ALU.add).then_inc(self.var_ready, 1)
                dve.wait_ge(self.rstd_ready, OPEN + g + 1)
                for k in range(GB):
                    dve.tensor_scalar(self.xn[:, k, :], X[:, g * GB + k, :], self.mv[:, k, 0:1],
                                      self.rstd[:, k:k + 1], ALU.subtract, ALU.mult).then_inc(self.xn_ready, 1)

            def gpsimd_init(self, pool):
                pool.memset(self.half[:, :], -0.5).then_inc(self.var_ready, 1)

            def gpsimd(self, pool, g):
                pool.wait_ge(self.var_ready, OPEN + g + 2)
                pool.tensor_tensor(self.rstd[:, :], self.ve[:, :], self.half[:, :], ALU.pow).then_inc(self.rstd_ready, 1)

            def tensor(self, pe, g, bank):
                for k in range(GB):
                    pe.wait_ge(self.xn_ready, OPEN + g * GB + k + 1)
                    tr = pe.transpose(bank[:, k * TOK:(k + 1) * TOK], self.xn[:, k, :], ident[0:TOK, 0:TOK])
                tr.then_inc(self.xnT_ready, 1)

            def scalar(self, act, g, bank, scale, shift):
                act.wait_ge(self.xnT_ready, OPEN + g + 1)
                act.sem_inc(passed, 1)
                if scale is None:
                    act.activation(self.h[:, :], bank[:, 0:GT], ACT.Copy).then_inc(self.h_ready, GB)
                    return
                for k in range(GB):
                    act.activation(self.h[:, k * TOK:(k + 1) * TOK], bank[:, k * TOK:(k + 1) * TOK], ACT.Identity,
                                   scale=scale(g, k), bias=shift(g, k)).then_inc(self.h_ready, 1)

        def by_mod(n):
            return lambda g, k: MOD[:, n, bass.ds(g * GB + k, 1)]

        def by_col(name):
            return lambda g, k: col(name)

        def pre(name, weights_name, scale, shift, eps, bk, bq):
            with Stage(name) as st:
                nw = 3 if bq else 2
                W = st.sb("w", [P, nw * P])
                w_in = st.sem("w_in")
                norm = Norm(st, "ln", eps)
                k_ps, q_ps, v_ps = st.sem("k_ps"), st.sem("q_ps"), st.sem("v_ps")
                qk_out, v_out = st.sem("qk_out"), st.sem("v_out")
                ps = st.ps
                nqk = nw - 1
                with st.block() as block:
                    @block.sync
                    def _(sp):
                        weights_in(sp, W, weights_name, w_in)

                    @block.vector
                    def _(dve):
                        with dve.Fori(0, NG) as g:
                            dve.wait_ge(qk_out, OPEN + g * nqk)
                            dve.sem_inc(passed, 1)
                            norm.vector(dve, g)
                            dve.wait_ge(v_ps, OPEN + g + 1)
                            dve.tensor_copy(V0[:, bass.ds(g * GB, GB), :],
                                            ps[0:TOK, 3, 0:GB * P].rearrange("p (k c) -> p k c", k=GB)).then_inc(v_out, 1)

                    @block.gpsimd
                    def _(pool):
                        norm.gpsimd_init(pool)
                        with pool.Fori(0, NG) as g:
                            norm.gpsimd(pool, g)

                    @block.tensor
                    def _(pe):
                        pe.wait_ge(w_in, OPEN + 16)
                        with pe.Fori(0, NG) as g:
                            norm.tensor(pe, g, ps[:, 0, :])
                            pe.wait_ge(norm.h_ready, OPEN + (g + 1) * GB)
                            pe.wait_ge(qk_out, OPEN + g * nqk)
                            pe.matmul(ps[:, 1, 0:GT], W[:, 0:P], norm.h[:, :], start=True, stop=True).then_inc(k_ps, 1)
                            if bq:
                                pe.matmul(ps[:, 2, 0:GT], W[:, 2 * P:3 * P], norm.h[:, :], start=True, stop=True).then_inc(q_ps, 1)
                            pe.wait_ge(v_out, OPEN + g)
                            for k in range(GB):
                                mm = pe.matmul(ps[0:TOK, 3, k * P:(k + 1) * P], norm.h[:, k * TOK:(k + 1) * TOK],
                                               W[:, P:2 * P], start=True, stop=True)
                            mm.then_inc(v_ps, 1)

                    @block.scalar
                    def _(act):
                        with act.Fori(0, NG) as g:
                            act.wait_ge(v_ps, OPEN + g)
                            norm.scalar(act, g, ps[:, 0, :], scale, shift)
                            act.wait_ge(k_ps, OPEN + g + 1)
                            act.sem_inc(passed, 1)
                            act.activation(KT[:, bass.ds(g * GT, GT)], ps[:, 1, 0:GT], ACT.Identity, bias=col(bk)).then_inc(qk_out, 1)
                            if bq:
                                act.wait_ge(q_ps, OPEN + g + 1)
                                act.sem_inc(passed, 1)
                                act.activation(QT[:, bass.ds(g * GT, GT)], ps[:, 2, 0:GT], ACT.Identity, bias=col(bq)).then_inc(qk_out, 1)

        class Residual:

            def __init__(self, st, tag, bias, gate):
                self.bias, self.gate = bias, gate
                self.y = st.sb(tag + "_y", [P, GT])
                self.y_ps = st.sem(tag + "_y_ps")
                self.y_ready = st.sem(tag + "_y_ready")
                self.yT_ready = st.sem(tag + "_yT_ready")
                self.x_ready = st.sem(tag + "_x_ready")

            def product(self, pe, g, bank, W):
                for u in range(NHALF):
                    mm = pe.matmul(bank[:, 0:GT], W[:, u * P:(u + 1) * P], AT[:, u, bass.ds(g * GT, GT)],
                                   start=(u == 0), stop=(u == NHALF - 1))
                mm.then_inc(self.y_ps, 1)

            def vector_gate(self, dve, g, bank):
                dve.wait_ge(self.y_ps, OPEN + g + 1)
                for k in range(GB):
                    s = slice(k * TOK, (k + 1) * TOK)
                    if self.gate is None:
                        ins = dve.tensor_scalar(self.y[:, s], bank[:, s], col(self.bias), None, ALU.add)
                    else:
                        ins = dve.tensor_scalar(self.y[:, s], bank[:, s], col(self.bias), self.gate(g, k), ALU.add, ALU.mult)
                    ins.then_inc(self.y_ready, 1)

            def tensor(self, pe, g, bank):
                for k in range(GB):
                    pe.wait_ge(self.y_ready, OPEN + g * GB + k + 1)
                    tr = pe.transpose(bank[0:TOK, k * P:(k + 1) * P], self.y[:, k * TOK:(k + 1) * TOK], ident)
                tr.then_inc(self.yT_ready, 1)

            def vector_add(self, dve, g, bank):
                dve.wait_ge(self.yT_ready, OPEN + g + 1)
                xs = X[:, bass.ds(g * GB, GB), :]
                dve.tensor_tensor(xs, xs, bank[0:TOK, 0:GB * P].rearrange("p (k c) -> p k c", k=GB), ALU.add).then_inc(self.x_ready, 1)
                dve.wait_ge(self.x_ready, OPEN + g + 1)
                dve.sem_inc(passed, 1)

        def mid(name, weights_name, bo, gate, scale, shift, bq):
            with Stage(name) as st:
                W = st.sb("w", [P, 3 * P])
                w_in = st.sem("w_in")
                res = Residual(st, "o", bo, gate)
                norm = Norm(st, "ln", 1e-6)
                q_ps, q_out = st.sem("q_ps"), st.sem("q_out")
                ps = st.ps
                with st.block() as block:
                    @block.sync
                    def _(sp):
                        weights_in(sp, W, weights_name, w_in)

                    @block.vector
                    def _(dve):
                        with dve.Fori(0, NG) as g:
                            res.vector_gate(dve, g, ps[:, 0, :])
                            res.vector_add(dve, g, ps[:, 1, :])
                            norm.vector(dve, g)

                    @block.gpsimd
                    def _(pool):
                        norm.gpsimd_init(pool)
                        with pool.Fori(0, NG) as g:
                            norm.gpsimd(pool, g)

                    @block.tensor
                    def _(pe):
                        pe.wait_ge(w_in, OPEN + 16)
                        with pe.Fori(0, NG) as g:
                            res.product(pe, g, ps[:, 0, :], W)
                            res.tensor(pe, g, ps[:, 1, :])
                            norm.tensor(pe, g, ps[:, 2, :])
                            pe.wait_ge(norm.h_ready, OPEN + (g + 1) * GB)
                            pe.wait_ge(q_out, OPEN + g)
                            pe.matmul(ps[:, 3, 0:GT], W[:, 2 * P:3 * P], norm.h[:, :], start=True, stop=True).then_inc(q_ps, 1)

                    @block.scalar
                    def _(act):
                        with act.Fori(0, NG) as g:
                            norm.scalar(act, g, ps[:, 2, :], scale, shift)
                            act.wait_ge(q_ps, OPEN + g + 1)
                            act.sem_inc(passed, 1)
                            act.activation(QT[:, bass.ds(g * GT, GT)], ps[:, 3, 0:GT], ACT.Identity, bias=col(bq)).then_inc(q_out, 1)

        def post(name, weights_name, bo, scale, shift, b1, b2, gate):
            with Stage(name) as st:
                W = st.sb("w", [P, 10 * P])
                hid = st.sb("hidden", [P, 4, GT])
                w_in = st.sem("w_in")
                res = Residual(st, "o", bo, None)
                norm = Norm(st, "ln", 1e-6)
                res2 = Residual(st, "mlp", b2, gate)
                hid_ps, hid_ready = st.sem("hid_ps"), st.sem("hid_ready")
                ps = st.ps
                with st.block() as block:
                    @block.sync
                    def _(sp):
                        weights_in(sp, W, weights_name, w_in)

                    @block.vector
                    def _(dve):
                        with dve.Fori(0, NG) as g:
                            res.vector_gate(dve, g, ps[:, 0, :])
                            res.vector_add(dve, g, ps[:, 1, :])
                            norm.vector(dve, g)
                            res2.vector_gate(dve, g, ps[:, 3, :])
                            res2.vector_add(dve, g, ps[:, 1, :])

                    @block.gpsimd
                    def _(pool):
                        norm.gpsimd_init(pool)
                        with pool.Fori(0, NG) as g:
                            norm.gpsimd(pool, g)

                    @block.tensor
                    def _(pe):
                        pe.wait_ge(w_in, OPEN + 16)
                        with pe.Fori(0, NG) as g:
                            pe.wait_ge(res2.x_ready, OPEN + g)
                            res.product(pe, g, ps[:, 0, :], W)
                            res.tensor(pe, g, ps[:, 1, :])
                            norm.tensor(pe, g, ps[:, 2, :])
                            pe.wait_ge(norm.h_ready, OPEN + (g + 1) * GB)
                            for n in range(4):
                                pe.matmul(ps[:, 4 + n, 0:GT], W[:, (2 + n) * P:(3 + n) * P], norm.h[:, :],
                                          start=True, stop=True).then_inc(hid_ps, 1)
                            for n in range(4):
                                pe.wait_ge(hid_ready, OPEN + g * 4 + n + 1)
                                mm = pe.matmul(ps[:, 3, 0:GT], W[:, (6 + n) * P:(7 + n) * P], hid[:, n, :],
                                               start=(n == 0), stop=(n == 3))
                            mm.then_inc(res2.y_ps, 1)
                            pe.wait_ge(res.x_ready, OPEN + g + 1)
                            res2.tensor(pe, g, ps[:, 1, :])

                    @block.scalar
                    def _(act):
                        with act.Fori(0, NG) as g:
                            norm.scalar(act, g, ps[:, 2, :], scale, shift)
                            for n in range(4):
                                act.wait_ge(hid_ps, OPEN + g * 4 + n + 1)
                                act.activation(hid[:, n, :], ps[:, 4 + n, 0:GT], ACT.Gelu_apprx_tanh,
                                               bias=col(b1, n)).then_inc(hid_ready, 1)

        def split_rest(pool, link, parts, rest):
            link(pool.tensor_copy(parts[1], rest))
            link(pool.tensor_tensor(parts[2], rest, parts[1], ALU.subtract))

        def split(pool, link, value, parts, rest):
            link(pool.tensor_copy(parts[0], value))
            link(pool.tensor_tensor(rest, value, parts[0], ALU.subtract))
            split_rest(pool, link, parts, rest)

        def slot_rows(a, j):
            at = a * SLOT + MROWS + j * DH
            return slice(at, at + DH)

        def at(count):
            return OPEN + (max(count, 0) if isinstance(count, int) else count)

        DEN_ROWS = [2 * DH + r % (2 * DH) for r in range(32)]
        NFIN = 6

        def finish(dve, link, o_read, bank, sel, den, b, bv):
            half = bank[:, 0:NHALF * 2 * TOK].rearrange("p (u a q) -> p u a q", u=NHALF, a=2)
            link(dve.tensor_scalar(sel[:, :, :], half[:, :, 0, :], mask[:, 0:1], None, ALU.mult))
            link(dve.scalar_tensor_tensor(sel[:, :, :], half[:, :, 1, :], mask[:, 1:2], sel[:, :, :], ALU.mult, ALU.add))
            dve.sem_inc(o_read, 1)
            link(dve.stream_shuffle(den[:, :, :], sel[:, :, :], DEN_ROWS))
            link(dve.reciprocal(den[:, :, :], den[:, :, :]))
            link(dve.tensor_tensor(sel[:, :, :], sel[:, :, :], den[:, :, :], ALU.mult))
            c0 = COLS[bv][0]
            link(dve.tensor_tensor(AT[:, :, bass.ds(b * TOK, TOK)], sel[:, :, :],
                                   C[:, c0:c0 + NHALF].rearrange("p (u o) -> p u o", o=1).to_broadcast([P, NHALF, TOK]), ALU.add))

        def self_attend(name, bv):
            NU = NHALF
            MAXN = 4
            NPART = 8
            with Stage(name) as st:
                ps = st.ps
                kx = st.sb("k_packed", [P, PAIRS, TOK], BF16)
                qx = st.sb("q_packed", [P, PAIRS, 2 * TOK], BF16)
                kp = [st.sb(f"k_part{i}", [P, TOK], BF16) for i in range(3)]
                qp = [st.sb(f"q_part{i}", [P, TOK], BF16) for i in range(3)]
                krest = st.sb("k_rest", [P, TOK])
                qrest = st.sb("q_rest", [P, TOK])
                v = st.sb("v_and_ones", [TOK, PAIRS, 32])
                prob = st.sb("prob", [TOK, 2, 2 * GT])
                nmax = st.sb("minus_max", [TOK, HEADS])
                nmax1 = st.sb("minus_max_part", [TOK, HEADS], BF16)
                mcols = st.sb("shift_columns", [TOK, 2, MROWS, PAIRS])
                mrows = st.sb("shift_rows", [2 * MROWS * PAIRS, TOK], BF16)
                sel = st.sb("own_head", [P, NHALF, TOK])
                den = st.sb("denominators", [P, NHALF, TOK])
                prepared = st.sem("prepared")
                parts_ready, cleared = st.sem("parts_ready"), st.sem("cleared")
                packed_in, shift_in = st.sem("packed_in"), st.sem("shift_in")
                v_ready = st.sem("v_ready")
                max_ps, max_done = st.sem("max_ps"), st.sem("max_done")
                shift_ps, shift_ready, shift_chain = st.sem("shift_ps"), st.sem("shift_ready"), st.sem("shift_chain")
                score_ps, prob_ready, pv_done = st.sem("score_ps"), st.sem("prob_ready"), st.sem("pv_done")
                fin = st.sem("fin")

                with st.block() as block:
                    @block.sync
                    def _(sp):
                        sp.wait_ge(prepared, OPEN + 3)
                        with sp.Fori(0, NB) as b:
                            sp.wait_ge(score_ps, OPEN + b * NU)
                            sp.wait_ge(parts_ready, OPEN + (b + 1) * NPART)
                            sp.sem_inc(passed, 1)
                            for a in range(2):
                                for j in range(TERMS):
                                    sp.dma_start(qx[slot_rows(a, j), :, a * TOK:(a + 1) * TOK],
                                                 qp[Q_PART[j]][a * SLOT:(a + 1) * SLOT, :]).then_inc(packed_in, 16)
                            for a in range(2):
                                for j in range(TERMS):
                                    sp.dma_start(kx[slot_rows(a, j), :, :],
                                                 kp[K_PART[j]][a * SLOT:(a + 1) * SLOT, :]).then_inc(packed_in, 16)
                            sp.wait_ge(shift_ready, OPEN + b + 1)
                            for a in range(2):
                                n = MROWS * PAIRS
                                sp.dma_start(qx[a * SLOT:a * SLOT + MROWS, :, a * TOK:(a + 1) * TOK],
                                             mrows[a * n:(a + 1) * n, :]).then_inc(shift_in, 16)

                    @block.gpsimd
                    def _(pool):
                        pool.memset(kx[:, :, :], 1.0).then_inc(prepared, 1)
                        pool.memset(qx[:, :, :], 0.0).then_inc(prepared, 1)
                        pool.memset(v[:, :, :], 1.0).then_inc(prepared, 1)
                        with pool.Fori(0, NB) as b:
                            link = Chain(pool, parts_ready, b, NPART, own=True)
                            pool.wait_ge(packed_in, OPEN + b * 2 * 2 * TERMS * 16)
                            pool.sem_inc(passed, 1)
                            split(pool, link, QT[:, bass.ds(b * TOK, TOK)], [t[:, :] for t in qp], qrest[:, :])
                            split(pool, link, KT[:, bass.ds(b * TOK, TOK)], [t[:, :] for t in kp], krest[:, :])
                            assert link.n == NPART

                    @block.tensor
                    def _(pe):
                        with pe.Fori(0, NB) as b:
                            pe.wait_ge(prob_ready, OPEN + b * NU)
                            pe.wait_ge(v_ready, OPEN + b + 1)
                            pe.wait_ge(packed_in, OPEN + (b + 1) * 2 * 2 * TERMS * 16)
                            pe.wait_ge(cleared, OPEN + (b + 1) * 2)
                            for n in range(MAXN):
                                for i in range(4):
                                    p, a = (4 * n + i) // 2, i % 2
                                    mm = pe.matmul(ps[0:TOK, n, i * TOK:(i + 1) * TOK],
                                                   qx[:, p, a * TOK:(a + 1) * TOK], kx[:, p, :],
                                                   start=True, stop=True)
                                mm.then_inc(max_ps, 1)
                            pe.wait_ge(shift_chain, OPEN + (b + 1) * 3)
                            pe.transpose(ps[0:2 * MROWS * PAIRS, 4, 0:TOK],
                                         mcols[:, :, :, :].rearrange("q a i p -> q (a i p)"), ident[0:TOK, 0:TOK]).then_inc(shift_ps, 1)
                            pe.wait_ge(shift_in, OPEN + (b + 1) * 32)
                            for n in range(NU):
                                for i in range(4):
                                    p = 4 * n + i
                                    mm = pe.matmul(ps[0:TOK, 2 * n + i // 2, (i % 2) * 2 * TOK:(i % 2 + 1) * 2 * TOK],
                                                   kx[:, p, :], qx[:, p, :], start=True, stop=True)
                                mm.then_inc(score_ps, 1)
                            pe.wait_ge(fin, OPEN + b * NFIN)
                            for n in range(NU):
                                pe.wait_ge(prob_ready, OPEN + b * NU + n + 1)
                                for j in range(COLT):
                                    mm = pe.matmul(ps[32 * j:32 * j + 32, 7, n * 2 * TOK:(n + 1) * 2 * TOK], v[:, COLT * n + j, :],
                                                   prob[:, n, j * 2 * TOK:(j + 1) * 2 * TOK],
                                                   start=True, stop=True, tile_position=(0, 32 * j))
                                mm.then_inc(pv_done, 1)

                    @block.scalar
                    def _(act):
                        act.wait_ge(prepared, OPEN + 3)
                        with act.Fori(0, NB) as b:
                            act.wait_ge(pv_done, OPEN + b * NU)
                            act.sem_inc(passed, 1)
                            act.activation(v[:, :, 0:2 * DH], V0[:, bass.ds(b, 1), :].rearrange("p o (i c) -> p (o i) c", i=PAIRS),
                                           ACT.Copy).then_inc(v_ready, 1)
                            for n in range(NU):
                                act.wait_ge(score_ps, OPEN + b * NU + n + 1)
                                act.activation(prob[:, n, :].rearrange("p (i c) -> p i c", i=2),
                                               ps[0:TOK, 2 * n:2 * n + 2, 0:GT], ACT.Exp, scale=ISQ).then_inc(prob_ready, 1)

                    @block.vector
                    def _(dve):
                        dve.wait_ge(prepared, OPEN + 3)
                        with dve.Fori(0, NB) as b:
                            dve.wait_ge(score_ps, OPEN + b * NU)
                            for a in range(2):
                                dve.memset(qx[a * SLOT:a * SLOT + MROWS, :, a * TOK:(a + 1) * TOK], 0.0).then_inc(cleared, 1)
                            for n in range(MAXN):
                                dve.wait_ge(max_ps, OPEN + b * MAXN + n + 1)
                                dve.tensor_reduce(nmax[:, 4 * n:4 * n + 4], ps[0:TOK, n, 0:GT].rearrange("p (h k) -> p h k", h=4),
                                                  AX.X, ALU.max, negate=True).then_inc(max_done, 1)
                            link = Chain(dve, shift_chain, b, 3)
                            dve.wait_ge(max_done, OPEN + (b + 1) * MAXN)
                            shift_columns(dve, link, nmax, nmax1, mcols)
                            dve.wait_ge(shift_ps, OPEN + b + 1)
                            dve.wait_ge(shift_in, OPEN + b * 32)
                            dve.tensor_copy(mrows[:, :], ps[0:2 * MROWS * PAIRS, 4, 0:TOK]).then_inc(shift_ready, 1)
                            dve.wait_ge(pv_done, OPEN + (b + 1) * NU)
                            flink = Chain(dve, fin, b, NFIN)
                            finish(dve, flink, passed, ps[:, 7, :], sel, den, b, bv)
                            assert flink.n == NFIN

        def shift_columns(dve, link, nmax, nmax1, mcols):
            link(dve.tensor_copy(nmax1[:, :], nmax[:, :]))
            hv = nmax1[:, :].rearrange("q (p a) -> q a p", a=2)
            link(dve.tensor_copy(mcols[:, :, 0, :], hv))
            link(dve.tensor_tensor(mcols[:, :, 1, :], nmax[:, :].rearrange("q (p a) -> q a p", a=2), hv, ALU.subtract))

        def cross_attend(name, kv, bk, bv, loads_before, normed=False, eps=1e-6, modulated=False):
            spans = [(c * KC, KC if c < CHUNKS - 1 else KLAST) for c in range(CHUNKS)]
            NU = NHALF * CHUNKS
            blocks = [(t * BLK, min(BLK, CTX - t * BLK)) for t in range(3)]
            MAXK = CTX // 3 + 1
            MAXN = 3 * HEADS
            NQPART, NKPART = 4, 6
            NSHIFT = 4
            NV = 4
            NCTX = 32 if normed else 16
            NPACK = 2 * 2 * TERMS * 16
            WORK = 4
            MAXB = 5
            AHEAD = 4
            STATS_AT, X_AT, V_AT = 0, 4, 0
            T_AT = X_AT + 1
            K_AT = T_AT + 3 if normed else V_AT + 3
            CLEAR_AT = 1

            def maxima_of(u):
                upto = [0] + [min(AHEAD + 2 * x, MAXN) for x in range(NU + 1)]
                return range(upto[u + 1], upto[u + 2])

            with Stage(name) as st:
                ps = st.ps
                kx = [st.sb(f"k_packed{s}", [P, PAIRS, CTX], BF16) for s in range(3)]
                qx = [st.sb(f"q_packed{s}", [P, PAIRS, 2 * TOK], BF16) for s in range(3)]
                kp = [st.sb(f"k_part{i}", [P, CTX], BF16) for i in range(3)]
                qp = [st.sb(f"q_part{i}", [P, TOK], BF16) for i in range(3)]
                v = [st.sb(f"v_and_ones{s}", [KC, CHUNKS, PAIRS, 32]) for s in range(2)]
                krest = st.sb("k_rest", [P, CTX])
                qrest = st.sb("q_rest", [P, TOK])
                prob = st.sb("prob", [KC, 3, 2 * GT])
                zeros = st.sb("zeros", [P, PAIRS, TOK], BF16)
                bmax = st.sb("block_max", [TOK, MAXN])
                nmax = st.sb("minus_max", [TOK, HEADS])
                nmax1 = st.sb("minus_max_part", [TOK, HEADS], BF16)
                mcols = st.sb("shift_columns", [TOK, 2, MROWS, PAIRS])
                mrows = st.sb("shift_rows", [2 * MROWS * PAIRS, TOK], BF16)
                sel = st.sb("own_head", [P, NHALF, TOK])
                den = st.sb("denominators", [P, NHALF, TOK])
                W = st.sb("w", [P, 2 * P])
                xt_one = [st.sb(f"ctx_channels{s}", [P, CTX]) for s in range(1 if normed else 2)]
                xt = xt_one if not normed else xt_one * 2
                prepared, w_in = st.sem("prepared"), st.sem("w_in")
                k_ps, v_ps = st.sem("k_ps"), st.sem("v_ps")
                k1_ready, rest_ready = st.sem("k1_ready"), st.sem("rest_ready")
                qparts_ready, kparts_ready, cleared = st.sem("qparts_ready"), st.sem("kparts_ready"), st.sem("cleared")
                packed_in, shift_in = st.sem("packed_in"), st.sem("shift_in")
                v_ready = st.sem("v_ready")
                max_ps, max_done = st.sem("max_ps"), st.sem("max_done")
                shift_ps, shift_ready, shift_chain = st.sem("shift_ps"), st.sem("shift_ready"), st.sem("shift_chain")
                score_ps, prob_ready, pv_done = st.sem("score_ps"), st.sem("prob_ready"), st.sem("pv_done")
                fin, sums_read = st.sem("fin"), st.sem("sums_read")
                if normed:
                    xn = st.sb("ctx_tokens", [KC, CHUNKS, P])
                    stats = st.sb("stats", [KC, CHUNKS, 6])
                    mv = st.sb("mean_var", [KC, CHUNKS, 2])
                    ve = st.sb("var_eps", [KC, CHUNKS])
                    half = st.sb("minus_half", [KC, CHUNKS])
                    rstd = st.sb("rstd", [KC, CHUNKS])
                    mv_zero = st.sem("mv_zero")
                    stats_done, var_ready, rstd_ready = st.sem("stats_done"), st.sem("var_ready"), st.sem("rstd_ready")
                    xn_ready, xnT_ps, xt_ready = st.sem("xn_ready"), st.sem("xnT_ps"), st.sem("xt_ready")

                def periods(eng, body):
                    body(-2, -2, False, False, True)
                    body(-1, -1, False, True, True)
                    with eng.Fori(0, (NB - 2) // 6) as i:
                        for r in range(6):
                            body(6 * i + r, r, True, True, True)
                    body(NB - 2, 0, True, True, False)
                    body(NB - 1, 1, True, False, False)

                with st.block() as block:
                    @block.sync
                    def _(sp):
                        weights_in(sp, W, kv, w_in)
                        sp.wait_ge(prepared, OPEN + 9)

                        def period(b, r, now, nxt, prep):
                            n, p = b + 1, b + 2
                            if prep:
                                sp.wait_ge(score_ps, at(b * NU))
                                sp.wait_ge(qparts_ready, at((p + 1) * NQPART))
                                sp.sem_inc(passed, 1)
                                for a in range(2):
                                    for j in range(TERMS):
                                        sp.dma_start(qx[(r + 2) % 3][slot_rows(a, j), :, a * TOK:(a + 1) * TOK],
                                                     qp[Q_PART[j]][a * SLOT:(a + 1) * SLOT, :]).then_inc(packed_in, 16)
                                sp.wait_ge(k1_ready, at((p + 1) * 3))
                                sp.wait_ge(kparts_ready, at((p + 1) * NKPART))
                                sp.sem_inc(passed, 1)
                                for a in range(2):
                                    for j in range(TERMS):
                                        sp.dma_start(kx[(r + 2) % 3][slot_rows(a, j), :, :],
                                                     kp[K_PART[j]][a * SLOT:(a + 1) * SLOT, :]).then_inc(packed_in, 16)
                            if nxt:
                                sp.wait_ge(shift_ready, at(n + 1))
                                for a in range(2):
                                    m = MROWS * PAIRS
                                    sp.dma_start(qx[(r + 1) % 3][a * SLOT:a * SLOT + MROWS, :, a * TOK:(a + 1) * TOK],
                                                 mrows[a * m:(a + 1) * m, :]).then_inc(shift_in, 16)

                        periods(sp, period)

                    @block.gpsimd
                    def _(pool):
                        for s in range(3):
                            pool.memset(qx[s][:, :, :], 0.0).then_inc(prepared, 1)
                        pool.memset(zeros[:, :, :], 0.0).then_inc(prepared, 1)
                        for s in range(2):
                            pool.memset(v[s][:, :, :, :], 1.0).then_inc(prepared, 1)
                        pool.memset(kx[2][:, :, :], 1.0).then_inc(prepared, 1)
                        if normed:
                            pool.memset(half[:, :], -0.5).then_inc(var_ready, 1)

                        def period(b, r, now, nxt, prep):
                            if not prep:
                                return
                            p, s = b + 2, r % 2
                            if normed:
                                pool.wait_ge(xnT_ps, at(p * 3))
                                pool.sem_inc(passed, 1)
                                pool.dma_start(xn[:, 0:CHUNKS - 1, :],
                                               ctx_n[p, 0:(CHUNKS - 1) * KC, :].rearrange("(c p) d -> p c d", p=KC)).then_inc(ctx_in, 16)
                                pool.dma_start(xn[0:KLAST, CHUNKS - 1, :], ctx_n[p, (CHUNKS - 1) * KC:CTX, :]).then_inc(ctx_in, 16)
                            else:
                                pool.wait_ge(v_ps, at((p - 1) * 3))
                                pool.sem_inc(passed, 1)
                                pool.dma_start(xt[s][:, :], ctx_t[p]).then_inc(ctx_in, 16)
                            pool.wait_ge(packed_in, at(p * NPACK))
                            pool.sem_inc(passed, 1)
                            qlink = Chain(pool, qparts_ready, p, NQPART, own=True)
                            split(pool, qlink, QT[:, bass.ds(p * TOK, TOK)], [t[:, :] for t in qp], qrest[:, :])
                            assert qlink.n == NQPART
                            if normed:
                                pool.wait_ge(var_ready, at(p + 2))
                                pool.tensor_tensor(rstd[:, :], ve[:, :], half[:, :], ALU.pow).then_inc(rstd_ready, 1)
                            klink = Chain(pool, kparts_ready, p, NKPART, own=True)
                            for t, (k0, kn) in enumerate(blocks):
                                pool.wait_ge(rest_ready, at(p * 3 + t + 1))
                                pool.sem_inc(passed, 1)
                                split_rest(pool, klink, [part[:, k0:k0 + kn] for part in kp], krest[:, k0:k0 + kn])
                            assert klink.n == NKPART

                        periods(pool, period)

                    @block.tensor
                    def _(pe):
                        pe.wait_ge(w_in, OPEN + 16)

                        def period(b, r, now, nxt, prep):
                            n, p = b + 1, b + 2
                            s, o, now_x, next_x = r % 2, 1 - r % 2, r % 3, (r + 1) % 3

                            def scores(u):
                                c, half_ = u // 2, u % 2
                                pe.wait_ge(prob_ready, at(b * NU + max(u - 1, 0)))
                                k0, kn = spans[c]
                                for i in range(4):
                                    pr = 4 * half_ + i
                                    mm = pe.matmul(ps[0:kn, 2 * (u % 2) + i // 2, (i % 2) * 2 * TOK:(i % 2 + 1) * 2 * TOK],
                                                   kx[now_x][:, pr, k0:k0 + kn], qx[now_x][:, pr, :], start=True, stop=True)
                                mm.then_inc(score_ps, 1)

                            def values(u):
                                c, half_ = u // 2, u % 2
                                if u == 0:
                                    pe.wait_ge(sums_read, at(b))
                                pe.wait_ge(prob_ready, at(b * NU + u + 1))
                                kn = spans[c][1]
                                for j in range(COLT):
                                    mm = pe.matmul(ps[32 * j:32 * j + 32, 7, half_ * 2 * TOK:(half_ + 1) * 2 * TOK],
                                                   v[s][0:kn, c, COLT * half_ + j, :], prob[0:kn, u % 3, j * 2 * TOK:(j + 1) * 2 * TOK],
                                                   start=(u == 0), stop=(u == NU - 1), tile_position=(0, 32 * j))
                                mm.then_inc(pv_done, 1)

                            def project_v(t):
                                pe.wait_ge(shift_ready, at(n))
                                pe.wait_ge(k1_ready, at((n + 1) * 3))
                                pe.wait_ge(rest_ready, at((n + 1) * 3))
                                pe.wait_ge(v_ready, at(n * NV + t))
                                if not normed:
                                    pe.wait_ge(ctx_in, loads_before + (n + 1) * NCTX)
                                else:
                                    pe.wait_ge(xt_ready, at((n + 1) * 3))
                                for c in range(4 * t, 4 * t + 4):
                                    k0, kn = spans[c]
                                    mm = pe.matmul(ps[0:kn, WORK, (c % 4) * P:(c % 4 + 1) * P], xt[o][:, k0:k0 + kn],
                                                   W[:, P:2 * P], start=True, stop=True)
                                mm.then_inc(v_ps, 1)

                            def turn(t):
                                pe.wait_ge(v_ready, at((n + 1) * NV))
                                pe.wait_ge(xt_ready, at(p * 3 + t))
                                pe.wait_ge(xn_ready, at(p * CHUNKS + 4 * t + 4))
                                for c in range(4 * t, 4 * t + 4):
                                    kn = spans[c][1]
                                    tr = pe.transpose(ps[:, WORK, (c % 4) * KC:(c % 4) * KC + kn],
                                                      xn[0:kn, c, :], ident[0:kn, 0:kn])
                                tr.then_inc(xnT_ps, 1)

                            def project_k(t):
                                if normed:
                                    pe.wait_ge(xt_ready, at((p + 1) * 3))
                                else:
                                    pe.wait_ge(ctx_in, loads_before + (p + 1) * NCTX)
                                    pe.wait_ge(v_ready, at((n + 1) * NV))
                                pe.wait_ge(k1_ready, at(p * 3 + t))
                                pe.wait_ge(rest_ready, at(p * 3 + t))
                                k0, kn = blocks[t]
                                pe.matmul(ps[:, WORK, 0:kn], W[:, 0:P], xt[s][:, k0:k0 + kn],
                                          start=True, stop=True).then_inc(k_ps, 1)

                            def maximum(m):
                                h, t = m // 3, m % 3
                                if m == 0:
                                    pe.wait_ge(packed_in, at((n + 1) * NPACK))
                                    pe.wait_ge(cleared, at((n + 1) * 2))
                                pe.wait_ge(max_done, at(n * MAXN + max(m - 1, 0)))
                                pr, a, k0 = h // 2, h % 2, t * (CTX // 3)
                                pe.matmul(ps[0:TOK, MAXB + m % 2, 0:MAXK], qx[next_x][:, pr, a * TOK:(a + 1) * TOK],
                                          kx[next_x][:, pr, k0:k0 + MAXK], start=True, stop=True).then_inc(max_ps, 1)

                            def turn_shift():
                                pe.wait_ge(shift_chain, at((n + 1) * NSHIFT))
                                pe.wait_ge(v_ready, at((n + 1) * NV))
                                if prep:
                                    pe.wait_ge(k1_ready, at((p + 1) * 3))
                                    pe.wait_ge(rest_ready, at((p + 1) * 3))
                                pe.transpose(ps[0:2 * MROWS * PAIRS, WORK, 0:TOK],
                                             mcols[:, :, :, :].rearrange("q a i p -> q (a i p)"), ident[0:TOK, 0:TOK]).then_inc(shift_ps, 1)

                            if nxt:
                                for m in maxima_of(-1):
                                    maximum(m)
                            if now:
                                pe.wait_ge(shift_in, at(n * 32))
                            for u in range(NU):
                                ms = maxima_of(u) if nxt else ()
                                if now:
                                    scores(u)
                                for m in ms[:1]:
                                    maximum(m)
                                if now and u >= 1:
                                    values(u - 1)
                                for m in ms[1:]:
                                    maximum(m)
                                if nxt and V_AT <= u < V_AT + 3:
                                    project_v(u - V_AT)
                                if prep and normed and T_AT <= u < T_AT + 3:
                                    turn(u - T_AT)
                                if prep and K_AT <= u < K_AT + 3:
                                    project_k(u - K_AT)
                            if nxt:
                                turn_shift()
                            if now:
                                values(NU - 1)

                        periods(pe, period)

                    @block.scalar
                    def _(act):
                        act.wait_ge(prepared, OPEN + 9)

                        def period(b, r, now, nxt, prep):
                            n, p = b + 1, b + 2
                            s, o, now_x, next_x = r % 2, 1 - r % 2, r % 3, (r + 1) % 3
                            for u in range(NU):
                                if now:
                                    kn = spans[u // 2][1]
                                    act.wait_ge(score_ps, at(b * NU + u + 1))
                                    act.wait_ge(pv_done, at(b * NU + max(u - 2, 0)))
                                    act.activation(prob[0:kn, u % 3, :].rearrange("p (i c) -> p i c", i=2),
                                                   ps[0:kn, 2 * (u % 2):2 * (u % 2) + 2, 0:GT], ACT.Exp, scale=ISQ).then_inc(prob_ready, 1)
                                if nxt and V_AT <= u < V_AT + 3:
                                    t = u - V_AT
                                    act.wait_ge(pv_done, at(b * NU))
                                    for c0, m, kn in [((0, 4, KC),), ((4, 4, KC),), ((8, 3, KC), (11, 1, KLAST))][t]:
                                        act.wait_ge(v_ps, at(n * 3 + t + 1))
                                        act.activation(v[o][0:kn, c0:c0 + m, :, 0:2 * DH],
                                                       ps[0:kn, WORK, (c0 % 4) * P:(c0 % 4 + m) * P].rearrange(
                                                           "p (c i d) -> p c i d", c=m, i=PAIRS), ACT.Copy).then_inc(v_ready, 1)
                                if prep and u == CLEAR_AT:
                                    act.wait_ge(score_ps, at(b * NU))
                                    for a in range(2):
                                        rows_ = slice(a * SLOT, a * SLOT + MROWS)
                                        act.activation(qx[(r + 2) % 3][rows_, :, a * TOK:(a + 1) * TOK], zeros[rows_, :, :], ACT.Copy).then_inc(cleared, 1)
                                if prep and normed and T_AT <= u < T_AT + 3:
                                    t = u - T_AT
                                    k0, kn = blocks[t]
                                    act.wait_ge(v_ps, at((n + 1) * 3))
                                    act.wait_ge(xnT_ps, at(p * 3 + t + 1))
                                    act.sem_inc(passed, 1)
                                    if modulated:
                                        act.activation(xt[s][:, k0:k0 + kn], ps[:, WORK, 0:kn], ACT.Identity,
                                                       scale=MOD[:, 14, bass.ds(p, 1)], bias=MOD[:, 15, bass.ds(p, 1)]).then_inc(xt_ready, 1)
                                    else:
                                        act.activation(xt[s][:, k0:k0 + kn], ps[:, WORK, 0:kn], ACT.Copy).then_inc(xt_ready, 1)
                                if prep and K_AT <= u < K_AT + 3:
                                    t = u - K_AT
                                    k0, kn = blocks[t]
                                    act.wait_ge(packed_in, at(p * NPACK))
                                    act.wait_ge(k_ps, at(p * 3 + t + 1))
                                    act.activation(kp[0][:, k0:k0 + kn], ps[:, WORK, 0:kn], ACT.Identity,
                                                   bias=col(bk)).then_inc(k1_ready, 1)

                        periods(act, period)

                    @block.vector
                    def _(dve):
                        if normed:
                            dve.memset(mv[:, :, :], 0.0).then_inc(mv_zero, 1)
                            dve.wait_ge(mv_zero, OPEN + 1)
                        for s in range(2):
                            dve.memset(kx[s][:, :, :], 1.0).then_inc(prepared, 1)

                        def period(b, r, now, nxt, prep):
                            n, p = b + 1, b + 2
                            for u in range(-1, NU):
                                for m in maxima_of(u) if nxt else ():
                                    dve.wait_ge(max_ps, at(n * MAXN + m + 1))
                                    dve.tensor_reduce(bmax[:, m:m + 1], ps[0:TOK, MAXB + m % 2, 0:MAXK], AX.X, ALU.max).then_inc(max_done, 1)
                                if prep and normed and STATS_AT <= u < STATS_AT + 3:
                                    t = u - STATS_AT
                                    dve.wait_ge(ctx_in, loads_before + (p + 1) * NCTX)
                                    for c in range(4 * t, 4 * t + 4):
                                        kn = spans[c][1]
                                        dve.bn_stats(stats[0:kn, c, :], xn[0:kn, c, :]).then_inc(stats_done, 1)
                                    for c in range(4 * t, 4 * t + 4):
                                        kn = spans[c][1]
                                        dve.wait_ge(stats_done, at(p * 2 * CHUNKS + 8 * t + 4))
                                        dve.sem_inc(passed, 1)
                                        dve.bn_aggr(mv[0:kn, c, :], stats[0:kn, c, :]).then_inc(stats_done, 1)
                                    if t == 2:
                                        dve.wait_ge(stats_done, at((p + 1) * 2 * CHUNKS))
                                        dve.tensor_scalar(ve[:, :], mv[:, :, 1], eps, None, ALU.add).then_inc(var_ready, 1)
                                if prep and normed and X_AT <= u < X_AT + 3:
                                    dve.wait_ge(rstd_ready, at(p + 1))
                                    for c in range(4 * (u - X_AT), 4 * (u - X_AT) + 4):
                                        kn = spans[c][1]
                                        dve.tensor_scalar(xn[0:kn, c, :], xn[0:kn, c, :], mv[0:kn, c, 0:1], rstd[0:kn, c:c + 1],
                                                          ALU.subtract, ALU.mult).then_inc(xn_ready, 1)
                                if prep and K_AT + 1 <= u < K_AT + 4:
                                    t = u - K_AT - 1
                                    k0, kn = blocks[t]
                                    dve.wait_ge(k1_ready, at(p * 3 + t + 1))
                                    dve.wait_ge(kparts_ready, at(p * NKPART))
                                    dve.scalar_tensor_tensor(krest[:, k0:k0 + kn], ps[:, WORK, 0:kn], col(bk), kp[0][:, k0:k0 + kn],
                                                             ALU.add, ALU.subtract).then_inc(rest_ready, 1)
                            if nxt:
                                link = Chain(dve, shift_chain, n, NSHIFT)
                                dve.wait_ge(max_done, at((n + 1) * MAXN))
                                link(dve.tensor_reduce(nmax[:, :], bmax[:, :].rearrange("q (h t) -> q h t", t=3), AX.X, ALU.max, negate=True))
                                shift_columns(dve, link, nmax, nmax1, mcols)
                                assert link.n == NSHIFT
                                dve.wait_ge(shift_ps, at(n + 1))
                                dve.wait_ge(shift_in, at(n * 32))
                                dve.tensor_copy(mrows[:, :], ps[0:2 * MROWS * PAIRS, WORK, 0:TOK]).then_inc(shift_ready, 1)
                            if now:
                                dve.wait_ge(pv_done, at(n * NU))
                                flink = Chain(dve, fin, b, NFIN)
                                finish(dve, flink, sums_read, ps[:, 7, :], sel, den, b, bv)
                                assert flink.n == NFIN

                        periods(dve, period)

        def pre2():
            with Stage("pre2") as st:
                W = st.sb("w", [P, 2 * P])
                w_in = st.sem("w_in")
                norm = Norm(st, "ln", 1e-5)
                q = st.sb("q", [P, GT])
                q_ps, q_ready, qk_ps, qk_out = st.sem("q_ps"), st.sem("q_ready"), st.sem("qk_ps"), st.sem("qk_out")
                ps = st.ps
                with st.block() as block:
                    @block.sync
                    def _(sp):
                        weights_in(sp, W, "pre2", w_in)

                    @block.vector
                    def _(dve):
                        with dve.Fori(0, NG) as g:
                            norm.vector(dve, g)
                            dve.wait_ge(norm.h_ready, OPEN + (g + 1) * GB)
                            dve.tensor_copy(KT[:, bass.ds(g * GT, GT)], norm.h[:, :]).then_inc(qk_out, 1)
                            dve.wait_ge(qk_ps, OPEN + g + 1)
                            dve.tensor_copy(QT[:, bass.ds(g * GT, GT)], ps[:, 2, 0:GT]).then_inc(qk_out, 1)

                    @block.gpsimd
                    def _(pool):
                        norm.gpsimd_init(pool)
                        with pool.Fori(0, NG) as g:
                            norm.gpsimd(pool, g)

                    @block.tensor
                    def _(pe):
                        pe.wait_ge(w_in, OPEN + 16)
                        with pe.Fori(0, NG) as g:
                            norm.tensor(pe, g, ps[:, 0, :])
                            pe.wait_ge(norm.h_ready, OPEN + (g + 1) * GB)
                            pe.matmul(ps[:, 1, 0:GT], W[:, 0:P], norm.h[:, :], start=True, stop=True).then_inc(q_ps, 1)
                            pe.wait_ge(q_ready, OPEN + g + 1)
                            pe.matmul(ps[:, 2, 0:GT], W[:, P:2 * P], q[:, :], start=True, stop=True).then_inc(qk_ps, 1)

                    @block.scalar
                    def _(act):
                        with act.Fori(0, NG) as g:
                            act.wait_ge(qk_out, OPEN + g * 2)
                            norm.scalar(act, g, ps[:, 0, :], by_col("ng2"), by_col("nb2"))
                            act.wait_ge(q_ps, OPEN + g + 1)
                            act.sem_inc(passed, 1)
                            act.activation(q[:, :], ps[:, 1, 0:GT], ACT.Copy).then_inc(q_ready, 1)

        def attend2():
            scale = float(P) ** -0.5
            with Stage("attend2") as st:
                ps = st.ps
                q = st.sb("q", [P, TOK])
                xt = st.sb("ctx_channels", [P, CTX])
                xn = st.sb("ctx_tokens", [KC, CHUNKS, P])
                prob = st.sb("prob", [TOK, CTX])
                probn = st.sb("prob_normal", [TOK, CTX])
                probT = st.sb("prob_turned", [KC, CHUNKS, TOK])
                mx = st.sb("minus_max", [TOK, 3])
                nm = st.sb("shift", [TOK, 1])
                den = st.sb("den", [TOK, 3])
                den1 = st.sb("den_sum", [TOK, 1])
                rden = st.sb("den_reciprocal", [TOK, 1])
                xt_in, xn_in = st.sem("xt_in"), st.sem("xn_in")
                q_ready, score_ps, chain = st.sem("q_ready"), st.sem("score_ps"), st.sem("chain")
                prob_ready, norm_ready, norm_chain = st.sem("prob_ready"), st.sem("norm_ready"), st.sem("norm_chain")
                turned_ps, turned_ready, o_ps, o_out = st.sem("turned_ps"), st.sem("turned_ready"), st.sem("o_ps"), st.sem("o_out")
                spans = [(t * BLK, min(BLK, CTX - t * BLK)) for t in range(3)]
                rows_of = [KC if c < CHUNKS - 1 else KLAST for c in range(CHUNKS)]
                with st.block() as block:
                    @block.sync
                    def _(sp):
                        with sp.Fori(0, NB) as b:
                            sp.wait_ge(score_ps, OPEN + b * 3)
                            sp.sem_inc(passed, 1)
                            sp.dma_start(xt[:, :], ctx_t[b]).then_inc(xt_in, 16)
                            sp.wait_ge(o_ps, OPEN + b)
                            sp.sem_inc(passed, 1)
                            sp.dma_start(xn[:, 0:CHUNKS - 1, :],
                                         ctx_n[b, 0:(CHUNKS - 1) * KC, :].rearrange("(c p) d -> p c d", p=KC)).then_inc(xn_in, 16)
                            sp.dma_start(xn[0:KLAST, CHUNKS - 1, :], ctx_n[b, (CHUNKS - 1) * KC:CTX, :]).then_inc(xn_in, 16)

                    @block.tensor
                    def _(pe):
                        with pe.Fori(0, NB) as b:
                            pe.wait_ge(xt_in, OPEN + (b + 1) * 16)
                            pe.wait_ge(q_ready, OPEN + b + 1)
                            pe.wait_ge(prob_ready, OPEN + b * 3)
                            for t, (k0, n) in enumerate(spans):
                                pe.matmul(ps[0:TOK, t, 0:n], q[:, :], xt[:, k0:k0 + n], start=True, stop=True).then_inc(score_ps, 1)
                            pe.wait_ge(turned_ready, OPEN + b * 4)
                            for t in range(3):
                                pe.wait_ge(norm_ready, OPEN + b * 3 + t + 1)
                                for c in range(4 * t, 4 * t + 4):
                                    tr = pe.transpose(ps[0:rows_of[c], 3 + t, (c % 4) * TOK:(c % 4 + 1) * TOK],
                                                      probn[:, c * KC:c * KC + rows_of[c]], ident[0:TOK, 0:TOK])
                                tr.then_inc(turned_ps, 1)
                            pe.wait_ge(xn_in, OPEN + (b + 1) * 32)
                            pe.wait_ge(o_out, OPEN + b)
                            for c in range(CHUNKS):
                                if c % 4 == 0:
                                    pe.wait_ge(turned_ready, OPEN + (b * 4 + (c // 4 + 1 if c < 8 else 4)))
                                mm = pe.matmul(ps[:, 6, 0:TOK], xn[0:rows_of[c], c, :], probT[0:rows_of[c], c, :],
                                               start=(c == 0), stop=(c == CHUNKS - 1))
                            mm.then_inc(o_ps, 1)

                    @block.scalar
                    def _(act):
                        with act.Fori(0, NB) as b:
                            act.wait_ge(score_ps, OPEN + b * 3)
                            act.sem_inc(passed, 1)
                            act.activation(q[:, :], QT[:, bass.ds(b * TOK, TOK)], ACT.Copy).then_inc(q_ready, 1)
                            act.wait_ge(chain, OPEN + (b + 1) * 5)
                            for t, (k0, n) in enumerate(spans):
                                act.activation(prob[:, k0:k0 + n], ps[0:TOK, t, 0:n], ACT.Exp, scale=scale,
                                               bias=nm[:, 0:1], accum_out=den[:, t:t + 1]).then_inc(prob_ready, 1)
                            act.wait_ge(o_ps, OPEN + b)
                            for t in range(3):
                                act.wait_ge(turned_ps, OPEN + b * 3 + t + 1)
                                m = 4 if t < 2 else 3
                                act.activation(probT[:, 4 * t:4 * t + m, :],
                                               ps[0:KC, 3 + t, 0:m * TOK].rearrange("p (c q) -> p c q", c=m), ACT.Copy).then_inc(turned_ready, 1)
                            act.activation(probT[0:KLAST, CHUNKS - 1, :], ps[0:KLAST, 5, 3 * TOK:4 * TOK], ACT.Copy).then_inc(turned_ready, 1)

                    @block.vector
                    def _(dve):
                        with dve.Fori(0, NB) as b:
                            link = Chain(dve, chain, b, 5)
                            for t, (k0, n) in enumerate(spans[:2]):
                                dve.wait_ge(score_ps, OPEN + b * 3 + t + 1)
                                link(dve.tensor_reduce(mx[:, t:t + 1], ps[0:TOK, t, 0:n], AX.X, ALU.max))
                            dve.wait_ge(score_ps, OPEN + b * 3 + 3)
                            link(dve.tensor_reduce(mx[:, 2:3], ps[0:TOK, 2, 0:spans[2][1]], AX.X, ALU.max))
                            link(dve.tensor_reduce(nm[:, 0:1], mx[:, :], AX.X, ALU.max, negate=True))
                            link(dve.tensor_scalar(nm[:, 0:1], nm[:, 0:1], scale, None, ALU.mult))
                            dve.wait_ge(prob_ready, OPEN + b * 3 + 3)
                            dlink = Chain(dve, norm_chain, b, 2)
                            dlink(dve.tensor_reduce(den1[:, 0:1], den[:, :], AX.X, ALU.add))
                            dlink(dve.reciprocal(rden[:, 0:1], den1[:, 0:1]))
                            for t, (k0, n) in enumerate(spans):
                                dve.tensor_scalar(probn[:, k0:k0 + n], prob[:, k0:k0 + n], rden[:, 0:1], None, ALU.mult).then_inc(norm_ready, 1)
                            dve.wait_ge(o_ps, OPEN + b + 1)
                            dve.tensor_copy(AT[:, 0, bass.ds(b * TOK, TOK)], ps[:, 6, 0:TOK]).then_inc(o_out, 1)

        def experts():
            a, n = 0, {}
            for key, width in [("wv", P), ("router", 9), ("w1", 18 * P), ("gw1", 3 * P), ("w2", 6 * P), ("gw2", P), ("out", P)]:
                n[key] = a
                a += width
            with Stage("experts") as st:
                ps = st.ps
                W = st.sb("w", [P, a])
                R = st.sb("rows", [TOK, ROWS.width])
                comb = st.sb("combined", [P, 3, GT])
                hid = st.sb("hidden", [P, 7, GT])
                probs = st.sb("probs", [TOK, GB, 3])
                logit = st.sb("logits", [TOK, GB, 3])
                lmax = st.sb("logit_max", [TOK, GB])
                lsum = st.sb("logit_sum", [TOK, GB])
                lrec = st.sb("logit_rec", [TOK, GB])
                eo = st.sb("expert_out", [TOK, GB, 3 * P])
                routed = st.sb("routed", [TOK, GB, P])
                gp = st.sb("gate_pre", [TOK, GB, P])
                gt = st.sb("gate_tanh", [TOK, GB, P])
                gate = st.sb("gate", [TOK, GB, P])
                rT = st.sb("routed_turned", [P, GT])
                dx = st.sb("delta", [TOK, GB, P])
                w_in = st.sem("w_in")
                ev_ps, comb_ready = st.sem("ev_ps"), st.sem("comb_ready")
                logit_ps, lchain, exp_ready = st.sem("logit_ps"), st.sem("logit_chain"), st.sem("exp_ready")
                hid_ps, hid_ready = st.sem("hid_ps"), st.sem("hid_ready")
                eo_ps, eo_out = st.sem("eo_ps"), st.sem("eo_out")
                gp_ready, tanh_ready, rchain = st.sem("gp_ready"), st.sem("tanh_ready"), st.sem("routed_chain")
                rT_ps, rT_ready, out_ps, out_chain = st.sem("rT_ps"), st.sem("rT_ready"), st.sem("out_ps"), st.sem("out_chain")

                def row(name, shape):
                    r0, r1 = ROWS[name]
                    return R[:, r0:r1].rearrange("p (o c) -> p o c", o=1).to_broadcast(shape)

                with st.block() as block:
                    @block.sync
                    def _(sp):
                        weights_in(sp, W, "moe", w_in)
                        sp.dma_start(R[:, :], rows.to_broadcast([TOK, ROWS.width])).then_inc(w_in, 16)

                    @block.vector
                    def _(dve):
                        dve.wait_ge(w_in, OPEN + 32)
                        with dve.Fori(0, NG) as g:
                            dve.tensor_copy(comb[:, 0, :], KT[:, bass.ds(g * GT, GT)]).then_inc(comb_ready, 1)
                            dve.tensor_copy(comb[:, 2, :].rearrange("p (k t) -> p k t", k=GB),
                                            COND[:, bass.ds(g * GB, GB)].rearrange("p (k o) -> p k o", o=1).to_broadcast([P, GB, TOK])).then_inc(comb_ready, 1)
                            dve.wait_ge(ev_ps, OPEN + g + 1)
                            dve.tensor_copy(comb[:, 1, :], ps[:, 0, 0:GT]).then_inc(comb_ready, 1)
                            link = Chain(dve, lchain, g, 3)
                            dve.wait_ge(logit_ps, OPEN + g + 1)
                            link(dve.tensor_tensor(logit[:, :, :], ps[0:TOK, 1, 0:GB * 3].rearrange("p (k e) -> p k e", k=GB),
                                                   row("router", [TOK, GB, 3]), ALU.add))
                            link(dve.tensor_reduce(lmax[:, :], logit[:, :, :], AX.X, ALU.max))
                            link(dve.tensor_tensor(logit[:, :, :], logit[:, :, :],
                                                   lmax[:, :].rearrange("p (k o) -> p k o", o=1).to_broadcast([TOK, GB, 3]), ALU.subtract))
                            dve.wait_ge(exp_ready, OPEN + g + 1)
                            link = Chain(dve, rchain, g, 3 + 3 * GB)
                            link(dve.tensor_reduce(lsum[:, :], probs[:, :, :], AX.X, ALU.add))
                            link(dve.reciprocal(lrec[:, :], lsum[:, :]))
                            link(dve.tensor_tensor(probs[:, :, :], probs[:, :, :],
                                                   lrec[:, :].rearrange("p (k o) -> p k o", o=1).to_broadcast([TOK, GB, 3]), ALU.mult))
                            for k in range(GB):
                                dve.wait_ge(eo_ps, OPEN + g * GB + k + 1)
                                bank = ps[0:TOK, 4 + k, :]
                                dve.tensor_tensor(eo[:, k, :], bank[:, 0:3 * P], R[:, ROWS["eb2"][0]:ROWS["eb2"][1]], ALU.add).then_inc(eo_out, 1)
                                dve.tensor_tensor(gp[:, k, :], bank[:, 3 * P:4 * P], R[:, ROWS["gb2"][0]:ROWS["gb2"][1]], ALU.add).then_inc(gp_ready, 1)
                            for k in range(GB):
                                dve.wait_ge(eo_out, OPEN + g * GB + k + 1)
                                link(dve.tensor_scalar(routed[:, k, :], eo[:, k, 0:P], probs[:, k, 0:1], None, ALU.mult))
                                for e in (1, 2):
                                    link(dve.scalar_tensor_tensor(routed[:, k, :], eo[:, k, e * P:(e + 1) * P], probs[:, k, e:e + 1],
                                                                  routed[:, k, :], ALU.mult, ALU.add))
                            olink = Chain(dve, out_chain, g, 4)
                            dve.wait_ge(tanh_ready, OPEN + g + 1)
                            olink(dve.tensor_scalar(gate[:, :, :], gt[:, :, :], 0.5, 0.5, ALU.mult, ALU.add))
                            dve.wait_ge(out_ps, OPEN + g + 1)
                            olink(dve.tensor_tensor(dx[:, :, :], ps[0:TOK, 3, 0:GB * P].rearrange("p (k c) -> p k c", k=GB),
                                                    row("outb", [TOK, GB, P]), ALU.add))
                            olink(dve.tensor_tensor(dx[:, :, :], dx[:, :, :], gate[:, :, :], ALU.mult))
                            xs = X[:, bass.ds(g * GB, GB), :]
                            olink(dve.tensor_tensor(xs, xs, dx[:, :, :], ALU.add))

                    @block.tensor
                    def _(pe):
                        pe.wait_ge(w_in, OPEN + 32)

                        def over_inputs(o, w0, width, dst_cols=None):
                            for i in range(3):
                                mm = pe.matmul(o, W[:, w0 + i * width:w0 + i * width + P], comb[:, i, :], start=(i == 0), stop=(i == 2))
                            return mm

                        with pe.Fori(0, NG) as g:
                            pe.wait_ge(out_chain, OPEN + g * 4)
                            pe.matmul(ps[:, 0, 0:GT], W[:, n["wv"]:n["wv"] + P], AT[:, 0, bass.ds(g * GT, GT)], start=True, stop=True).then_inc(ev_ps, 1)
                            pe.wait_ge(comb_ready, OPEN + (g + 1) * 3)
                            for k in range(GB):
                                for i in range(3):
                                    mm = pe.matmul(ps[0:TOK, 1, 3 * k:3 * k + 3], comb[:, i, k * TOK:(k + 1) * TOK],
                                                   W[:, n["router"] + 3 * i:n["router"] + 3 * i + 3], start=(i == 0), stop=(i == 2))
                            mm.then_inc(logit_ps, 1)
                            for j in range(7):
                                if j >= 2:
                                    pe.wait_ge(hid_ready, OPEN + g * 7 + j - 1)
                                o = ps[:, 2 + j % 2, 0:GT]
                                if j < 6:
                                    over_inputs(o, n["w1"] + (j // 2) * 6 * P + (j % 2) * P, 2 * P).then_inc(hid_ps, 1)
                                else:
                                    over_inputs(o, n["gw1"], P).then_inc(hid_ps, 1)
                            pe.wait_ge(hid_ready, OPEN + (g + 1) * 7)
                            for k in range(GB):
                                s = slice(k * TOK, (k + 1) * TOK)
                                bank = ps[0:TOK, 4 + k, :]
                                for e in range(3):
                                    for i in range(2):
                                        pe.matmul(bank[:, e * P:(e + 1) * P], hid[:, 2 * e + i, s],
                                                  W[:, n["w2"] + (2 * e + i) * P:n["w2"] + (2 * e + i + 1) * P], start=(i == 0), stop=(i == 1))
                                pe.matmul(bank[:, 3 * P:4 * P], hid[:, 6, s], W[:, n["gw2"]:n["gw2"] + P], start=True, stop=True).then_inc(eo_ps, 1)
                            for k in range(GB):
                                pe.wait_ge(rchain, OPEN + g * (3 + 3 * GB) + 3 + 3 * (k + 1))
                                tr = pe.transpose(ps[:, 2, k * TOK:(k + 1) * TOK], routed[:, k, :], ident[0:TOK, 0:TOK])
                            tr.then_inc(rT_ps, 1)
                            pe.wait_ge(rT_ready, OPEN + g + 1)
                            for k in range(GB):
                                mm = pe.matmul(ps[0:TOK, 3, k * P:(k + 1) * P], rT[:, k * TOK:(k + 1) * TOK],
                                               W[:, n["out"]:n["out"] + P], start=True, stop=True)
                            mm.then_inc(out_ps, 1)

                    @block.scalar
                    def _(act):
                        with act.Fori(0, NG) as g:
                            act.wait_ge(lchain, OPEN + (g + 1) * 3)
                            act.activation(probs[:, :, :], logit[:, :, :], ACT.Exp).then_inc(exp_ready, 1)
                            for j in range(7):
                                act.wait_ge(hid_ps, OPEN + g * 7 + j + 1)
                                act.activation(hid[:, j, :], ps[:, 2 + j % 2, 0:GT], ACT.Silu,
                                               bias=col("eb1", j) if j < 6 else col("gb1")).then_inc(hid_ready, 1)
                            act.wait_ge(gp_ready, OPEN + (g + 1) * GB)
                            act.activation(gt[:, :, :], gp[:, :, :], ACT.Tanh, scale=0.5).then_inc(tanh_ready, 1)
                            act.wait_ge(rT_ps, OPEN + g + 1)
                            act.activation(rT[:, :], ps[:, 2, 0:GT], ACT.Copy).then_inc(rT_ready, 1)

        def pre3():
            with Stage("pre3") as st:
                W = st.sb("w", [P, P])
                w_in = st.sem("w_in")
                norm = Norm(st, "ln", 1e-5)
                q_ps, q_out = st.sem("q_ps"), st.sem("q_out")
                ps = st.ps
                with st.block() as block:
                    @block.sync
                    def _(sp):
                        weights_in(sp, W, "pre3", w_in)

                    @block.vector
                    def _(dve):
                        with dve.Fori(0, NG) as g:
                            dve.wait_ge(norm.xnT_ready, OPEN + g)
                            dve.sem_inc(passed, 1)
                            norm.vector(dve, g)

                    @block.gpsimd
                    def _(pool):
                        norm.gpsimd_init(pool)
                        with pool.Fori(0, NG) as g:
                            norm.gpsimd(pool, g)

                    @block.tensor
                    def _(pe):
                        pe.wait_ge(w_in, OPEN + 16)
                        with pe.Fori(0, NG) as g:
                            norm.tensor(pe, g, ps[:, 2, :])
                            pe.wait_ge(norm.h_ready, OPEN + (g + 1) * GB)
                            pe.wait_ge(q_out, OPEN + g)
                            pe.matmul(ps[:, 3, 0:GT], W[:, :], norm.h[:, :], start=True, stop=True).then_inc(q_ps, 1)

                    @block.scalar
                    def _(act):
                        with act.Fori(0, NG) as g:
                            norm.scalar(act, g, ps[:, 2, :], by_mod(12), by_mod(13))
                            act.wait_ge(q_ps, OPEN + g + 1)
                            act.sem_inc(passed, 1)
                            act.activation(QT[:, bass.ds(g * GT, GT)], ps[:, 3, 0:GT], ACT.Identity, bias=col("bq3")).then_inc(q_out, 1)

        def post3():
            with Stage("post3") as st:
                W = st.sb("w", [P, 2 * P])
                w_in, out_done = st.sem("w_in"), st.sem("out_done")
                res = Residual(st, "o", "bo3", None)
                ps = st.ps
                with st.block() as block:
                    @block.sync
                    def _(sp):
                        weights_in(sp, W, "post3", w_in)
                        with sp.Fori(0, NG) as g:
                            sp.wait_ge(res.x_ready, OPEN + g + 1)
                            sp.sem_inc(passed, 1)
                            sp.dma_start(out[bass.ds(g * GB, GB)].rearrange("b t c -> t b c"),
                                         X[:, bass.ds(g * GB, GB), :]).then_inc(out_done, 16)
                        sp.wait_ge(out_done, OPEN + 16 * NG)

                    @block.vector
                    def _(dve):
                        with dve.Fori(0, NG) as g:
                            res.vector_gate(dve, g, ps[:, 0, :])
                            res.vector_add(dve, g, ps[:, 1, :])

                    @block.tensor
                    def _(pe):
                        pe.wait_ge(w_in, OPEN + 16)
                        with pe.Fori(0, NG) as g:
                            pe.wait_ge(res.x_ready, OPEN + g)
                            res.product(pe, g, ps[:, 0, :], W)
                            res.tensor(pe, g, ps[:, 1, :])

        stages = [
            lambda: pre("pre0", "pre0", by_mod(1), by_mod(0), 1e-6, "bk0", "bq0"),
            lambda: self_attend("self0", "bv0"),
            lambda: mid("mid0", "mid0", "bo0", by_mod(2), by_col("ng0"), by_col("nb0"), "bqc0"),
            lambda: cross_attend("cross0", "kv0", "bkc0", "bvc0", 0),
            lambda: post("post0", "post0", "boc0", by_mod(4), by_mod(3), "b10", "b20", by_mod(5)),
            lambda: pre("pre1", "pre1", by_mod(7), by_mod(6), 1e-6, "bk1", "bq1"),
            lambda: self_attend("self1", "bv1"),
            lambda: mid("mid1", "mid1", "bo1", by_mod(8), None, None, "bqc1"),
            lambda: cross_attend("cross1", "kv1", "bkc1", "bvc1", NB * 16, normed=True),
            lambda: post("post1", "post1", "boc1", by_mod(10), by_mod(9), "b11", "b21", by_mod(11)),
            pre2, attend2, experts, pre3,
            lambda: cross_attend("cross3", "kv3", "bkc3", "bvc3", NB * (16 + 32), normed=True, eps=1e-5, modulated=True),
            post3,
        ]
        KT = V0 = None
        for n, s in enumerate(stages[:last]):
            if n in (0, 5, 10):
                kv_scope = ExitStack()
                KT = kv_scope.enter_context(nc.sbuf_tensor(f"k_channels_{n}", [P, NB * TOK], F32))
                if n < 10:
                    V0 = kv_scope.enter_context(nc.sbuf_tensor(f"v_tokens_{n}", [TOK, NB, P], F32))
            s()
            if n in (1, 6, 12):
                kv_scope.close()
        if probe is not None:
            probe(nc, dict(X=X, QT=QT, KT=KT, V0=V0, AT=AT, MOD=MOD))


def layout(t):
    L0, L1, L2, L3 = ({k[len(f"L{n}_xcond_"):]: v for k, v in t.items() if k.startswith(f"L{n}_xcond_")} for n in range(4))

    def blocks(w):
        n = w.shape[0] // P
        return [w[i * P:(i + 1) * P] for i in range(n)]

    def cat(*parts):
        return np.concatenate([np.ascontiguousarray(x) for x in parts], axis=1)

    kvc = L1["W_kvc"]
    place = np.array([[(2 * (COLT * u + r // 32) + r % 32 // DH) * DH + r % DH if r % 32 < 2 * DH else -1
                       for u in range(NHALF)] for r in range(P)])

    def halves(w):
        return [np.where(place[:, u:u + 1] >= 0, w[place[:, u]], np.float32(0)) for u in range(NHALF)]

    def half_columns(v):
        return np.where(place >= 0, v[place], np.float32(0))

    groups = {
        "mod": cat(L0["ada_w"], L1["W_mod"], L3["Wss_q"], L3["Wss_kv"]),
        "pre0": cat(L0["qkv_w"][:, P:2 * P][:, PERM], L0["qkv_w"][:, 2 * P:], L0["qkv_w"][:, :P][:, PERM]),
        "mid0": cat(*halves(L0["self_o_w"]), L0["q_w"][:, PERM]),
        "kv0": cat(L0["kv_w"][:, :P][:, PERM], L0["kv_w"][:, P:]),
        "post0": cat(*halves(L0["cross_o_w"]), L0["mlp_w1"], *blocks(L0["mlp_w2"])),
        "pre1": cat(L1["W_qkv"][:, P:2 * P][:, PERM], L1["W_qkv"][:, 2 * P:], L1["W_qkv"][:, :P][:, PERM]),
        "mid1": cat(*halves(L1["W_proj"]), L1["W_qc"][:, PERM]),
        "kv1": cat(kvc[:, :P][:, PERM], kvc[:, P:]),
        "post1": cat(*halves(L1["W_cproj"]), L1["W_mlp1"], *blocks(L1["W_mlp2"])),
        "pre2": cat(L2["Wq"], L2["Wk"].T),
        "moe": cat(L2["Wv"], *blocks(L2["router_W"]), *[b for e in range(3) for b in blocks(L2["e_w1"][e])],
                   *blocks(L2["gate_w1"]), *[b for e in range(3) for b in blocks(L2["e_w2"][e])],
                   L2["gate_w2"], L2["out_w"]),
        "pre3": L3["Wq"][:, PERM],
        "kv3": cat(L3["Wkv"][:, :P][:, PERM], L3["Wkv"][:, P:]),
        "post3": cat(*halves(L3["Wp"])),
    }
    for n, g in groups.items():
        a, b = WEIGHTS[n]
        assert g.shape == (P, b - a), (n, g.shape, b - a)

    def columns(v):
        return np.ascontiguousarray(v.reshape(-1, P).T)

    cols = {
        "mod": cat(columns(L0["ada_b"]), columns(L1["b_mod"]), columns(L3["bss_q"]), columns(L3["bss_kv"])),
        "bq0": columns(L0["qkv_b"][:P][PERM]), "bk0": columns(L0["qkv_b"][P:2 * P][PERM]), "bv0": half_columns(L0["qkv_b"][2 * P:]),
        "bo0": columns(L0["self_o_b"]), "ng0": columns(L0["norm2_g"]), "nb0": columns(L0["norm2_b"]),
        "bqc0": columns(L0["q_b"][PERM]), "bkc0": columns(L0["kv_b"][:P][PERM]), "bvc0": half_columns(L0["kv_b"][P:]),
        "boc0": columns(L0["cross_o_b"]), "b10": columns(L0["mlp_b1"]), "b20": columns(L0["mlp_b2"]),
        "bq1": columns(L1["b_qkv"][:P][PERM]), "bk1": columns(L1["b_qkv"][P:2 * P][PERM]), "bv1": half_columns(L1["b_qkv"][2 * P:]),
        "bo1": columns(L1["b_proj"]), "bqc1": columns(L1["b_qc"][PERM]), "bkc1": columns(L1["b_kvc"][:P][PERM]),
        "bvc1": half_columns(L1["b_kvc"][P:]), "boc1": columns(L1["b_cproj"]), "b11": columns(L1["b_mlp1"]), "b21": columns(L1["b_mlp2"]),
        "ng2": columns(L2["ln_gamma"]), "nb2": columns(L2["ln_beta"]), "eb1": columns(L2["e_b1"]), "gb1": columns(L2["gate_b1"]),
        "bq3": columns(L3["bq"][PERM]), "bkc3": columns(L3["bkv"][:P][PERM]), "bvc3": half_columns(L3["bkv"][P:]), "bo3": columns(L3["bp"]),
    }
    assert list(cols) == list(COLS.at)
    rows = [L2["router_b"], L2["e_b2"].reshape(-1), L2["gate_b2"], L2["out_b"]]
    lane = np.arange(P)
    own = (lane[:, None] // DH % 2 == np.arange(2)[None, :])
    arrays = {
        "x": t["x"],
        "ctx_t": np.swapaxes(t["ctx_1024"], 1, 2),
        "ctx_n": t["ctx_1024"],
        "cond_t": t["cond_1024"].T,
        "weights": cat(*groups.values()),
        "cols": cat(*cols.values()),
        "rows": np.concatenate(rows)[None, :],
        "const": cat(np.eye(P, dtype=np.float32), own.astype(np.float32)),
    }
    return {k: np.ascontiguousarray(v) for k, v in arrays.items()}, t["x"].shape


def kernel(**inputs):
    import numpy as _np
    import concourse.bacc as _bacc
    from concourse import mybir as _mybir
    from concourse.bass_utils import run_bass_kernel_spmd as _run

    arrays, shape = layout({k: _np.asarray(v) for k, v in inputs.items()})
    nc = _bacc.Bacc("TRN2", target_bir_lowering=False, num_devices=1)
    aps = {n: nc.dram_tensor(f"in_{n}", a.shape, _mybir.dt.float32, kind="ExternalInput").ap() for n, a in arrays.items()}
    out = nc.dram_tensor("out_0", shape, _mybir.dt.float32, kind="ExternalOutput").ap()
    build(nc, out=out, NB=shape[0], **aps)
    r = _run(nc, [{f"in_{n}": a for n, a in arrays.items()}], core_ids=[0])
    return r.results[0]["out_0"]
```

```python
from contextlib import ExitStack

import numpy as np
import concourse.bass as bass
from concourse import mybir

F32 = mybir.dt.float32
BF16 = mybir.dt.bfloat16
ALU = mybir.AluOpType
ACT = mybir.ActivationFunctionType
AX = mybir.AxisListType

P = 128
TOK = 100
CTX = 1444
HEADS = 16
DH = 8
PAIRS = HEADS // 2
GB = 4
GT = GB * TOK
KC = 121
CHUNKS = -(-CTX // KC)
KLAST = CTX - (CHUNKS - 1) * KC
BLK = 4 * KC
ISQ = float(DH) ** -0.5
SLOT = 64
MROWS = 2
TERMS = 6
K_PART = (0, 0, 0, 1, 1, 2)
Q_PART = (0, 1, 2, 0, 1, 0)
QBLK = CTX // 4

OPEN = 1
COLT = 4
NHALF = PAIRS // COLT
PERM = [(2 * p + a) * DH + d for a in range(2) for d in range(DH) for p in range(PAIRS)]


class Layout:

    def __init__(self):
        self.at, self.width = {}, 0

    def add(self, name, n):
        self.at[name] = (self.width, self.width + n)
        self.width += n

    def __getitem__(self, name):
        return self.at[name]


WEIGHTS = Layout()
COLS = Layout()
ROWS = Layout()
CONST = Layout()

for _name, _n in [("mod", 16 * P),
                  ("pre0", 3 * P), ("mid0", 3 * P), ("kv0", 2 * P), ("post0", 10 * P),
                  ("pre1", 3 * P), ("mid1", 3 * P), ("kv1", 2 * P), ("post1", 10 * P),
                  ("pre2", 2 * P), ("moe", P + 9 + 18 * P + 3 * P + 6 * P + 2 * P),
                  ("pre3", P), ("kv3", 2 * P), ("post3", 2 * P)]:
    WEIGHTS.add(_name, _n)
for _name, _n in [("mod", 16), ("bq0", 1), ("bk0", 1), ("bv0", 2), ("bo0", 1), ("ng0", 1), ("nb0", 1), ("bqc0", 1),
                  ("bkc0", 1), ("bvc0", 2), ("boc0", 1), ("b10", 4), ("b20", 1),
                  ("bq1", 1), ("bk1", 1), ("bv1", 2), ("bo1", 1), ("bqc1", 1),
                  ("bkc1", 1), ("bvc1", 2), ("boc1", 1), ("b11", 4), ("b21", 1),
                  ("ng2", 1), ("nb2", 1), ("eb1", 6), ("gb1", 1),
                  ("bq3", 1), ("bkc3", 1), ("bvc3", 2), ("bo3", 1)]:
    COLS.add(_name, _n)
for _name, _n in [("router", 3), ("eb2", 3 * P), ("gb2", P), ("outb", P)]:
    ROWS.add(_name, _n)
CONST.add("ident", P)
CONST.add("mask", 2)


def build(nc, x, ctx_t, ctx_n, cond_t, weights, cols, rows, const, out, NB, last=99, probe=None):
    NG = NB // GB
    with ExitStack() as top:
        def keep(name, shape, dt=F32):
            return top.enter_context(nc.sbuf_tensor(name, shape, dt))

        X = keep("x_tokens", [TOK, NB, P])
        QT = keep("q_channels", [P, NB * TOK])
        AT = keep("attn_channels", [P, NHALF, NB * TOK])
        MOD = keep("modulation", [P, 16, NB])
        COND = keep("cond", [P, NB])
        C = keep("bias_columns", [P, COLS.width])
        K = keep("constants", [P, CONST.width])
        passed = top.enter_context(nc.semaphore("passed"))
        ctx_in = top.enter_context(nc.semaphore("ctx_in"))
        ident = K[:, CONST["ident"][0]:CONST["ident"][1]]
        mask = K[:, CONST["mask"][0]:CONST["mask"][1]]

        def col(name, n=0, rows=P):
            return C[0:rows, COLS[name][0] + n:COLS[name][0] + n + 1]

        class Stage:

            def __init__(self, name):
                self.name = name

            def __enter__(self):
                self.stack = ExitStack()
                self.sems = []
                self.ps = self.stack.enter_context(nc.psum_tensor(f"{self.name}_psum", [P, 8, 512], F32))
                return self

            def sb(self, name, shape, dt=F32):
                return self.stack.enter_context(nc.sbuf_tensor(f"{self.name}_{name}", shape, dt))

            def sem(self, name):
                s = self.stack.enter_context(nc.semaphore(f"{self.name}_{name}"))
                self.sems.append(s)
                return s

            def block(self):
                for s in self.sems:
                    nc.gpsimd.sem_inc(s, 1)
                nc.all_engine_barrier()
                return nc.Block()

            def __exit__(self, *a):
                if a[0] is None:
                    nc.all_engine_barrier()
                    for s in self.sems:
                        nc.gpsimd.sem_clear(s)
                    nc.all_engine_barrier()
                self.stack.close()

        class Chain:

            def __init__(self, eng, sem, it, per, own=False):
                self.eng, self.sem, self.it, self.per, self.n, self.own = eng, sem, it, per, 0, own

            def __call__(self, ins):
                self.n += 1
                ins.then_inc(self.sem, 1)
                if self.own:
                    self.eng.wait_ge(self.sem, OPEN + self.it * self.per + self.n)
                    self.eng.sem_inc(passed, 1)
                else:
                    self.eng.wait_ge(self.sem, OPEN + self.it * self.per + self.n)

        def weights_in(sp, tile, name, sem):
            a, b = WEIGHTS[name]
            sp.dma_start(tile[:, :], weights[:, a:b]).then_inc(sem, 16)

        with Stage("mods") as st:
            W = st.sb("w", [P, 16 * P])
            SC = st.sb("silu_cond", [P, NB])
            x_in = st.sem("x_in")
            constants_in = st.sem("constants_in")
            w_in = st.sem("w_in")
            silu_ready = st.sem("silu_ready")
            mod_ps = st.sem("mod_ps")
            mod_ready = st.sem("mod_ready")
            with st.block() as block:
                @block.sync
                def _(sp):
                    sp.dma_start(COND[:, :], cond_t).then_inc(constants_in, 16)
                    sp.dma_start(C[:, :], cols).then_inc(constants_in, 16)
                    sp.dma_start(K[:, :], const).then_inc(constants_in, 16)
                    weights_in(sp, W, "mod", w_in)
                    sp.dma_start(X[:, :, :], x.rearrange("b t c -> t b c")).then_inc(x_in, 16)
                    sp.wait_ge(x_in, OPEN + 16)

                @block.scalar
                def _(act):
                    act.wait_ge(constants_in, OPEN + 48)
                    act.activation(SC[:, :], COND[:, :], ACT.Silu).then_inc(silu_ready, 1)

                @block.tensor
                def _(pe):
                    pe.wait_ge(silu_ready, OPEN + 1)
                    pe.wait_ge(w_in, OPEN + 16)
                    for k in range(16):
                        mm = pe.matmul(st.ps[:, 0, k * NB:(k + 1) * NB], W[:, k * P:(k + 1) * P], SC[:, :],
                                       start=True, stop=True)
                    mm.then_inc(mod_ps, 1)

                @block.vector
                def _(dve):
                    dve.wait_ge(mod_ps, OPEN + 1)
                    b0 = COLS["mod"][0]
                    dve.tensor_tensor(MOD[:, :, :], st.ps[:, 0, 0:16 * NB].rearrange("p (k b) -> p k b", k=16),
                                      C[:, b0:b0 + 16].rearrange("p (k o) -> p k o", o=1).to_broadcast([P, 16, NB]), ALU.add).then_inc(mod_ready, 1)
                    dve.wait_ge(mod_ready, OPEN + 1)
                    for n in (1, 4, 7, 10, 12, 14):
                        dve.tensor_scalar(MOD[:, n, :], MOD[:, n, :], 1.0, None, ALU.add).then_inc(mod_ready, 1)
                    dve.wait_ge(mod_ready, OPEN + 7)

        class Norm:

            def __init__(self, st, tag, eps):
                self.eps = eps
                self.stats = st.sb(tag + "_stats", [TOK, GB, 6])
                self.mv = st.sb(tag + "_mean_var", [TOK, GB, 2])
                self.ve = st.sb(tag + "_var_eps", [TOK, GB])
                self.half = st.sb(tag + "_minus_half", [TOK, GB])
                self.rstd = st.sb(tag + "_rstd", [TOK, GB])
                self.xn = st.sb(tag + "_xn", [TOK, GB, P])
                self.h = st.sb(tag + "_h", [P, GT])
                self.stats_done = st.sem(tag + "_stats_done")
                self.var_ready = st.sem(tag + "_var_ready")
                self.rstd_ready = st.sem(tag + "_rstd_ready")
                self.xn_ready = st.sem(tag + "_xn_ready")
                self.xnT_ready = st.sem(tag + "_xnT_ready")
                self.h_ready = st.sem(tag + "_h_ready")

            def vector(self, dve, g):
                for k in range(GB):
                    ins = dve.bn_stats(self.stats[:, k, :], X[:, g * GB + k, :])
                    ins.then_inc(self.stats_done, 1)
                for k in range(GB):
                    dve.wait_ge(self.stats_done, OPEN + g * 2 * GB + GB)
                    dve.sem_inc(passed, 1)
                    dve.bn_aggr(self.mv[:, k, :], self.stats[:, k, :]).then_inc(self.stats_done, 1)
                dve.wait_ge(self.stats_done, OPEN + g * 2 * GB + 2 * GB)
                dve.tensor_scalar(self.ve[:, :], self.mv[:, :, 1], self.eps, None, ALU.add).then_inc(self.var_ready, 1)
                dve.wait_ge(self.rstd_ready, OPEN + g + 1)
                for k in range(GB):
                    dve.tensor_scalar(self.xn[:, k, :], X[:, g * GB + k, :], self.mv[:, k, 0:1],
                                      self.rstd[:, k:k + 1], ALU.subtract, ALU.mult).then_inc(self.xn_ready, 1)

            def gpsimd_init(self, pool):
                pool.memset(self.half[:, :], -0.5).then_inc(self.var_ready, 1)

            def gpsimd(self, pool, g):
                pool.wait_ge(self.var_ready, OPEN + g + 2)
                pool.tensor_tensor(self.rstd[:, :], self.ve[:, :], self.half[:, :], ALU.pow).then_inc(self.rstd_ready, 1)

            def tensor(self, pe, g, bank):
                for k in range(GB):
                    pe.wait_ge(self.xn_ready, OPEN + g * GB + k + 1)
                    tr = pe.transpose(bank[:, k * TOK:(k + 1) * TOK], self.xn[:, k, :], ident[0:TOK, 0:TOK])
                tr.then_inc(self.xnT_ready, 1)

            def scalar(self, act, g, bank, scale, shift):
                act.wait_ge(self.xnT_ready, OPEN + g + 1)
                act.sem_inc(passed, 1)
                if scale is None:
                    act.activation(self.h[:, :], bank[:, 0:GT], ACT.Copy).then_inc(self.h_ready, GB)
                    return
                for k in range(GB):
                    act.activation(self.h[:, k * TOK:(k + 1) * TOK], bank[:, k * TOK:(k + 1) * TOK], ACT.Identity,
                                   scale=scale(g, k), bias=shift(g, k)).then_inc(self.h_ready, 1)

        def by_mod(n):
            return lambda g, k: MOD[:, n, bass.ds(g * GB + k, 1)]

        def by_col(name):
            return lambda g, k: col(name)

        def pre(name, weights_name, scale, shift, eps, bk, bq):
            with Stage(name) as st:
                nw = 3 if bq else 2
                W = st.sb("w", [P, nw * P])
                w_in = st.sem("w_in")
                norm = Norm(st, "ln", eps)
                k_ps, q_ps, v_ps = st.sem("k_ps"), st.sem("q_ps"), st.sem("v_ps")
                qk_out, v_out = st.sem("qk_out"), st.sem("v_out")
                ps = st.ps
                nqk = nw - 1
                with st.block() as block:
                    @block.sync
                    def _(sp):
                        weights_in(sp, W, weights_name, w_in)

                    @block.vector
                    def _(dve):
                        with dve.Fori(0, NG) as g:
                            dve.wait_ge(qk_out, OPEN + g * nqk)
                            dve.sem_inc(passed, 1)
                            norm.vector(dve, g)
                            dve.wait_ge(v_ps, OPEN + g + 1)
                            dve.tensor_copy(V0[:, bass.ds(g * GB, GB), :],
                                            ps[0:TOK, 3, 0:GB * P].rearrange("p (k c) -> p k c", k=GB)).then_inc(v_out, 1)

                    @block.gpsimd
                    def _(pool):
                        norm.gpsimd_init(pool)
                        with pool.Fori(0, NG) as g:
                            norm.gpsimd(pool, g)

                    @block.tensor
                    def _(pe):
                        pe.wait_ge(w_in, OPEN + 16)
                        with pe.Fori(0, NG) as g:
                            norm.tensor(pe, g, ps[:, 0, :])
                            pe.wait_ge(norm.h_ready, OPEN + (g + 1) * GB)
                            pe.wait_ge(qk_out, OPEN + g * nqk)
                            pe.matmul(ps[:, 1, 0:GT], W[:, 0:P], norm.h[:, :], start=True, stop=True).then_inc(k_ps, 1)
                            if bq:
                                pe.matmul(ps[:, 2, 0:GT], W[:, 2 * P:3 * P], norm.h[:, :], start=True, stop=True).then_inc(q_ps, 1)
                            pe.wait_ge(v_out, OPEN + g)
                            for k in range(GB):
                                mm = pe.matmul(ps[0:TOK, 3, k * P:(k + 1) * P], norm.h[:, k * TOK:(k + 1) * TOK],
                                               W[:, P:2 * P], start=True, stop=True)
                            mm.then_inc(v_ps, 1)

                    @block.scalar
                    def _(act):
                        with act.Fori(0, NG) as g:
                            act.wait_ge(v_ps, OPEN + g)
                            norm.scalar(act, g, ps[:, 0, :], scale, shift)
                            act.wait_ge(k_ps, OPEN + g + 1)
                            act.sem_inc(passed, 1)
                            act.activation(KT[:, bass.ds(g * GT, GT)], ps[:, 1, 0:GT], ACT.Identity, bias=col(bk)).then_inc(qk_out, 1)
                            if bq:
                                act.wait_ge(q_ps, OPEN + g + 1)
                                act.sem_inc(passed, 1)
                                act.activation(QT[:, bass.ds(g * GT, GT)], ps[:, 2, 0:GT], ACT.Identity, bias=col(bq)).then_inc(qk_out, 1)

        class Residual:

            def __init__(self, st, tag, bias, gate):
                self.bias, self.gate = bias, gate
                self.y = st.sb(tag + "_y", [P, GT])
                self.y_ps = st.sem(tag + "_y_ps")
                self.y_ready = st.sem(tag + "_y_ready")
                self.yT_ready = st.sem(tag + "_yT_ready")
                self.x_ready = st.sem(tag + "_x_ready")

            def product(self, pe, g, bank, W):
                for u in range(NHALF):
                    mm = pe.matmul(bank[:, 0:GT], W[:, u * P:(u + 1) * P], AT[:, u, bass.ds(g * GT, GT)],
                                   start=(u == 0), stop=(u == NHALF - 1))
                mm.then_inc(self.y_ps, 1)

            def vector_gate(self, dve, g, bank):
                dve.wait_ge(self.y_ps, OPEN + g + 1)
                for k in range(GB):
                    s = slice(k * TOK, (k + 1) * TOK)
                    if self.gate is None:
                        ins = dve.tensor_scalar(self.y[:, s], bank[:, s], col(self.bias), None, ALU.add)
                    else:
                        ins = dve.tensor_scalar(self.y[:, s], bank[:, s], col(self.bias), self.gate(g, k), ALU.add, ALU.mult)
                    ins.then_inc(self.y_ready, 1)

            def tensor(self, pe, g, bank):
                for k in range(GB):
                    pe.wait_ge(self.y_ready, OPEN + g * GB + k + 1)
                    tr = pe.transpose(bank[0:TOK, k * P:(k + 1) * P], self.y[:, k * TOK:(k + 1) * TOK], ident)
                tr.then_inc(self.yT_ready, 1)

            def vector_add(self, dve, g, bank):
                dve.wait_ge(self.yT_ready, OPEN + g + 1)
                xs = X[:, bass.ds(g * GB, GB), :]
                dve.tensor_tensor(xs, xs, bank[0:TOK, 0:GB * P].rearrange("p (k c) -> p k c", k=GB), ALU.add).then_inc(self.x_ready, 1)
                dve.wait_ge(self.x_ready, OPEN + g + 1)
                dve.sem_inc(passed, 1)

        def mid(name, weights_name, bo, gate, scale, shift, bq):
            with Stage(name) as st:
                W = st.sb("w", [P, 3 * P])
                w_in = st.sem("w_in")
                res = Residual(st, "o", bo, gate)
                norm = Norm(st, "ln", 1e-6)
                q_ps, q_out = st.sem("q_ps"), st.sem("q_out")
                ps = st.ps
                with st.block() as block:
                    @block.sync
                    def _(sp):
                        weights_in(sp, W, weights_name, w_in)

                    @block.vector
                    def _(dve):
                        with dve.Fori(0, NG) as g:
                            res.vector_gate(dve, g, ps[:, 0, :])
                            res.vector_add(dve, g, ps[:, 1, :])
                            norm.vector(dve, g)

                    @block.gpsimd
                    def _(pool):
                        norm.gpsimd_init(pool)
                        with pool.Fori(0, NG) as g:
                            norm.gpsimd(pool, g)

                    @block.tensor
                    def _(pe):
                        pe.wait_ge(w_in, OPEN + 16)
                        with pe.Fori(0, NG) as g:
                            res.product(pe, g, ps[:, 0, :], W)
                            res.tensor(pe, g, ps[:, 1, :])
                            norm.tensor(pe, g, ps[:, 2, :])
                            pe.wait_ge(norm.h_ready, OPEN + (g + 1) * GB)
                            pe.wait_ge(q_out, OPEN + g)
                            pe.matmul(ps[:, 3, 0:GT], W[:, 2 * P:3 * P], norm.h[:, :], start=True, stop=True).then_inc(q_ps, 1)

                    @block.scalar
                    def _(act):
                        with act.Fori(0, NG) as g:
                            norm.scalar(act, g, ps[:, 2, :], scale, shift)
                            act.wait_ge(q_ps, OPEN + g + 1)
                            act.sem_inc(passed, 1)
                            act.activation(QT[:, bass.ds(g * GT, GT)], ps[:, 3, 0:GT], ACT.Identity, bias=col(bq)).then_inc(q_out, 1)

        def post(name, weights_name, bo, scale, shift, b1, b2, gate):
            with Stage(name) as st:
                W = st.sb("w", [P, 10 * P])
                hid = st.sb("hidden", [P, 4, GT])
                w_in = st.sem("w_in")
                res = Residual(st, "o", bo, None)
                norm = Norm(st, "ln", 1e-6)
                res2 = Residual(st, "mlp", b2, gate)
                hid_ps, hid_ready = st.sem("hid_ps"), st.sem("hid_ready")
                ps = st.ps
                with st.block() as block:
                    @block.sync
                    def _(sp):
                        weights_in(sp, W, weights_name, w_in)

                    @block.vector
                    def _(dve):
                        with dve.Fori(0, NG) as g:
                            res.vector_gate(dve, g, ps[:, 0, :])
                            res.vector_add(dve, g, ps[:, 1, :])
                            norm.vector(dve, g)
                            res2.vector_gate(dve, g, ps[:, 3, :])
                            res2.vector_add(dve, g, ps[:, 1, :])

                    @block.gpsimd
                    def _(pool):
                        norm.gpsimd_init(pool)
                        with pool.Fori(0, NG) as g:
                            norm.gpsimd(pool, g)

                    @block.tensor
                    def _(pe):
                        pe.wait_ge(w_in, OPEN + 16)
                        with pe.Fori(0, NG) as g:
                            pe.wait_ge(res2.x_ready, OPEN + g)
                            res.product(pe, g, ps[:, 0, :], W)
                            res.tensor(pe, g, ps[:, 1, :])
                            norm.tensor(pe, g, ps[:, 2, :])
                            pe.wait_ge(norm.h_ready, OPEN + (g + 1) * GB)
                            for n in range(4):
                                pe.matmul(ps[:, 4 + n, 0:GT], W[:, (2 + n) * P:(3 + n) * P], norm.h[:, :],
                                          start=True, stop=True).then_inc(hid_ps, 1)
                            for n in range(4):
                                pe.wait_ge(hid_ready, OPEN + g * 4 + n + 1)
                                mm = pe.matmul(ps[:, 3, 0:GT], W[:, (6 + n) * P:(7 + n) * P], hid[:, n, :],
                                               start=(n == 0), stop=(n == 3))
                            mm.then_inc(res2.y_ps, 1)
                            pe.wait_ge(res.x_ready, OPEN + g + 1)
                            res2.tensor(pe, g, ps[:, 1, :])

                    @block.scalar
                    def _(act):
                        with act.Fori(0, NG) as g:
                            norm.scalar(act, g, ps[:, 2, :], scale, shift)
                            for n in range(4):
                                act.wait_ge(hid_ps, OPEN + g * 4 + n + 1)
                                act.activation(hid[:, n, :], ps[:, 4 + n, 0:GT], ACT.Gelu_apprx_tanh,
                                               bias=col(b1, n)).then_inc(hid_ready, 1)

        def split_rest(pool, link, parts, rest):
            link(pool.tensor_copy(parts[1], rest))
            link(pool.tensor_tensor(parts[2], rest, parts[1], ALU.subtract))

        def split(pool, link, value, parts, rest):
            link(pool.tensor_copy(parts[0], value))
            link(pool.tensor_tensor(rest, value, parts[0], ALU.subtract))
            split_rest(pool, link, parts, rest)

        def slot_rows(a, j):
            at = a * SLOT + MROWS + j * DH
            return slice(at, at + DH)

        def at(count):
            return OPEN + (max(count, 0) if isinstance(count, int) else count)

        DEN_ROWS = [2 * DH + r % (2 * DH) for r in range(32)]
        NFIN = 6

        def finish(dve, link, o_read, bank, sel, den, b, bv):
            half = bank[:, 0:NHALF * 2 * TOK].rearrange("p (u a q) -> p u a q", u=NHALF, a=2)
            link(dve.tensor_scalar(sel[:, :, :], half[:, :, 0, :], mask[:, 0:1], None, ALU.mult))
            link(dve.scalar_tensor_tensor(sel[:, :, :], half[:, :, 1, :], mask[:, 1:2], sel[:, :, :], ALU.mult, ALU.add))
            dve.sem_inc(o_read, 1)
            link(dve.stream_shuffle(den[:, :, :], sel[:, :, :], DEN_ROWS))
            link(dve.reciprocal(den[:, :, :], den[:, :, :]))
            link(dve.tensor_tensor(sel[:, :, :], sel[:, :, :], den[:, :, :], ALU.mult))
            c0 = COLS[bv][0]
            link(dve.tensor_tensor(AT[:, :, bass.ds(b * TOK, TOK)], sel[:, :, :],
                                   C[:, c0:c0 + NHALF].rearrange("p (u o) -> p u o", o=1).to_broadcast([P, NHALF, TOK]), ALU.add))

        def self_attend(name, bv):
            NU = GB * NHALF
            MAXN = GB * 4
            NPART = 8
            NPACK = (2 + 2 * 2 * TERMS) * 16
            SUMS = 4
            with Stage(name) as st:
                ps = st.ps
                kx = [st.sb(f"k_packed{s}", [P, PAIRS, GB, TOK], BF16) for s in range(2)]
                qx = [st.sb(f"q_packed{s}", [P, PAIRS, GB, 2 * TOK], BF16) for s in range(2)]
                kp = [st.sb(f"k_part{i}", [P, GT], BF16) for i in range(3)]
                qp = [st.sb(f"q_part{i}", [P, GT], BF16) for i in range(3)]
                krest = st.sb("k_rest", [P, GT])
                qrest = st.sb("q_rest", [P, GT])
                zeros = st.sb("zeros", [MROWS, PAIRS, GT], BF16)
                v = st.sb("v_and_ones", [TOK, GB, PAIRS, 32])
                prob = st.sb("prob", [TOK, 3, 2 * GT])
                nmax = st.sb("minus_max", [TOK, GB, HEADS])
                nmax1 = st.sb("minus_max_part", [TOK, GB, HEADS], BF16)
                mcols = st.sb("shift_columns", [TOK, GB, 2, MROWS, PAIRS])
                mrows = st.sb("shift_rows", [2 * MROWS * PAIRS, GT], BF16)
                sel = st.sb("own_head", [P, NHALF, TOK])
                den = st.sb("denominators", [P, NHALF, TOK])
                prepared = st.sem("prepared")
                parts_ready = st.sem("parts_ready")
                packed_in, shift_in = st.sem("packed_in"), st.sem("shift_in")
                v_ready = st.sem("v_ready")
                max_ps, max_done = st.sem("max_ps"), st.sem("max_done")
                shift_ps, shift_ready, shift_chain = st.sem("shift_ps"), st.sem("shift_ready"), st.sem("shift_chain")
                score_ps, prob_ready, pv_done = st.sem("score_ps"), st.sem("prob_ready"), st.sem("pv_done")
                fin, sums_read = st.sem("fin"), st.sem("sums_read")

                def groups(eng, body):
                    with eng.Fori(0, NG // 2) as i:
                        for s in range(2):
                            body(2 * i + s, s)

                with st.block() as block:
                    @block.sync
                    def _(sp):
                        sp.wait_ge(prepared, OPEN + 6)

                        def pack(g, s):
                            sp.wait_ge(score_ps, at((g - 1) * NU))
                            sp.wait_ge(parts_ready, at((g + 1) * NPART))
                            sp.sem_inc(passed, 1)
                            for a in range(2):
                                sp.dma_start(qx[s][a * SLOT:a * SLOT + MROWS, :, :, a * TOK:(a + 1) * TOK],
                                             zeros[:, :, :]).then_inc(packed_in, 16)
                            for a in range(2):
                                for j in range(TERMS):
                                    sp.dma_start(qx[s][slot_rows(a, j), :, :, a * TOK:(a + 1) * TOK],
                                                 qp[Q_PART[j]][a * SLOT:(a + 1) * SLOT, :]).then_inc(packed_in, 16)
                                    sp.dma_start(kx[s][slot_rows(a, j), :, :, :],
                                                 kp[K_PART[j]][a * SLOT:(a + 1) * SLOT, :]).then_inc(packed_in, 16)

                        def shift(g, s):
                            sp.wait_ge(shift_ready, at(g + 1))
                            for a in range(2):
                                n = MROWS * PAIRS
                                sp.dma_start(qx[s][a * SLOT:a * SLOT + MROWS, :, :, a * TOK:(a + 1) * TOK],
                                             mrows[a * n:(a + 1) * n, :]).then_inc(shift_in, 16)

                        for s in range(2):
                            pack(s, s)
                        with sp.Fori(0, NG // 2 - 1) as i:
                            for s in range(2):
                                shift(2 * i + s, s)
                                pack(2 * i + s + 2, s)
                        for s in range(2):
                            shift(NG - 2 + s, s)

                    @block.gpsimd
                    def _(pool):
                        pool.memset(zeros[:, :, :], 0.0).then_inc(prepared, 1)
                        for s in range(2):
                            pool.memset(kx[s][:, :, :, :], 1.0).then_inc(prepared, 1)
                        pool.memset(v[:, :, :, :], 1.0).then_inc(prepared, 1)
                        with pool.Fori(0, NG) as g:
                            link = Chain(pool, parts_ready, g, NPART, own=True)
                            pool.wait_ge(packed_in, OPEN + g * NPACK)
                            pool.sem_inc(passed, 1)
                            split(pool, link, QT[:, bass.ds(g * GT, GT)], [t[:, :] for t in qp], qrest[:, :])
                            split(pool, link, KT[:, bass.ds(g * GT, GT)], [t[:, :] for t in kp], krest[:, :])
                            assert link.n == NPART

                    @block.tensor
                    def _(pe):
                        def group(g, s):
                            pe.wait_ge(packed_in, at((g + 1) * NPACK))
                            pe.wait_ge(prob_ready, at(g * NU))
                            for n in range(MAXN):
                                if n >= 4:
                                    pe.wait_ge(max_done, at(g * MAXN + n - 3))
                                k = n // 4
                                for i in range(4):
                                    h = 4 * (n % 4) + i
                                    p, a = h // 2, h % 2
                                    mm = pe.matmul(ps[0:TOK, n % 4, i * TOK:(i + 1) * TOK],
                                                   qx[s][:, p, k, a * TOK:(a + 1) * TOK], kx[s][:, p, k, :],
                                                   start=True, stop=True)
                                mm.then_inc(max_ps, 1)
                            pe.wait_ge(shift_chain, at((g + 1) * 3))
                            pe.wait_ge(sums_read, at(g * GB))
                            for k in range(GB):
                                tr = pe.transpose(ps[0:2 * MROWS * PAIRS, SUMS, k * TOK:(k + 1) * TOK],
                                                  mcols[:, k, :, :, :].rearrange("q a i p -> q (a i p)"), ident[0:TOK, 0:TOK])
                            tr.then_inc(shift_ps, 1)
                            pe.wait_ge(v_ready, at(g + 1))
                            pe.wait_ge(shift_in, at((g + 1) * 32))
                            for n in range(NU + 1):
                                if n < NU:
                                    k, half_ = n // 2, n % 2
                                    pe.wait_ge(prob_ready, at(g * NU + max(n - 1, 0)))
                                    for i in range(4):
                                        mm = pe.matmul(ps[0:TOK, 2 * half_ + i // 2, (i % 2) * 2 * TOK:(i % 2 + 1) * 2 * TOK],
                                                       kx[s][:, 4 * half_ + i, k, :], qx[s][:, 4 * half_ + i, k, :], start=True, stop=True)
                                    mm.then_inc(score_ps, 1)
                                if n >= 1:
                                    k, half_ = (n - 1) // 2, (n - 1) % 2
                                    pe.wait_ge(prob_ready, at(g * NU + n))
                                    for j in range(COLT):
                                        mm = pe.matmul(ps[32 * j:32 * j + 32, SUMS + k, half_ * 2 * TOK:(half_ + 1) * 2 * TOK],
                                                       v[:, k, COLT * half_ + j, :], prob[:, (n - 1) % 3, j * 2 * TOK:(j + 1) * 2 * TOK],
                                                       start=True, stop=True, tile_position=(0, 32 * j))
                                    mm.then_inc(pv_done, 1)

                        groups(pe, group)

                    @block.scalar
                    def _(act):
                        act.wait_ge(prepared, OPEN + 6)
                        with act.Fori(0, NG) as g:
                            act.wait_ge(pv_done, OPEN + g * NU)
                            act.sem_inc(passed, 1)
                            act.activation(v[:, :, :, 0:2 * DH],
                                           V0[:, bass.ds(g * GB, GB), :].rearrange("p k (i c) -> p k i c", i=PAIRS),
                                           ACT.Copy).then_inc(v_ready, 1)
                            for n in range(NU):
                                act.wait_ge(score_ps, OPEN + g * NU + n + 1)
                                act.wait_ge(pv_done, OPEN + (g * NU + max(n - 2, 0)))
                                act.activation(prob[:, n % 3, :].rearrange("p (i c) -> p i c", i=2),
                                               ps[0:TOK, 2 * (n % 2):2 * (n % 2) + 2, 0:GT], ACT.Exp, scale=ISQ).then_inc(prob_ready, 1)

                    @block.vector
                    def _(dve):
                        for s in range(2):
                            dve.memset(qx[s][:, :, :, :], 0.0).then_inc(prepared, 1)
                        with dve.Fori(0, NG) as g:
                            for n in range(MAXN):
                                dve.wait_ge(max_ps, OPEN + g * MAXN + n + 1)
                                dve.tensor_reduce(nmax[:, n // 4, 4 * (n % 4):4 * (n % 4) + 4],
                                                  ps[0:TOK, n % 4, 0:GT].rearrange("p (h k) -> p h k", h=4),
                                                  AX.X, ALU.max, negate=True).then_inc(max_done, 1)
                            link = Chain(dve, shift_chain, g, 3)
                            dve.wait_ge(max_done, OPEN + (g + 1) * MAXN)
                            link(dve.tensor_copy(nmax1[:, :, :], nmax[:, :, :]))
                            hv = nmax1[:, :, :].rearrange("q k (p a) -> q k a p", a=2)
                            link(dve.tensor_copy(mcols[:, :, :, 0, :], hv))
                            link(dve.tensor_tensor(mcols[:, :, :, 1, :], nmax[:, :, :].rearrange("q k (p a) -> q k a p", a=2), hv, ALU.subtract))
                            dve.wait_ge(shift_ps, OPEN + g + 1)
                            dve.wait_ge(shift_in, OPEN + g * 32)
                            dve.tensor_copy(mrows[:, :], ps[0:2 * MROWS * PAIRS, SUMS, 0:GT]).then_inc(shift_ready, 1)
                            flink = Chain(dve, fin, g, GB * NFIN)
                            for k in range(GB):
                                dve.wait_ge(pv_done, OPEN + (g * NU + 2 * k + 2))
                                finish(dve, flink, sums_read, ps[:, SUMS + k, :], sel, den, g * GB + k, bv)
                            assert flink.n == GB * NFIN

        def shift_columns(dve, link, nmax, nmax1, mcols):
            link(dve.tensor_copy(nmax1[:, :], nmax[:, :]))
            hv = nmax1[:, :].rearrange("q (p a) -> q a p", a=2)
            link(dve.tensor_copy(mcols[:, :, 0, :], hv))
            link(dve.tensor_tensor(mcols[:, :, 1, :], nmax[:, :].rearrange("q (p a) -> q a p", a=2), hv, ALU.subtract))

        def cross_attend(name, kv, bk, bv, loads_before, normed=False, eps=1e-6, modulated=False):
            spans = [(c * KC, KC if c < CHUNKS - 1 else KLAST) for c in range(CHUNKS)]
            NU = NHALF * CHUNKS
            blocks = [(t * BLK, min(BLK, CTX - t * BLK)) for t in range(3)]
            MAXK = CTX // 3 + 1
            MAXN = 3 * HEADS
            NQPART, NKPART = 4, 6
            NSHIFT = 4
            NV = 4
            NCTX = 32 if normed else 16
            NPACK = 2 * 2 * TERMS * 16
            WORK = 4
            MAXB = 5
            FIRST = 1
            STATS_AT, V_AT = -1, -1
            X_AT, T_AT = 1, 2
            K_AT = range(T_AT + 3, T_AT + 9, 2) if normed else range(V_AT + 4, V_AT + 10, 2)
            LAG = 2
            CLEAR_AT = 1

            def maxima_of(u):
                lo, hi = (max(x - FIRST, 0) * MAXN // (NU - 1 - FIRST) for x in (u, u + 1))
                return range(min(lo, MAXN), min(hi, MAXN))

            with Stage(name) as st:
                ps = st.ps
                kx = [st.sb(f"k_packed{s}", [P, PAIRS, CTX], BF16) for s in range(3)]
                qx = [st.sb(f"q_packed{s}", [P, PAIRS, 2 * TOK], BF16) for s in range(3)]
                kp = [st.sb(f"k_part{i}", [P, CTX], BF16) for i in range(3)]
                qp = [st.sb(f"q_part{i}", [P, TOK], BF16) for i in range(3)]
                v = [st.sb(f"v_and_ones{s}", [KC, CHUNKS, PAIRS, 32]) for s in range(2)]
                krest = st.sb("k_rest", [P, CTX])
                qrest = st.sb("q_rest", [P, TOK])
                prob = st.sb("prob", [KC, 3, 2 * GT])
                zeros = st.sb("zeros", [P, PAIRS, TOK], BF16)
                bmax = st.sb("block_max", [TOK, MAXN])
                nmax = st.sb("minus_max", [TOK, HEADS])
                nmax1 = st.sb("minus_max_part", [TOK, HEADS], BF16)
                mcols = st.sb("shift_columns", [TOK, 2, MROWS, PAIRS])
                mrows = st.sb("shift_rows", [2 * MROWS * PAIRS, TOK], BF16)
                sel = st.sb("own_head", [P, NHALF, TOK])
                den = st.sb("denominators", [P, NHALF, TOK])
                W = st.sb("w", [P, 2 * P])
                xt_one = [st.sb(f"ctx_channels{s}", [P, CTX]) for s in range(1 if normed else 2)]
                xt = xt_one if not normed else xt_one * 2
                prepared, w_in = st.sem("prepared"), st.sem("w_in")
                k_ps, v_ps = st.sem("k_ps"), st.sem("v_ps")
                k1_ready, rest_ready = st.sem("k1_ready"), st.sem("rest_ready")
                qparts_ready, kparts_ready, cleared = st.sem("qparts_ready"), st.sem("kparts_ready"), st.sem("cleared")
                packed_in, shift_in = st.sem("packed_in"), st.sem("shift_in")
                v_ready = st.sem("v_ready")
                max_ps, max_done = st.sem("max_ps"), st.sem("max_done")
                shift_ps, shift_ready, shift_chain = st.sem("shift_ps"), st.sem("shift_ready"), st.sem("shift_chain")
                score_ps, prob_ready, pv_done = st.sem("score_ps"), st.sem("prob_ready"), st.sem("pv_done")
                fin, sums_read = st.sem("fin"), st.sem("sums_read")
                if normed:
                    xn = st.sb("ctx_tokens", [KC, CHUNKS, P])
                    stats = st.sb("stats", [KC, CHUNKS, 6])
                    mv = st.sb("mean_var", [KC, CHUNKS, 2])
                    ve = st.sb("var_eps", [KC, CHUNKS])
                    half = st.sb("minus_half", [KC, CHUNKS])
                    rstd = st.sb("rstd", [KC, CHUNKS])
                    xshift = st.sb("minus_mean_rstd", [KC, CHUNKS])
                    xshift_ready = st.sem("xshift_ready")
                    mv_zero = st.sem("mv_zero")
                    stats_done, var_ready, rstd_ready = st.sem("stats_done"), st.sem("var_ready"), st.sem("rstd_ready")
                    xn_ready, xnT_ps, xt_ready = st.sem("xn_ready"), st.sem("xnT_ps"), st.sem("xt_ready")

                def periods(eng, body):
                    body(-2, -2, False, False, True)
                    body(-1, -1, False, True, True)
                    with eng.Fori(0, (NB - 2) // 6) as i:
                        for r in range(6):
                            body(6 * i + r, r, True, True, True)
                    body(NB - 2, 0, True, True, False)
                    body(NB - 1, 1, True, False, False)

                with st.block() as block:
                    @block.sync
                    def _(sp):
                        weights_in(sp, W, kv, w_in)
                        sp.wait_ge(prepared, OPEN + 9)

                        def period(b, r, now, nxt, prep):
                            n, p = b + 1, b + 2
                            if prep:
                                sp.wait_ge(score_ps, at(b * NU))
                                sp.wait_ge(qparts_ready, at((p + 1) * NQPART))
                                sp.sem_inc(passed, 1)
                                for a in range(2):
                                    for j in range(TERMS):
                                        sp.dma_start(qx[(r + 2) % 3][slot_rows(a, j), :, a * TOK:(a + 1) * TOK],
                                                     qp[Q_PART[j]][a * SLOT:(a + 1) * SLOT, :]).then_inc(packed_in, 16)
                                sp.wait_ge(k1_ready, at((p + 1) * 3))
                                sp.wait_ge(kparts_ready, at((p + 1) * NKPART))
                                sp.sem_inc(passed, 1)
                                for a in range(2):
                                    for j in range(TERMS):
                                        sp.dma_start(kx[(r + 2) % 3][slot_rows(a, j), :, :],
                                                     kp[K_PART[j]][a * SLOT:(a + 1) * SLOT, :]).then_inc(packed_in, 16)
                            if nxt:
                                sp.wait_ge(shift_ready, at(n + 1))
                                for a in range(2):
                                    m = MROWS * PAIRS
                                    sp.dma_start(qx[(r + 1) % 3][a * SLOT:a * SLOT + MROWS, :, a * TOK:(a + 1) * TOK],
                                                 mrows[a * m:(a + 1) * m, :]).then_inc(shift_in, 16)

                        periods(sp, period)

                    @block.gpsimd
                    def _(pool):
                        for s in range(3):
                            pool.memset(qx[s][:, :, :], 0.0).then_inc(prepared, 1)
                        pool.memset(zeros[:, :, :], 0.0).then_inc(prepared, 1)
                        for s in range(2):
                            pool.memset(v[s][:, :, :, :], 1.0).then_inc(prepared, 1)
                        pool.memset(kx[2][:, :, :], 1.0).then_inc(prepared, 1)
                        if normed:
                            pool.memset(half[:, :], -0.5).then_inc(var_ready, 1)

                        def period(b, r, now, nxt, prep):
                            if not prep:
                                return
                            p, s = b + 2, r % 2
                            if normed:
                                pool.wait_ge(xnT_ps, at(p * 3))
                                pool.sem_inc(passed, 1)
                                pool.dma_start(xn[:, 0:CHUNKS - 1, :],
                                               ctx_n[p, 0:(CHUNKS - 1) * KC, :].rearrange("(c p) d -> p c d", p=KC)).then_inc(ctx_in, 16)
                                pool.dma_start(xn[0:KLAST, CHUNKS - 1, :], ctx_n[p, (CHUNKS - 1) * KC:CTX, :]).then_inc(ctx_in, 16)
                            else:
                                pool.wait_ge(v_ps, at((p - 1) * 3))
                                pool.sem_inc(passed, 1)
                                pool.dma_start(xt[s][:, :], ctx_t[p]).then_inc(ctx_in, 16)
                            pool.wait_ge(packed_in, at(p * NPACK))
                            pool.sem_inc(passed, 1)
                            qlink = Chain(pool, qparts_ready, p, NQPART, own=True)
                            split(pool, qlink, QT[:, bass.ds(p * TOK, TOK)], [t[:, :] for t in qp], qrest[:, :])
                            assert qlink.n == NQPART
                            if normed:
                                pool.wait_ge(var_ready, at(p + 2))
                                pool.tensor_tensor(rstd[:, :], ve[:, :], half[:, :], ALU.pow).then_inc(rstd_ready, 1)
                            klink = Chain(pool, kparts_ready, p, NKPART, own=True)
                            for t, (k0, kn) in enumerate(blocks):
                                pool.wait_ge(rest_ready, at(p * 3 + t + 1))
                                pool.sem_inc(passed, 1)
                                split_rest(pool, klink, [part[:, k0:k0 + kn] for part in kp], krest[:, k0:k0 + kn])
                            assert klink.n == NKPART

                        periods(pool, period)

                    @block.tensor
                    def _(pe):
                        pe.wait_ge(w_in, OPEN + 16)

                        def period(b, r, now, nxt, prep):
                            n, p = b + 1, b + 2
                            s, o, now_x, next_x = r % 2, 1 - r % 2, r % 3, (r + 1) % 3

                            def scores(u):
                                c, half_ = u // 2, u % 2
                                pe.wait_ge(prob_ready, at(b * NU + max(u - 1, 0)))
                                k0, kn = spans[c]
                                for i in range(4):
                                    pr = 4 * half_ + i
                                    mm = pe.matmul(ps[0:kn, 2 * (u % 2) + i // 2, (i % 2) * 2 * TOK:(i % 2 + 1) * 2 * TOK],
                                                   kx[now_x][:, pr, k0:k0 + kn], qx[now_x][:, pr, :], start=True, stop=True)
                                mm.then_inc(score_ps, 1)

                            def values(u):
                                c, half_ = u // 2, u % 2
                                if u == 0:
                                    pe.wait_ge(sums_read, at(b))
                                pe.wait_ge(prob_ready, at(b * NU + u + 1))
                                kn = spans[c][1]
                                for j in range(COLT):
                                    mm = pe.matmul(ps[32 * j:32 * j + 32, 7, half_ * 2 * TOK:(half_ + 1) * 2 * TOK],
                                                   v[s][0:kn, c, COLT * half_ + j, :], prob[0:kn, u % 3, j * 2 * TOK:(j + 1) * 2 * TOK],
                                                   start=(u == 0), stop=(u == NU - 1), tile_position=(0, 32 * j))
                                mm.then_inc(pv_done, 1)

                            def project_v(t):
                                pe.wait_ge(shift_ready, at(n))
                                pe.wait_ge(k1_ready, at((n + 1) * 3))
                                pe.wait_ge(rest_ready, at((n + 1) * 3))
                                pe.wait_ge(v_ready, at(n * NV + t))
                                if not normed:
                                    pe.wait_ge(ctx_in, loads_before + (n + 1) * NCTX)
                                else:
                                    pe.wait_ge(xt_ready, at((n + 1) * 3))
                                for c in range(4 * t, 4 * t + 4):
                                    k0, kn = spans[c]
                                    mm = pe.matmul(ps[0:kn, WORK, (c % 4) * P:(c % 4 + 1) * P], xt[o][:, k0:k0 + kn],
                                                   W[:, P:2 * P], start=True, stop=True)
                                mm.then_inc(v_ps, 1)

                            def turn(t):
                                pe.wait_ge(v_ready, at((n + 1) * NV))
                                pe.wait_ge(xt_ready, at(p * 3 + t))
                                pe.wait_ge(xn_ready, at(p * CHUNKS + 4 * t + 4))
                                for c in range(4 * t, 4 * t + 4):
                                    kn = spans[c][1]
                                    tr = pe.transpose(ps[:, WORK, (c % 4) * KC:(c % 4) * KC + kn],
                                                      xn[0:kn, c, :], ident[0:kn, 0:kn])
                                tr.then_inc(xnT_ps, 1)

                            def project_k(t):
                                if normed:
                                    pe.wait_ge(xt_ready, at((p + 1) * 3))
                                else:
                                    pe.wait_ge(ctx_in, loads_before + (p + 1) * NCTX)
                                    pe.wait_ge(v_ready, at((n + 1) * NV))
                                pe.wait_ge(k1_ready, at(p * 3 + t))
                                pe.wait_ge(rest_ready, at(p * 3 + t))
                                k0, kn = blocks[t]
                                pe.matmul(ps[:, WORK, 0:kn], W[:, 0:P], xt[s][:, k0:k0 + kn],
                                          start=True, stop=True).then_inc(k_ps, 1)

                            def maximum(m):
                                h, t = m // 3, m % 3
                                if m == 0:
                                    pe.wait_ge(packed_in, at((n + 1) * NPACK))
                                    pe.wait_ge(cleared, at((n + 1) * 2))
                                pe.wait_ge(max_done, at(n * MAXN + max(m - 1, 0)))
                                pr, a, k0 = h // 2, h % 2, t * (CTX // 3)
                                pe.matmul(ps[0:TOK, MAXB + m % 2, 0:MAXK], qx[next_x][:, pr, a * TOK:(a + 1) * TOK],
                                          kx[next_x][:, pr, k0:k0 + MAXK], start=True, stop=True).then_inc(max_ps, 1)

                            def turn_shift():
                                pe.wait_ge(shift_chain, at((n + 1) * NSHIFT))
                                pe.wait_ge(v_ready, at((n + 1) * NV))
                                if prep:
                                    pe.wait_ge(k1_ready, at((p + 1) * 3))
                                    pe.wait_ge(rest_ready, at((p + 1) * 3))
                                pe.transpose(ps[0:2 * MROWS * PAIRS, WORK, 0:TOK],
                                             mcols[:, :, :, :].rearrange("q a i p -> q (a i p)"), ident[0:TOK, 0:TOK]).then_inc(shift_ps, 1)

                            for u in range(-1, NU):
                                ms = maxima_of(u) if nxt else ()
                                if now and u == 0:
                                    pe.wait_ge(shift_in, at(n * 32))
                                if now and u >= 0:
                                    scores(u)
                                for m in ms[:1]:
                                    maximum(m)
                                if now and u >= LAG:
                                    values(u - LAG)
                                for m in ms[1:]:
                                    maximum(m)
                                if nxt and V_AT <= u < V_AT + 3:
                                    project_v(u - V_AT)
                                if prep and normed and T_AT <= u < T_AT + 3:
                                    turn(u - T_AT)
                                if prep and u in K_AT:
                                    project_k(K_AT.index(u))
                            if nxt:
                                turn_shift()
                            for u in range(NU - LAG, NU) if now else ():
                                values(u)

                        periods(pe, period)

                    @block.scalar
                    def _(act):
                        act.wait_ge(prepared, OPEN + 9)

                        def period(b, r, now, nxt, prep):
                            n, p = b + 1, b + 2
                            s, o, now_x, next_x = r % 2, 1 - r % 2, r % 3, (r + 1) % 3
                            for u in range(-1, NU):
                                if now and u >= 0:
                                    kn = spans[u // 2][1]
                                    act.wait_ge(score_ps, at(b * NU + u + 1))
                                    act.wait_ge(pv_done, at(b * NU + max(u - 2, 0)))
                                    act.activation(prob[0:kn, u % 3, :].rearrange("p (i c) -> p i c", i=2),
                                                   ps[0:kn, 2 * (u % 2):2 * (u % 2) + 2, 0:GT], ACT.Exp, scale=ISQ).then_inc(prob_ready, 1)
                                if nxt and V_AT <= u < V_AT + 3:
                                    t = u - V_AT
                                    act.wait_ge(pv_done, at(b * NU))
                                    for c0, m, kn in [((0, 4, KC),), ((4, 4, KC),), ((8, 3, KC), (11, 1, KLAST))][t]:
                                        act.wait_ge(v_ps, at(n * 3 + t + 1))
                                        act.activation(v[o][0:kn, c0:c0 + m, :, 0:2 * DH],
                                                       ps[0:kn, WORK, (c0 % 4) * P:(c0 % 4 + m) * P].rearrange(
                                                           "p (c i d) -> p c i d", c=m, i=PAIRS), ACT.Copy).then_inc(v_ready, 1)
                                if prep and u == CLEAR_AT:
                                    act.wait_ge(score_ps, at(b * NU))
                                    for a in range(2):
                                        rows_ = slice(a * SLOT, a * SLOT + MROWS)
                                        act.activation(qx[(r + 2) % 3][rows_, :, a * TOK:(a + 1) * TOK], zeros[rows_, :, :], ACT.Copy).then_inc(cleared, 1)
                                if prep and normed and u == X_AT:
                                    act.wait_ge(rstd_ready, at(p + 1))
                                if prep and normed and X_AT <= u < X_AT + 3:
                                    act.wait_ge(xshift_ready, at(p + 1))
                                    act.sem_inc(passed, 1)
                                    for c in range(4 * (u - X_AT), 4 * (u - X_AT) + 4):
                                        kn = spans[c][1]
                                        act.activation(xn[0:kn, c, :], xn[0:kn, c, :], ACT.Identity, scale=rstd[0:kn, c:c + 1],
                                                       bias=xshift[0:kn, c:c + 1]).then_inc(xn_ready, 1)
                                if prep and normed and T_AT <= u < T_AT + 3:
                                    t = u - T_AT
                                    k0, kn = blocks[t]
                                    act.wait_ge(v_ps, at((n + 1) * 3))
                                    act.wait_ge(xnT_ps, at(p * 3 + t + 1))
                                    act.sem_inc(passed, 1)
                                    if modulated:
                                        act.activation(xt[s][:, k0:k0 + kn], ps[:, WORK, 0:kn], ACT.Identity,
                                                       scale=MOD[:, 14, bass.ds(p, 1)], bias=MOD[:, 15, bass.ds(p, 1)]).then_inc(xt_ready, 1)
                                    else:
                                        act.activation(xt[s][:, k0:k0 + kn], ps[:, WORK, 0:kn], ACT.Copy).then_inc(xt_ready, 1)
                                if prep and u in K_AT:
                                    t = K_AT.index(u)
                                    k0, kn = blocks[t]
                                    act.wait_ge(packed_in, at(p * NPACK))
                                    act.wait_ge(k_ps, at(p * 3 + t + 1))
                                    act.activation(kp[0][:, k0:k0 + kn], ps[:, WORK, 0:kn], ACT.Identity,
                                                   bias=col(bk)).then_inc(k1_ready, 1)

                        periods(act, period)

                    @block.vector
                    def _(dve):
                        if normed:
                            dve.memset(mv[:, :, :], 0.0).then_inc(mv_zero, 1)
                            dve.wait_ge(mv_zero, OPEN + 1)
                        for s in range(2):
                            dve.memset(kx[s][:, :, :], 1.0).then_inc(prepared, 1)

                        def period(b, r, now, nxt, prep):
                            n, p = b + 1, b + 2
                            for u in range(-1, NU):
                                for m in maxima_of(u) if nxt else ():
                                    dve.wait_ge(max_ps, at(n * MAXN + m + 1))
                                    dve.tensor_reduce(bmax[:, m:m + 1], ps[0:TOK, MAXB + m % 2, 0:MAXK], AX.X, ALU.max).then_inc(max_done, 1)
                                if prep and normed and u == STATS_AT:
                                    dve.wait_ge(ctx_in, loads_before + (p + 1) * NCTX)
                                    for c in range(CHUNKS):
                                        kn = spans[c][1]
                                        dve.bn_stats(stats[0:kn, c, :], xn[0:kn, c, :]).then_inc(stats_done, 1)
                                    for c in range(CHUNKS):
                                        kn = spans[c][1]
                                        dve.wait_ge(stats_done, at(p * 2 * CHUNKS + CHUNKS))
                                        dve.sem_inc(passed, 1)
                                        dve.bn_aggr(mv[0:kn, c, :], stats[0:kn, c, :]).then_inc(stats_done, 1)
                                    dve.wait_ge(stats_done, at((p + 1) * 2 * CHUNKS))
                                    dve.tensor_scalar(ve[:, :], mv[:, :, 1], eps, None, ALU.add).then_inc(var_ready, 1)
                                if prep and normed and u == X_AT:
                                    dve.wait_ge(xn_ready, at(p * CHUNKS))
                                    dve.wait_ge(rstd_ready, at(p + 1))
                                    dve.scalar_tensor_tensor(xshift[:, :], mv[:, :, 0], -1.0, rstd[:, :], ALU.mult, ALU.mult).then_inc(xshift_ready, 1)
                                if prep and u - 1 in K_AT:
                                    t = K_AT.index(u - 1)
                                    k0, kn = blocks[t]
                                    dve.wait_ge(k1_ready, at(p * 3 + t + 1))
                                    dve.wait_ge(kparts_ready, at(p * NKPART))
                                    dve.scalar_tensor_tensor(krest[:, k0:k0 + kn], ps[:, WORK, 0:kn], col(bk), kp[0][:, k0:k0 + kn],
                                                             ALU.add, ALU.subtract).then_inc(rest_ready, 1)
                            if nxt:
                                link = Chain(dve, shift_chain, n, NSHIFT)
                                dve.wait_ge(max_done, at((n + 1) * MAXN))
                                link(dve.tensor_reduce(nmax[:, :], bmax[:, :].rearrange("q (h t) -> q h t", t=3), AX.X, ALU.max, negate=True))
                                shift_columns(dve, link, nmax, nmax1, mcols)
                                assert link.n == NSHIFT
                                dve.wait_ge(shift_ps, at(n + 1))
                                dve.wait_ge(shift_in, at(n * 32))
                                dve.tensor_copy(mrows[:, :], ps[0:2 * MROWS * PAIRS, WORK, 0:TOK]).then_inc(shift_ready, 1)
                            if now:
                                dve.wait_ge(pv_done, at(n * NU))
                                flink = Chain(dve, fin, b, NFIN)
                                finish(dve, flink, sums_read, ps[:, 7, :], sel, den, b, bv)
                                assert flink.n == NFIN

                        periods(dve, period)

        def pre2():
            with Stage("pre2") as st:
                W = st.sb("w", [P, 2 * P])
                w_in = st.sem("w_in")
                norm = Norm(st, "ln", 1e-5)
                q = st.sb("q", [P, GT])
                q_ps, q_ready, qk_ps, qk_out = st.sem("q_ps"), st.sem("q_ready"), st.sem("qk_ps"), st.sem("qk_out")
                ps = st.ps
                with st.block() as block:
                    @block.sync
                    def _(sp):
                        weights_in(sp, W, "pre2", w_in)

                    @block.vector
                    def _(dve):
                        with dve.Fori(0, NG) as g:
                            norm.vector(dve, g)
                            dve.wait_ge(norm.h_ready, OPEN + (g + 1) * GB)
                            dve.tensor_copy(KT[:, bass.ds(g * GT, GT)], norm.h[:, :]).then_inc(qk_out, 1)
                            dve.wait_ge(qk_ps, OPEN + g + 1)
                            dve.tensor_copy(QT[:, bass.ds(g * GT, GT)], ps[:, 2, 0:GT]).then_inc(qk_out, 1)

                    @block.gpsimd
                    def _(pool):
                        norm.gpsimd_init(pool)
                        with pool.Fori(0, NG) as g:
                            norm.gpsimd(pool, g)

                    @block.tensor
                    def _(pe):
                        pe.wait_ge(w_in, OPEN + 16)
                        with pe.Fori(0, NG) as g:
                            norm.tensor(pe, g, ps[:, 0, :])
                            pe.wait_ge(norm.h_ready, OPEN + (g + 1) * GB)
                            pe.matmul(ps[:, 1, 0:GT], W[:, 0:P], norm.h[:, :], start=True, stop=True).then_inc(q_ps, 1)
                            pe.wait_ge(q_ready, OPEN + g + 1)
                            pe.matmul(ps[:, 2, 0:GT], W[:, P:2 * P], q[:, :], start=True, stop=True).then_inc(qk_ps, 1)

                    @block.scalar
                    def _(act):
                        with act.Fori(0, NG) as g:
                            act.wait_ge(qk_out, OPEN + g * 2)
                            norm.scalar(act, g, ps[:, 0, :], by_col("ng2"), by_col("nb2"))
                            act.wait_ge(q_ps, OPEN + g + 1)
                            act.sem_inc(passed, 1)
                            act.activation(q[:, :], ps[:, 1, 0:GT], ACT.Copy).then_inc(q_ready, 1)

        def attend2():
            scale = float(P) ** -0.5
            with Stage("attend2") as st:
                ps = st.ps
                q = st.sb("q", [P, TOK])
                xt = st.sb("ctx_channels", [P, CTX])
                xn = st.sb("ctx_tokens", [KC, CHUNKS, P])
                prob = st.sb("prob", [TOK, CTX])
                probn = st.sb("prob_normal", [TOK, CTX])
                probT = st.sb("prob_turned", [KC, CHUNKS, TOK])
                mx = st.sb("minus_max", [TOK, 3])
                nm = st.sb("shift", [TOK, 1])
                den = st.sb("den", [TOK, 3])
                den1 = st.sb("den_sum", [TOK, 1])
                rden = st.sb("den_reciprocal", [TOK, 1])
                xt_in, xn_in = st.sem("xt_in"), st.sem("xn_in")
                q_ready, score_ps, chain = st.sem("q_ready"), st.sem("score_ps"), st.sem("chain")
                prob_ready, norm_ready, norm_chain = st.sem("prob_ready"), st.sem("norm_ready"), st.sem("norm_chain")
                turned_ps, turned_ready, o_ps, o_out = st.sem("turned_ps"), st.sem("turned_ready"), st.sem("o_ps"), st.sem("o_out")
                spans = [(t * BLK, min(BLK, CTX - t * BLK)) for t in range(3)]
                rows_of = [KC if c < CHUNKS - 1 else KLAST for c in range(CHUNKS)]
                with st.block() as block:
                    @block.sync
                    def _(sp):
                        def load_channels(b):
                            sp.wait_ge(score_ps, at(b * 3))
                            sp.sem_inc(passed, 1)
                            sp.dma_start(xt[:, :], ctx_t[b]).then_inc(xt_in, 16)

                        def load_tokens(b):
                            sp.wait_ge(o_ps, at(b))
                            sp.sem_inc(passed, 1)
                            sp.dma_start(xn[:, 0:CHUNKS - 1, :],
                                         ctx_n[b, 0:(CHUNKS - 1) * KC, :].rearrange("(c p) d -> p c d", p=KC)).then_inc(xn_in, 16)
                            sp.dma_start(xn[0:KLAST, CHUNKS - 1, :], ctx_n[b, (CHUNKS - 1) * KC:CTX, :]).then_inc(xn_in, 16)

                        load_channels(0)
                        with sp.Fori(0, NB - 1) as b:
                            load_channels(b + 1)
                            load_tokens(b)
                        load_tokens(NB - 1)

                    @block.tensor
                    def _(pe):
                        def scores(b):
                            pe.wait_ge(xt_in, at((b + 1) * 16))
                            pe.wait_ge(q_ready, at(b + 1))
                            pe.wait_ge(prob_ready, at(b * 3))
                            for t, (k0, n) in enumerate(spans):
                                pe.matmul(ps[0:TOK, t, 0:n], q[:, :], xt[:, k0:k0 + n], start=True, stop=True).then_inc(score_ps, 1)

                        def values(b):
                            pe.wait_ge(turned_ready, at(b * 4))
                            for t in range(3):
                                pe.wait_ge(norm_ready, at(b * 3 + t + 1))
                                for c in range(4 * t, 4 * t + 4):
                                    tr = pe.transpose(ps[0:rows_of[c], 3 + t, (c % 4) * TOK:(c % 4 + 1) * TOK],
                                                      probn[:, c * KC:c * KC + rows_of[c]], ident[0:TOK, 0:TOK])
                                tr.then_inc(turned_ps, 1)
                            pe.wait_ge(xn_in, at((b + 1) * 32))
                            pe.wait_ge(o_out, at(b))
                            for c in range(CHUNKS):
                                if c % 4 == 0:
                                    pe.wait_ge(turned_ready, at((b * 4 + (c // 4 + 1 if c < 8 else 4))))
                                mm = pe.matmul(ps[:, 6, 0:TOK], xn[0:rows_of[c], c, :], probT[0:rows_of[c], c, :],
                                               start=(c == 0), stop=(c == CHUNKS - 1))
                            mm.then_inc(o_ps, 1)

                        scores(0)
                        with pe.Fori(0, NB - 1) as b:
                            scores(b + 1)
                            values(b)
                        values(NB - 1)

                    @block.scalar
                    def _(act):
                        def copy_q(b):
                            act.wait_ge(score_ps, at(b * 3))
                            act.sem_inc(passed, 1)
                            act.activation(q[:, :], QT[:, bass.ds(b * TOK, TOK)], ACT.Copy).then_inc(q_ready, 1)

                        def exponentials(b):
                            act.wait_ge(chain, at((b + 1) * 5))
                            act.wait_ge(norm_ready, at(b * 3))
                            for t, (k0, n) in enumerate(spans):
                                act.activation(prob[:, k0:k0 + n], ps[0:TOK, t, 0:n], ACT.Exp, scale=scale,
                                               bias=nm[:, 0:1], accum_out=den[:, t:t + 1]).then_inc(prob_ready, 1)

                        def turned(b):
                            act.wait_ge(o_ps, at(b))
                            for t in range(3):
                                act.wait_ge(turned_ps, at(b * 3 + t + 1))
                                m = 4 if t < 2 else 3
                                act.activation(probT[:, 4 * t:4 * t + m, :],
                                               ps[0:KC, 3 + t, 0:m * TOK].rearrange("p (c q) -> p c q", c=m), ACT.Copy).then_inc(turned_ready, 1)
                            act.activation(probT[0:KLAST, CHUNKS - 1, :], ps[0:KLAST, 5, 3 * TOK:4 * TOK], ACT.Copy).then_inc(turned_ready, 1)

                        copy_q(0)
                        with act.Fori(0, NB - 1) as b:
                            exponentials(b)
                            copy_q(b + 1)
                            turned(b)
                        exponentials(NB - 1)
                        turned(NB - 1)

                    @block.vector
                    def _(dve):
                        def maximum(b):
                            dve.wait_ge(prob_ready, at(b * 3))
                            link = Chain(dve, chain, b, 5)
                            for t, (k0, n) in enumerate(spans):
                                dve.wait_ge(score_ps, at(b * 3 + t + 1))
                                link(dve.tensor_reduce(mx[:, t:t + 1], ps[0:TOK, t, 0:n], AX.X, ALU.max))
                            link(dve.tensor_reduce(nm[:, 0:1], mx[:, :], AX.X, ALU.max, negate=True))
                            link(dve.tensor_scalar(nm[:, 0:1], nm[:, 0:1], scale, None, ALU.mult))

                        def normalise(b):
                            dve.wait_ge(prob_ready, at(b * 3 + 3))
                            dlink = Chain(dve, norm_chain, b, 2)
                            dlink(dve.tensor_reduce(den1[:, 0:1], den[:, :], AX.X, ALU.add))
                            dlink(dve.reciprocal(rden[:, 0:1], den1[:, 0:1]))
                            dve.wait_ge(turned_ps, at(b * 3))
                            for t, (k0, n) in enumerate(spans):
                                dve.tensor_scalar(probn[:, k0:k0 + n], prob[:, k0:k0 + n], rden[:, 0:1], None, ALU.mult).then_inc(norm_ready, 1)

                        def copy_out(b):
                            dve.wait_ge(o_ps, at(b + 1))
                            dve.tensor_copy(AT[:, 0, bass.ds(b * TOK, TOK)], ps[:, 6, 0:TOK]).then_inc(o_out, 1)

                        maximum(0)
                        with dve.Fori(0, NB - 1) as b:
                            normalise(b)
                            maximum(b + 1)
                            copy_out(b)
                        normalise(NB - 1)
                        copy_out(NB - 1)

        def experts():
            a, n = 0, {}
            for key, width in [("wv", P), ("router", 9), ("w1", 18 * P), ("gw1", 3 * P), ("w2", 6 * P), ("gw2", P), ("out", P)]:
                n[key] = a
                a += width
            with Stage("experts") as st:
                ps = st.ps
                W = st.sb("w", [P, a])
                R = st.sb("rows", [TOK, ROWS.width])
                comb = st.sb("combined", [P, 3, GT])
                hid = st.sb("hidden", [P, 7, GT])
                probs = st.sb("probs", [TOK, GB, 3])
                logit = st.sb("logits", [TOK, GB, 3])
                lmax = st.sb("logit_max", [TOK, GB])
                lsum = st.sb("logit_sum", [TOK, GB])
                lrec = st.sb("logit_rec", [TOK, GB])
                eo = st.sb("expert_out", [TOK, GB, 3 * P])
                routed = st.sb("routed", [TOK, GB, P])
                gp = st.sb("gate_pre", [TOK, GB, P])
                gt = st.sb("gate_tanh", [TOK, GB, P])
                gate = st.sb("gate", [TOK, GB, P])
                rT = st.sb("routed_turned", [P, GT])
                dx = st.sb("delta", [TOK, GB, P])
                w_in = st.sem("w_in")
                ev_ps, comb_ready = st.sem("ev_ps"), st.sem("comb_ready")
                logit_ps, lchain, exp_ready = st.sem("logit_ps"), st.sem("logit_chain"), st.sem("exp_ready")
                hid_ps, hid_ready = st.sem("hid_ps"), st.sem("hid_ready")
                eo_ps, eo_out = st.sem("eo_ps"), st.sem("eo_out")
                gp_ready, tanh_ready, rchain = st.sem("gp_ready"), st.sem("tanh_ready"), st.sem("routed_chain")
                rT_ps, rT_ready, out_ps, out_chain = st.sem("rT_ps"), st.sem("rT_ready"), st.sem("out_ps"), st.sem("out_chain")

                def row(name, shape):
                    r0, r1 = ROWS[name]
                    return R[:, r0:r1].rearrange("p (o c) -> p o c", o=1).to_broadcast(shape)

                with st.block() as block:
                    @block.sync
                    def _(sp):
                        weights_in(sp, W, "moe", w_in)
                        sp.dma_start(R[:, :], rows.to_broadcast([TOK, ROWS.width])).then_inc(w_in, 16)

                    @block.vector
                    def _(dve):
                        dve.wait_ge(w_in, OPEN + 32)
                        with dve.Fori(0, NG) as g:
                            dve.tensor_copy(comb[:, 0, :], KT[:, bass.ds(g * GT, GT)]).then_inc(comb_ready, 1)
                            dve.tensor_copy(comb[:, 2, :].rearrange("p (k t) -> p k t", k=GB),
                                            COND[:, bass.ds(g * GB, GB)].rearrange("p (k o) -> p k o", o=1).to_broadcast([P, GB, TOK])).then_inc(comb_ready, 1)
                            dve.wait_ge(ev_ps, OPEN + g + 1)
                            dve.tensor_copy(comb[:, 1, :], ps[:, 0, 0:GT]).then_inc(comb_ready, 1)
                            link = Chain(dve, lchain, g, 3)
                            dve.wait_ge(logit_ps, OPEN + g + 1)
                            link(dve.tensor_tensor(logit[:, :, :], ps[0:TOK, 1, 0:GB * 3].rearrange("p (k e) -> p k e", k=GB),
                                                   row("router", [TOK, GB, 3]), ALU.add))
                            link(dve.tensor_reduce(lmax[:, :], logit[:, :, :], AX.X, ALU.max))
                            link(dve.tensor_tensor(logit[:, :, :], logit[:, :, :],
                                                   lmax[:, :].rearrange("p (k o) -> p k o", o=1).to_broadcast([TOK, GB, 3]), ALU.subtract))
                            dve.wait_ge(exp_ready, OPEN + g + 1)
                            link = Chain(dve, rchain, g, 3 + 3 * GB)
                            link(dve.tensor_reduce(lsum[:, :], probs[:, :, :], AX.X, ALU.add))
                            link(dve.reciprocal(lrec[:, :], lsum[:, :]))
                            link(dve.tensor_tensor(probs[:, :, :], probs[:, :, :],
                                                   lrec[:, :].rearrange("p (k o) -> p k o", o=1).to_broadcast([TOK, GB, 3]), ALU.mult))
                            for k in range(GB):
                                dve.wait_ge(eo_ps, OPEN + g * GB + k + 1)
                                bank = ps[0:TOK, 4 + k, :]
                                dve.tensor_tensor(eo[:, k, :], bank[:, 0:3 * P], R[:, ROWS["eb2"][0]:ROWS["eb2"][1]], ALU.add).then_inc(eo_out, 1)
                                dve.tensor_tensor(gp[:, k, :], bank[:, 3 * P:4 * P], R[:, ROWS["gb2"][0]:ROWS["gb2"][1]], ALU.add).then_inc(gp_ready, 1)
                            for k in range(GB):
                                dve.wait_ge(eo_out, OPEN + g * GB + k + 1)
                                link(dve.tensor_scalar(routed[:, k, :], eo[:, k, 0:P], probs[:, k, 0:1], None, ALU.mult))
                                for e in (1, 2):
                                    link(dve.scalar_tensor_tensor(routed[:, k, :], eo[:, k, e * P:(e + 1) * P], probs[:, k, e:e + 1],
                                                                  routed[:, k, :], ALU.mult, ALU.add))
                            olink = Chain(dve, out_chain, g, 4)
                            dve.wait_ge(tanh_ready, OPEN + g + 1)
                            olink(dve.tensor_scalar(gate[:, :, :], gt[:, :, :], 0.5, 0.5, ALU.mult, ALU.add))
                            dve.wait_ge(out_ps, OPEN + g + 1)
                            olink(dve.tensor_tensor(dx[:, :, :], ps[0:TOK, 3, 0:GB * P].rearrange("p (k c) -> p k c", k=GB),
                                                    row("outb", [TOK, GB, P]), ALU.add))
                            olink(dve.tensor_tensor(dx[:, :, :], dx[:, :, :], gate[:, :, :], ALU.mult))
                            xs = X[:, bass.ds(g * GB, GB), :]
                            olink(dve.tensor_tensor(xs, xs, dx[:, :, :], ALU.add))

                    @block.tensor
                    def _(pe):
                        pe.wait_ge(w_in, OPEN + 32)

                        def over_inputs(o, w0, width, dst_cols=None):
                            for i in range(3):
                                mm = pe.matmul(o, W[:, w0 + i * width:w0 + i * width + P], comb[:, i, :], start=(i == 0), stop=(i == 2))
                            return mm

                        with pe.Fori(0, NG) as g:
                            pe.wait_ge(out_chain, OPEN + g * 4)
                            pe.matmul(ps[:, 0, 0:GT], W[:, n["wv"]:n["wv"] + P], AT[:, 0, bass.ds(g * GT, GT)], start=True, stop=True).then_inc(ev_ps, 1)
                            pe.wait_ge(comb_ready, OPEN + (g + 1) * 3)
                            for k in range(GB):
                                for i in range(3):
                                    mm = pe.matmul(ps[0:TOK, 1, 3 * k:3 * k + 3], comb[:, i, k * TOK:(k + 1) * TOK],
                                                   W[:, n["router"] + 3 * i:n["router"] + 3 * i + 3], start=(i == 0), stop=(i == 2))
                            mm.then_inc(logit_ps, 1)
                            for j in range(7):
                                if j >= 2:
                                    pe.wait_ge(hid_ready, OPEN + g * 7 + j - 1)
                                o = ps[:, 2 + j % 2, 0:GT]
                                if j < 6:
                                    over_inputs(o, n["w1"] + (j // 2) * 6 * P + (j % 2) * P, 2 * P).then_inc(hid_ps, 1)
                                else:
                                    over_inputs(o, n["gw1"], P).then_inc(hid_ps, 1)
                            pe.wait_ge(hid_ready, OPEN + (g + 1) * 7)
                            for k in range(GB):
                                s = slice(k * TOK, (k + 1) * TOK)
                                bank = ps[0:TOK, 4 + k, :]
                                for e in range(3):
                                    for i in range(2):
                                        pe.matmul(bank[:, e * P:(e + 1) * P], hid[:, 2 * e + i, s],
                                                  W[:, n["w2"] + (2 * e + i) * P:n["w2"] + (2 * e + i + 1) * P], start=(i == 0), stop=(i == 1))
                                pe.matmul(bank[:, 3 * P:4 * P], hid[:, 6, s], W[:, n["gw2"]:n["gw2"] + P], start=True, stop=True).then_inc(eo_ps, 1)
                            for k in range(GB):
                                pe.wait_ge(rchain, OPEN + g * (3 + 3 * GB) + 3 + 3 * (k + 1))
                                tr = pe.transpose(ps[:, 2, k * TOK:(k + 1) * TOK], routed[:, k, :], ident[0:TOK, 0:TOK])
                            tr.then_inc(rT_ps, 1)
                            pe.wait_ge(rT_ready, OPEN + g + 1)
                            for k in range(GB):
                                mm = pe.matmul(ps[0:TOK, 3, k * P:(k + 1) * P], rT[:, k * TOK:(k + 1) * TOK],
                                               W[:, n["out"]:n["out"] + P], start=True, stop=True)
                            mm.then_inc(out_ps, 1)

                    @block.scalar
                    def _(act):
                        with act.Fori(0, NG) as g:
                            act.wait_ge(lchain, OPEN + (g + 1) * 3)
                            act.activation(probs[:, :, :], logit[:, :, :], ACT.Exp).then_inc(exp_ready, 1)
                            for j in range(7):
                                act.wait_ge(hid_ps, OPEN + g * 7 + j + 1)
                                act.activation(hid[:, j, :], ps[:, 2 + j % 2, 0:GT], ACT.Silu,
                                               bias=col("eb1", j) if j < 6 else col("gb1")).then_inc(hid_ready, 1)
                            act.wait_ge(gp_ready, OPEN + (g + 1) * GB)
                            act.activation(gt[:, :, :], gp[:, :, :], ACT.Tanh, scale=0.5).then_inc(tanh_ready, 1)
                            act.wait_ge(rT_ps, OPEN + g + 1)
                            act.activation(rT[:, :], ps[:, 2, 0:GT], ACT.Copy).then_inc(rT_ready, 1)

        def pre3():
            with Stage("pre3") as st:
                W = st.sb("w", [P, P])
                w_in = st.sem("w_in")
                norm = Norm(st, "ln", 1e-5)
                q_ps, q_out = st.sem("q_ps"), st.sem("q_out")
                ps = st.ps
                with st.block() as block:
                    @block.sync
                    def _(sp):
                        weights_in(sp, W, "pre3", w_in)

                    @block.vector
                    def _(dve):
                        with dve.Fori(0, NG) as g:
                            dve.wait_ge(norm.xnT_ready, OPEN + g)
                            dve.sem_inc(passed, 1)
                            norm.vector(dve, g)

                    @block.gpsimd
                    def _(pool):
                        norm.gpsimd_init(pool)
                        with pool.Fori(0, NG) as g:
                            norm.gpsimd(pool, g)

                    @block.tensor
                    def _(pe):
                        pe.wait_ge(w_in, OPEN + 16)
                        with pe.Fori(0, NG) as g:
                            norm.tensor(pe, g, ps[:, 2, :])
                            pe.wait_ge(norm.h_ready, OPEN + (g + 1) * GB)
                            pe.wait_ge(q_out, OPEN + g)
                            pe.matmul(ps[:, 3, 0:GT], W[:, :], norm.h[:, :], start=True, stop=True).then_inc(q_ps, 1)

                    @block.scalar
                    def _(act):
                        with act.Fori(0, NG) as g:
                            norm.scalar(act, g, ps[:, 2, :], by_mod(12), by_mod(13))
                            act.wait_ge(q_ps, OPEN + g + 1)
                            act.sem_inc(passed, 1)
                            act.activation(QT[:, bass.ds(g * GT, GT)], ps[:, 3, 0:GT], ACT.Identity, bias=col("bq3")).then_inc(q_out, 1)

        def post3():
            with Stage("post3") as st:
                W = st.sb("w", [P, 2 * P])
                w_in, out_done = st.sem("w_in"), st.sem("out_done")
                res = Residual(st, "o", "bo3", None)
                ps = st.ps
                with st.block() as block:
                    @block.sync
                    def _(sp):
                        weights_in(sp, W, "post3", w_in)
                        with sp.Fori(0, NG) as g:
                            sp.wait_ge(res.x_ready, OPEN + g + 1)
                            sp.sem_inc(passed, 1)
                            sp.dma_start(out[bass.ds(g * GB, GB)].rearrange("b t c -> t b c"),
                                         X[:, bass.ds(g * GB, GB), :]).then_inc(out_done, 16)
                        sp.wait_ge(out_done, OPEN + 16 * NG)

                    @block.vector
                    def _(dve):
                        with dve.Fori(0, NG) as g:
                            res.vector_gate(dve, g, ps[:, 0, :])
                            res.vector_add(dve, g, ps[:, 1, :])

                    @block.tensor
                    def _(pe):
                        pe.wait_ge(w_in, OPEN + 16)
                        with pe.Fori(0, NG) as g:
                            pe.wait_ge(res.x_ready, OPEN + g)
                            res.product(pe, g, ps[:, 0, :], W)
                            res.tensor(pe, g, ps[:, 1, :])

        stages = [
            lambda: pre("pre0", "pre0", by_mod(1), by_mod(0), 1e-6, "bk0", "bq0"),
            lambda: self_attend("self0", "bv0"),
            lambda: mid("mid0", "mid0", "bo0", by_mod(2), by_col("ng0"), by_col("nb0"), "bqc0"),
            lambda: cross_attend("cross0", "kv0", "bkc0", "bvc0", 0),
            lambda: post("post0", "post0", "boc0", by_mod(4), by_mod(3), "b10", "b20", by_mod(5)),
            lambda: pre("pre1", "pre1", by_mod(7), by_mod(6), 1e-6, "bk1", "bq1"),
            lambda: self_attend("self1", "bv1"),
            lambda: mid("mid1", "mid1", "bo1", by_mod(8), None, None, "bqc1"),
            lambda: cross_attend("cross1", "kv1", "bkc1", "bvc1", NB * 16, normed=True),
            lambda: post("post1", "post1", "boc1", by_mod(10), by_mod(9), "b11", "b21", by_mod(11)),
            pre2, attend2, experts, pre3,
            lambda: cross_attend("cross3", "kv3", "bkc3", "bvc3", NB * (16 + 32), normed=True, eps=1e-5, modulated=True),
            post3,
        ]
        KT = V0 = None
        for n, s in enumerate(stages[:last]):
            if n in (0, 5, 10):
                kv_scope = ExitStack()
                KT = kv_scope.enter_context(nc.sbuf_tensor(f"k_channels_{n}", [P, NB * TOK], F32))
                if n < 10:
                    V0 = kv_scope.enter_context(nc.sbuf_tensor(f"v_tokens_{n}", [TOK, NB, P], F32))
            s()
            if n in (1, 6, 12):
                kv_scope.close()
        if probe is not None:
            probe(nc, dict(X=X, QT=QT, KT=KT, V0=V0, AT=AT, MOD=MOD))


def layout(t):
    L0, L1, L2, L3 = ({k[len(f"L{n}_xcond_"):]: v for k, v in t.items() if k.startswith(f"L{n}_xcond_")} for n in range(4))

    def blocks(w):
        n = w.shape[0] // P
        return [w[i * P:(i + 1) * P] for i in range(n)]

    def cat(*parts):
        return np.concatenate([np.ascontiguousarray(x) for x in parts], axis=1)

    kvc = L1["W_kvc"]
    place = np.array([[(2 * (COLT * u + r // 32) + r % 32 // DH) * DH + r % DH if r % 32 < 2 * DH else -1
                       for u in range(NHALF)] for r in range(P)])

    def halves(w):
        return [np.where(place[:, u:u + 1] >= 0, w[place[:, u]], np.float32(0)) for u in range(NHALF)]

    def half_columns(v):
        return np.where(place >= 0, v[place], np.float32(0))

    groups = {
        "mod": cat(L0["ada_w"], L1["W_mod"], L3["Wss_q"], L3["Wss_kv"]),
        "pre0": cat(L0["qkv_w"][:, P:2 * P][:, PERM], L0["qkv_w"][:, 2 * P:], L0["qkv_w"][:, :P][:, PERM]),
        "mid0": cat(*halves(L0["self_o_w"]), L0["q_w"][:, PERM]),
        "kv0": cat(L0["kv_w"][:, :P][:, PERM], L0["kv_w"][:, P:]),
        "post0": cat(*halves(L0["cross_o_w"]), L0["mlp_w1"], *blocks(L0["mlp_w2"])),
        "pre1": cat(L1["W_qkv"][:, P:2 * P][:, PERM], L1["W_qkv"][:, 2 * P:], L1["W_qkv"][:, :P][:, PERM]),
        "mid1": cat(*halves(L1["W_proj"]), L1["W_qc"][:, PERM]),
        "kv1": cat(kvc[:, :P][:, PERM], kvc[:, P:]),
        "post1": cat(*halves(L1["W_cproj"]), L1["W_mlp1"], *blocks(L1["W_mlp2"])),
        "pre2": cat(L2["Wq"], L2["Wk"].T),
        "moe": cat(L2["Wv"], *blocks(L2["router_W"]), *[b for e in range(3) for b in blocks(L2["e_w1"][e])],
                   *blocks(L2["gate_w1"]), *[b for e in range(3) for b in blocks(L2["e_w2"][e])],
                   L2["gate_w2"], L2["out_w"]),
        "pre3": L3["Wq"][:, PERM],
        "kv3": cat(L3["Wkv"][:, :P][:, PERM], L3["Wkv"][:, P:]),
        "post3": cat(*halves(L3["Wp"])),
    }
    for n, g in groups.items():
        a, b = WEIGHTS[n]
        assert g.shape == (P, b - a), (n, g.shape, b - a)

    def columns(v):
        return np.ascontiguousarray(v.reshape(-1, P).T)

    cols = {
        "mod": cat(columns(L0["ada_b"]), columns(L1["b_mod"]), columns(L3["bss_q"]), columns(L3["bss_kv"])),
        "bq0": columns(L0["qkv_b"][:P][PERM]), "bk0": columns(L0["qkv_b"][P:2 * P][PERM]), "bv0": half_columns(L0["qkv_b"][2 * P:]),
        "bo0": columns(L0["self_o_b"]), "ng0": columns(L0["norm2_g"]), "nb0": columns(L0["norm2_b"]),
        "bqc0": columns(L0["q_b"][PERM]), "bkc0": columns(L0["kv_b"][:P][PERM]), "bvc0": half_columns(L0["kv_b"][P:]),
        "boc0": columns(L0["cross_o_b"]), "b10": columns(L0["mlp_b1"]), "b20": columns(L0["mlp_b2"]),
        "bq1": columns(L1["b_qkv"][:P][PERM]), "bk1": columns(L1["b_qkv"][P:2 * P][PERM]), "bv1": half_columns(L1["b_qkv"][2 * P:]),
        "bo1": columns(L1["b_proj"]), "bqc1": columns(L1["b_qc"][PERM]), "bkc1": columns(L1["b_kvc"][:P][PERM]),
        "bvc1": half_columns(L1["b_kvc"][P:]), "boc1": columns(L1["b_cproj"]), "b11": columns(L1["b_mlp1"]), "b21": columns(L1["b_mlp2"]),
        "ng2": columns(L2["ln_gamma"]), "nb2": columns(L2["ln_beta"]), "eb1": columns(L2["e_b1"]), "gb1": columns(L2["gate_b1"]),
        "bq3": columns(L3["bq"][PERM]), "bkc3": columns(L3["bkv"][:P][PERM]), "bvc3": half_columns(L3["bkv"][P:]), "bo3": columns(L3["bp"]),
    }
    assert list(cols) == list(COLS.at)
    rows = [L2["router_b"], L2["e_b2"].reshape(-1), L2["gate_b2"], L2["out_b"]]
    lane = np.arange(P)
    own = (lane[:, None] // DH % 2 == np.arange(2)[None, :])
    arrays = {
        "x": t["x"],
        "ctx_t": np.swapaxes(t["ctx_1024"], 1, 2),
        "ctx_n": t["ctx_1024"],
        "cond_t": t["cond_1024"].T,
        "weights": cat(*groups.values()),
        "cols": cat(*cols.values()),
        "rows": np.concatenate(rows)[None, :],
        "const": cat(np.eye(P, dtype=np.float32), own.astype(np.float32)),
    }
    return {k: np.ascontiguousarray(v) for k, v in arrays.items()}, t["x"].shape


def kernel(**inputs):
    import numpy as _np
    import concourse.bacc as _bacc
    from concourse import mybir as _mybir
    from concourse.bass_utils import run_bass_kernel_spmd as _run

    arrays, shape = layout({k: _np.asarray(v) for k, v in inputs.items()})
    nc = _bacc.Bacc("TRN2", target_bir_lowering=False, num_devices=1)
    aps = {n: nc.dram_tensor(f"in_{n}", a.shape, _mybir.dt.float32, kind="ExternalInput").ap() for n, a in arrays.items()}
    out = nc.dram_tensor("out_0", shape, _mybir.dt.float32, kind="ExternalOutput").ap()
    build(nc, out=out, NB=shape[0], **aps)
    r = _run(nc, [{f"in_{n}": a for n, a in arrays.items()}], core_ids=[0])
    return r.results[0]["out_0"]
```
